# Optimizing a Trainium2 kernel written in Bass

```python
import numpy as np
import jax
import jax.numpy as jnp

def _softmax(x, axis=-1):
    return jax.nn.softmax(x, axis=axis)

def _gelu(x):
    return jax.nn.gelu(x, approximate=True)

def _silu(x):
    return jax.nn.silu(x)

def _sigmoid(x):
    return jax.nn.sigmoid(x)

def _layernorm(x, axis=-1, eps=1e-05):
    m = jnp.mean(x, axis=axis, keepdims=True)
    v = jnp.var(x, axis=axis, keepdims=True)
    return (x - m) / jnp.sqrt(v + eps)

def _scatter_add(tgt, idx, src, axis=0):
    return tgt.at[idx].add(src)

def _segment_sum(src, seg, n):
    return jax.ops.segment_sum(src, seg, n)
kernel_name = 'mk_early_fusion_d1_tok_img256_r4_ed6d56'

def setup_inputs(seed: int=0):
    np.random.seed(seed)
    _w = jnp.asarray

    def _rec_inputs():
        import jax
        import jax.numpy as jnp
        _rk = jax.random.key(seed)
        x = -7.10856e-05 + 0.999911 * jax.random.normal(jax.random.fold_in(_rk, 1), (4, 64, 128, 64), jnp.float32)
        txt = -0.000161634 + 0.479995 * jax.random.normal(jax.random.fold_in(_rk, 2), (4, 32, 64), jnp.float32)
        return (x, txt)
    x, txt = _rec_inputs()

    def _L0_tok_setup():
        import jax, jax.numpy as jnp
        import numpy as np
        PATCH_LEN = 16
        STRIDE = 8
        PAD = 8
        key = jax.random.key(seed)
        k1, k2 = jax.random.split(key)
        x = jax.random.normal(k1, (32, 64, 128, 64), dtype=jnp.float32)
        in_feat = 64 * (PATCH_LEN // 2 + 1) * 2
        W = jax.random.normal(k2, (64, in_feat), dtype=jnp.float32) * 0.02
        return {'x': x, 'W': W}
    _L0_tok_all = _L0_tok_setup()
    _L0_tok_in = {k: v for k, v in _L0_tok_all.items() if k in ('W',)}
    del _L0_tok_all

    def _L0_attn_setup():
        import jax, jax.numpy as jnp
        import numpy as np
        SEQ_LEN = 512
        EMBED_DIM = 64
        BATCH = 8
        LN_EPS = 1e-05

        def _layernorm(x, g, b):
            mu = jnp.mean(x, axis=-1, keepdims=True)
            var = jnp.mean(jnp.square(x - mu), axis=-1, keepdims=True)
            return (x - mu) * jax.lax.rsqrt(var + LN_EPS) * g + b
        key = jax.random.key(seed)
        ks = jax.random.split(key, 8)
        C = EMBED_DIM
        x = jax.random.normal(ks[0], (BATCH, SEQ_LEN, C), dtype=jnp.float32)
        qkv_w = jax.random.normal(ks[1], (C, 3 * C), dtype=jnp.float32) * 0.02
        qkv_b = jnp.zeros((3 * C,), dtype=jnp.float32)
        proj_w = jax.random.normal(ks[2], (C, C), dtype=jnp.float32) * 0.02
        proj_b = jnp.zeros((C,), dtype=jnp.float32)
        ln1_g = jnp.ones((C,), dtype=jnp.float32)
        ln1_b = jnp.zeros((C,), dtype=jnp.float32)
        ln2_g = jnp.ones((C,), dtype=jnp.float32)
        ln2_b = jnp.zeros((C,), dtype=jnp.float32)
        bias_table = jax.random.truncated_normal(ks[3], -2.0, 2.0, (2 * SEQ_LEN - 1,), dtype=jnp.float32) * 0.02
        scale = jnp.asarray(1.0 / np.sqrt(C), dtype=jnp.float32)
        return {'x': x, 'ln1_g': ln1_g, 'ln1_b': ln1_b, 'qkv_w': qkv_w, 'qkv_b': qkv_b, 'bias_table': bias_table, 'scale': scale, 'proj_w': proj_w, 'proj_b': proj_b, 'ln2_g': ln2_g, 'ln2_b': ln2_b}
    _L0_attn_all = _L0_attn_setup()
    _L0_attn_in = {k: v for k, v in _L0_attn_all.items() if k in ('ln1_g', 'ln1_b', 'qkv_w', 'qkv_b', 'bias_table', 'scale', 'proj_w', 'proj_b', 'ln2_g', 'ln2_b')}
    del _L0_attn_all

    def _L0_ffn_setup():
        import jax, jax.numpy as jnp
        import numpy as np
        B, T, C = (64, 96, 64)
        NH, NKV = (4, 2)
        HD = C // NH
        NREP = NH // NKV
        NE, TOPK = (8, 2)
        HID = int(8 / 3 * C)
        EPS_RMS = 1e-06

        def _rope_tables(t_len):
            inv_freq = 1.0 / 10000.0 ** (np.arange(0, HD, 2, dtype=np.float32) / HD)
            t = np.arange(t_len, dtype=np.float32)
            freqs = np.outer(t, inv_freq)
            emb = np.concatenate([freqs, freqs], axis=-1)
            return (jnp.asarray(np.cos(emb)), jnp.asarray(np.sin(emb)))

        def _rotate_half(x):
            h = x.shape[-1] // 2
            return jnp.concatenate([-x[..., h:], x[..., :h]], axis=-1)

        def _rmsnorm(v, w):
            return v * jax.lax.rsqrt(jnp.mean(v * v, axis=-1, keepdims=True) + EPS_RMS) * w
        key = jax.random.key(seed)
        ks = jax.random.split(key, 10)
        s = lambda k, shape: jax.random.normal(k, shape, jnp.float32) * 0.02
        return {'x': jax.random.normal(ks[0], (B, T, C), jnp.float32), 'ln1_w': jnp.ones((C,), jnp.float32), 'ln2_w': jnp.ones((C,), jnp.float32), 'wq': s(ks[1], (NH * HD, C)), 'wk': s(ks[2], (NKV * HD, C)), 'wv': s(ks[3], (NKV * HD, C)), 'wo': s(ks[4], (C, C)), 'router_w': s(ks[5], (NE, C)), 'w1': s(ks[6], (NE, HID, C)), 'w2': s(ks[7], (NE, C, HID)), 'w3': s(ks[8], (NE, HID, C))}
    _L0_ffn_all = _L0_ffn_setup()
    _L0_ffn_in = {k: v for k, v in _L0_ffn_all.items() if k in ('ln1_w', 'ln2_w', 'wq', 'wk', 'wv', 'wo', 'router_w', 'w1', 'w2', 'w3')}
    del _L0_ffn_all
    return {'x': x, 'txt': txt, 'L0_tok_W': _L0_tok_in['W'], 'L0_attn_ln1_g': _L0_attn_in['ln1_g'], 'L0_attn_ln1_b': _L0_attn_in['ln1_b'], 'L0_attn_qkv_w': _L0_attn_in['qkv_w'], 'L0_attn_qkv_b': _L0_attn_in['qkv_b'], 'L0_attn_bias_table': _L0_attn_in['bias_table'], 'L0_attn_scale': _L0_attn_in['scale'], 'L0_attn_proj_w': _L0_attn_in['proj_w'], 'L0_attn_proj_b': _L0_attn_in['proj_b'], 'L0_attn_ln2_g': _L0_attn_in['ln2_g'], 'L0_attn_ln2_b': _L0_attn_in['ln2_b'], 'L0_ffn_ln1_w': _L0_ffn_in['ln1_w'], 'L0_ffn_ln2_w': _L0_ffn_in['ln2_w'], 'L0_ffn_wq': _L0_ffn_in['wq'], 'L0_ffn_wk': _L0_ffn_in['wk'], 'L0_ffn_wv': _L0_ffn_in['wv'], 'L0_ffn_wo': _L0_ffn_in['wo'], 'L0_ffn_router_w': _L0_ffn_in['router_w'], 'L0_ffn_w1': _L0_ffn_in['w1'], 'L0_ffn_w2': _L0_ffn_in['w2'], 'L0_ffn_w3': _L0_ffn_in['w3']}

def reference(x, txt, L0_tok_W, L0_attn_ln1_g, L0_attn_ln1_b, L0_attn_qkv_w, L0_attn_qkv_b, L0_attn_bias_table, L0_attn_scale, L0_attn_proj_w, L0_attn_proj_b, L0_attn_ln2_g, L0_attn_ln2_b, L0_ffn_ln1_w, L0_ffn_ln2_w, L0_ffn_wq, L0_ffn_wk, L0_ffn_wv, L0_ffn_wo, L0_ffn_router_w, L0_ffn_w1, L0_ffn_w2, L0_ffn_w3):
    import jax
    import jax.numpy as jnp

    def _L0_tok_ref(x, W):
        import jax, jax.numpy as jnp
        import numpy as np
        PATCH_LEN = 16
        STRIDE = 8
        PAD = 8
        B, C, T, V = x.shape
        xp = jnp.pad(x, ((0, 0), (0, 0), (0, PAD), (0, 0)), mode='edge')
        Tp = T + PAD
        N = (Tp - PATCH_LEN) // STRIDE + 1
        idx = jnp.arange(N)[:, None] * STRIDE + jnp.arange(PATCH_LEN)[None, :]
        patches = xp[:, :, idx, :]
        patches = jnp.transpose(patches, (0, 4, 2, 3, 1))
        xf = jnp.fft.rfft(patches, axis=-2, norm='ortho')
        F = xf.shape[-2]
        x_real = xf.real.reshape(B, V, N, F * C)
        x_imag = xf.imag.reshape(B, V, N, F * C)
        x_emb = jnp.concatenate([x_real, x_imag], axis=-1)
        x_emb = x_emb @ W.T
        return x_emb.reshape(B, V * N, -1)

    def _L0_attn_ref(x, ln1_g, ln1_b, qkv_w, qkv_b, bias_table, scale, proj_w, proj_b, ln2_g, ln2_b):
        import jax, jax.numpy as jnp
        import numpy as np
        SEQ_LEN = 512
        EMBED_DIM = 64
        BATCH = 8
        LN_EPS = 1e-05

        def _layernorm(x, g, b):
            mu = jnp.mean(x, axis=-1, keepdims=True)
            var = jnp.mean(jnp.square(x - mu), axis=-1, keepdims=True)
            return (x - mu) * jax.lax.rsqrt(var + LN_EPS) * g + b
        B, N, C = x.shape
        h = _layernorm(x, ln1_g, ln1_b)
        qkv = h @ qkv_w + qkv_b
        q, k, v = jnp.split(qkv, 3, axis=-1)
        coords = jnp.arange(N)
        rel_idx = coords[None, :] - coords[:, None] + (N - 1)
        rel_bias = bias_table[rel_idx]
        attn = jnp.einsum('bnc,bmc->bnm', q, k) + rel_bias
        attn = jax.nn.softmax(attn, axis=-1) * scale
        out = jnp.einsum('bnm,bmc->bnc', attn, v)
        out = out @ proj_w + proj_b
        out = _layernorm(out, ln2_g, ln2_b)
        return out

    def _L0_ffn_ref(x, ln1_w, ln2_w, wq, wk, wv, wo, router_w, w1, w2, w3):
        import jax, jax.numpy as jnp
        import numpy as np
        B, T, C = (64, 96, 64)
        NH, NKV = (4, 2)
        HD = C // NH
        NREP = NH // NKV
        NE, TOPK = (8, 2)
        HID = int(8 / 3 * C)
        EPS_RMS = 1e-06

        def _rope_tables(t_len):
            inv_freq = 1.0 / 10000.0 ** (np.arange(0, HD, 2, dtype=np.float32) / HD)
            t = np.arange(t_len, dtype=np.float32)
            freqs = np.outer(t, inv_freq)
            emb = np.concatenate([freqs, freqs], axis=-1)
            return (jnp.asarray(np.cos(emb)), jnp.asarray(np.sin(emb)))

        def _rotate_half(x):
            h = x.shape[-1] // 2
            return jnp.concatenate([-x[..., h:], x[..., :h]], axis=-1)

        def _rmsnorm(v, w):
            return v * jax.lax.rsqrt(jnp.mean(v * v, axis=-1, keepdims=True) + EPS_RMS) * w
        Bx, Tx, Cx = x.shape
        h = _rmsnorm(x, ln1_w)
        q = (h @ wq.T).reshape(Bx, Tx, NH, HD).transpose(0, 2, 1, 3)
        k = (h @ wk.T).reshape(Bx, Tx, NKV, HD).transpose(0, 2, 1, 3)
        v = (h @ wv.T).reshape(Bx, Tx, NKV, HD).transpose(0, 2, 1, 3)
        cos, sin = _rope_tables(Tx)
        cos, sin = (cos[None, None], sin[None, None])
        q = q * cos + _rotate_half(q) * sin
        k = k * cos + _rotate_half(k) * sin
        k = jnp.repeat(k, NREP, axis=1)
        v = jnp.repeat(v, NREP, axis=1)
        scores = jnp.einsum('bhtd,bhsd->bhts', q, k) / jnp.sqrt(jnp.float32(HD))
        causal = jnp.tril(jnp.ones((Tx, Tx), dtype=bool))
        scores = jnp.where(causal[None, None], scores, jnp.float32(-1e+30))
        att = jax.nn.softmax(scores, axis=-1)
        y = jnp.einsum('bhts,bhsd->bhtd', att, v).transpose(0, 2, 1, 3).reshape(Bx, Tx, Cx)
        x = x + y @ wo.T
        flat = _rmsnorm(x, ln2_w).reshape(-1, Cx)
        probs = jax.nn.softmax(flat @ router_w.T, axis=-1)
        tp, ti = jax.lax.top_k(probs, TOPK)
        tp = tp / (jnp.sum(tp, axis=-1, keepdims=True) + 1e-09)
        weights = jnp.sum(tp[..., None] * jax.nn.one_hot(ti, NE, dtype=flat.dtype), axis=1)
        out = jnp.zeros_like(flat)
        for e in range(NE):
            hh = jax.nn.silu(flat @ w1[e].T) * (flat @ w3[e].T)
            out = out + weights[:, e:e + 1] * (hh @ w2[e].T)
        return x + out.reshape(Bx, Tx, Cx)
    h = _L0_tok_ref(x, L0_tok_W)
    h = jnp.concatenate([h, txt], axis=1)
    h = h + _L0_attn_ref(_layernorm(h, axis=-1), L0_attn_ln1_g, L0_attn_ln1_b, L0_attn_qkv_w, L0_attn_qkv_b, L0_attn_bias_table, L0_attn_scale, L0_attn_proj_w, L0_attn_proj_b, L0_attn_ln2_g, L0_attn_ln2_b)
    h = h + _L0_ffn_ref(_layernorm(h, axis=-1), L0_ffn_ln1_w, L0_ffn_ln2_w, L0_ffn_wq, L0_ffn_wk, L0_ffn_wv, L0_ffn_wo, L0_ffn_router_w, L0_ffn_w1, L0_ffn_w2, L0_ffn_w3)
    return h

_drawn_inputs = setup_inputs


def setup_inputs(seed=0):
    import zlib

    import numpy as np

    out = dict(_drawn_inputs(seed))
    spreads = {'L0_attn_ln1_g': (1.0, 0.6),
     'L0_attn_ln1_b': (0.0, 0.8),
     'L0_attn_qkv_b': (0.0, 0.429),
     'L0_attn_proj_b': (0.0, 0.1),
     'L0_attn_ln2_g': (1.0, 0.2),
     'L0_attn_ln2_b': (0.0, 0.1),
     'L0_ffn_ln1_w': (1.0, 0.6),
     'L0_ffn_ln2_w': (1.0, 0.6)}
    factors = {'L0_attn_qkv_w': 8.0,
     'L0_attn_bias_table': 8.0,
     'L0_attn_proj_w': 3.34,
     'L0_ffn_wq': 8.0,
     'L0_ffn_wk': 8.0,
     'L0_ffn_wv': 4.869,
     'L0_ffn_wo': 4.577,
     'L0_ffn_router_w': 8.0,
     'L0_ffn_w1': 8.0,
     'L0_ffn_w2': 8.0,
     'L0_ffn_w3': 8.0}
    for name, (base, spread) in spreads.items():
        noise = np.random.default_rng([zlib.crc32(name.encode()), seed]).standard_normal(out[name].shape)
        drawn = base * np.exp(spread * noise) if base else spread * noise
        out[name] = jnp.asarray(drawn.astype(out[name].dtype))
    for name, factor in factors.items():
        out[name] = (out[name] * factor).astype(out[name].dtype)
    return out
```

```python
from contextlib import ExitStack

import concourse.bass as bass
from concourse import mybir

F32 = mybir.dt.float32
BF16 = mybir.dt.bfloat16
ALU = mybir.AluOpType
ACT = mybir.ActivationFunctionType
AX = mybir.AxisListType

B, C, TIME, V = 4, 64, 128, 64
TXT = 32
PATCH, STRIDE = 16, 8
NPATCH = TIME // STRIDE
NFREQ = PATCH // 2 + 1
TOK = V * NPATCH + TXT
P = 128
NT = (TOK + P - 1) // P
FULL = TOK // P
REST = TOK - FULL * P
SPAN = 1023
LN_EPS, RMS_EPS = 1e-5, 1e-6
NH, NKV, HD = 4, 2, 16
NE, HID = 8, 170
ROWS = NE * HID
NC = (ROWS + P - 1) // P
FS = 64
HALF = 4
G1, B1, BQKV, BPROJ, G2, B2, FW1, FW2 = 0, 64, 128, 320, 384, 448, 512, 576
NPAR = 640
K_ID, K_FLIP, K_MS, K_MT, K_COS, K_SIN, K_DESC, K_HALF = 0, 128, 256, 384, 512, 656, 800, 808
NCONST = 809
W_QKV2, W_WO, W_ROUTER, W_ONE, W_THREE = 0, 1, 2, 3, 3 + NC
NWT = 3 + 2 * NC
BIAS_PAD = 96
BIAS_W = NT * P
BIAS_LEN = BIAS_W + P - 1
PT_RING = 12
CHUNK_TILES = 3
CW = CHUNK_TILES * P


def tokens(i):
    return P if i < FULL else REST


def rows_of(c):
    return min(P, ROWS - c * P)


def w2_blocks():
    out, blk = [], 0
    for c in range(NC):
        e0, e1 = c * P // HID, (c * P + rows_of(c) - 1) // HID
        out.append((c, e0, e1 - e0 + 1, blk))
        blk += e1 - e0 + 1
    return out, blk


W2B, NBLK = w2_blocks()

A1_S = [(0, 384), (384, 768), (768, TOK)]
A1_K = [range(0, 4), range(4, 8), range(8, 9)]


def a2_s(i):
    n = min(TOK, (i + 1) * P)
    parts = (n + 511) // 512
    return [(n * g // parts, n * (g + 1) // parts) for g in range(parts)]


def a2_k(i):
    return [range(a, min(a + 4, i + 1)) for a in range(0, i + 1, 4)]


def program(nc, A, out):
    ctx = ExitStack()
    with ctx:
        def sb(name, shape, dt=F32):
            return ctx.enter_context(nc.sbuf_tensor(name, shape, dt))

        sems = []

        def sem(name):
            s = ctx.enter_context(nc.semaphore(name))
            sems.append(s)
            return s

        bank = [ctx.enter_context(nc.psum_tensor(f"bank{i}", [P, 512], F32)) for i in range(8)]
        bankb = [b[:, :].bitcast(BF16) for b in bank]

        const = sb("const", [P, NCONST])
        ident = const[:, K_ID:K_ID + P]
        identb = sb("identb", [P, P], BF16)
        flipb = sb("flipb", [P, P], BF16)
        mask_s = sb("mask_s", [P, P], BF16)
        mask_t = sb("mask_t", [P, P], BF16)
        par = sb("par", [P, NPAR])
        scale = sb("scale", [P, 1])
        dft = sb("dft", [2 * NFREQ, PATCH])
        w_tok = sb("w_tok", [P, HALF, 2, C])
        wa_hi, wa_lo = sb("wa_hi", [P, 256], BF16), sb("wa_lo", [P, 256], BF16)
        wt_hi, wt_lo = sb("wt_hi", [P, NWT * P], BF16), sb("wt_lo", [P, NWT * P], BF16)
        w2s = sb("w2s", [P, NBLK * C])
        rel_hi, rel_lo = sb("rel_hi", [P, BIAS_W], BF16), sb("rel_lo", [P, BIAS_W], BF16)

        xs = sb("xs", [P, NPATCH, HALF, V])
        xpad = sb("xpad", [P, V])
        h_feat = sb("h_feat", [C, V, NPATCH])
        h0 = sb("h0", [P, NT, C])
        xc = sb("xc", [P, NT, C])
        sq = sb("sq", [P, NT, C])
        hn = sb("hn", [P, NT, C])
        h1 = sb("h1", [P, NT, C])
        xl = sb("xl", [P, NT, C])
        x1 = sb("x1", [P, NT, C])
        stat = sb("stat", [P, 8, NT])
        hl = sb("hl", [P, NT, P], BF16)
        ht = sb("ht", [P, TOK], BF16)
        qkv = sb("qkv", [P, NT, 192])
        ql = sb("ql", [P, NT, P], BF16)
        qb = sb("qb", [P, NT, C + 2], BF16)
        ka = sb("ka", [P, NT, P], BF16)
        kb = sb("kb", [P, NT, C + 2], BF16)
        qt, qm = sb("qt", [P, TOK], BF16), sb("qm", [C + 2, TOK], BF16)
        kt1, kt2 = sb("kt1", [P, TOK], BF16), sb("kt2", [C + 2, TOK], BF16)
        v1 = sb("v1", [P, NT, C + 1])
        ao = sb("ao", [P, NT, C])
        rope = sb("rope", [P, 2, NT, 96])
        fqb = sb("fqb", [P, NT, 4, FS], BF16)
        fkb = sb("fkb", [P, NT, 2, FS], BF16)
        fq, fqm = sb("fq", [P, 2, TOK], BF16), sb("fqm", [P, 2, TOK], BF16)
        fk = sb("fk", [P, TOK], BF16)
        vf = sb("vf", [P, NT, NKV, HD + 1])
        pmax = sb("pmax", [P, 4, 4])
        rmax = sb("rmax", [P, NT, 4])
        rec = sb("rec", [P, 4])
        pt = sb("pt", [P, PT_RING, 512])
        gate_l = sb("gate_l", [P, NT, NE])
        gate_p = sb("gate_p", [P, NT, NE])
        gate_e = sb("gate_e", [P, NT, NE])
        gate_m = sb("gate_m", [P, NT, NE])
        gate_w = sb("gate_w", [P, NT, NE])
        gate_s = sb("gate_s", [P, 6, NT])
        silu = sb("silu", [P, 4, CW])
        hid = sb("hid", [P, NC, TOK])
        gated = sb("gated", [P, 2, NE * C])
        res = sb("res", [P, NT, C])

        hidf = hid[:, :, :].rearrange("p a b -> p (a b)")
        w_raw = hidf[0:2 * NFREQ, 0:C * P].rearrange("p (o c) -> p o c", o=C)
        nat = hidf[:, C * P:C * P + NWT * P].rearrange("p (k c) -> p k c", k=NWT)
        ptf = pt[:, :, :].rearrange("p a b -> p (a b)")
        c2 = ptf[0:C, 0:ROWS]
        c2b = ptf[0:C, ROWS:ROWS + NBLK * P].rearrange("p (k c) -> p k c", k=NBLK)
        used = ROWS + NBLK * P
        rel = ptf[:, used:used + BIAS_W]
        w_a = ptf[:, used + BIAS_W:used + BIAS_W + 256]
        ext = nc.dram_tensor("bias_ext", (1, BIAS_LEN), F32, kind="Internal").ap()

        def par_b(off, n=C, tiles=NT, np_=P):
            return par[0:np_, off:off + n].unsqueeze(1).to_broadcast([np_, tiles, n])

        def per_token(ap, n):
            return ap.unsqueeze(2).to_broadcast([ap.shape[0], ap.shape[1], n])

        def load_x(sp, b, s):
            v = A["x"][b].rearrange("c (u j q) v -> j c u (q v)", j=2, q=HALF)
            for j in range(2):
                sp.dma_start(xs[64 * j:64 * j + 64, :, :, :].rearrange("p u q v -> p u (q v)"),
                             v[j]).then_inc(s, 16)
                sp.dma_start(xpad[64 * j:64 * j + 64, :], A["x"][b][:, TIME - 1, :]).then_inc(s, 16)

        s_const, s_w, s_nat, s_c2, s_ext, s_x = (sem(n) for n in (
            "s_const", "s_w", "s_nat", "s_c2", "s_ext", "s_x"))
        s_rel, s_cast, s_zero, s_c2b = sem("s_rel"), sem("s_cast"), sem("s_zero"), sem("s_c2b")
        s_tokw, s_tokc, s_trn, s_hi, s_lo, s_wa = (sem(n) for n in (
            "s_tokw", "s_tokc", "s_trn", "s_hi", "s_lo", "s_wa"))
        NLOADW = 2 + 2 + 2 + 9
        wt_banks = [range(a, min(a + 4, NWT)) for a in range(0, NWT, 4)]
        w2_banks = [range(a, min(a + 8, NBLK)) for a in range(0, NBLK, 8)]

        def nat_rows(k):
            return {W_QKV2: P, W_WO: C, W_ROUTER: NE}.get(k) or rows_of((k - W_ONE) % NC)

        with nc.Block() as block:
            @block.sync
            def _(sp):
                tab = A["bias_table"]
                sp.dma_start(ext[:, 0:BIAS_PAD], tab[:, 0:BIAS_PAD]).then_inc(s_ext, 16)
                sp.dma_start(ext[:, BIAS_PAD:BIAS_PAD + SPAN], tab).then_inc(s_ext, 16)
                tail = BIAS_LEN - BIAS_PAD - SPAN
                sp.dma_start(ext[:, BIAS_PAD + SPAN:].unsqueeze(2),
                             tab[:, SPAN - 1:SPAN].unsqueeze(1).to_broadcast([1, tail, 1])).then_inc(s_ext, 16)
                sp.dma_start(const[:, :], A["const"]).then_inc(s_const, 16)
                sp.dma_start(dft[:, :], A["dft"]).then_inc(s_w, 16)
                sp.dma_start(scale[:, :], A["attn_scale"].to_broadcast([P, 1])).then_inc(s_w, 16)
                wv = A["tok_w"].rearrange("o (f c) -> f o c", c=C)
                for d in range(2):
                    sp.dma_start(w_raw[:, :, C * d:C * d + C], wv).then_inc(s_w, 16)
                for off, name, n in ((G1, "ln1_g", C), (B1, "ln1_b", C), (BQKV, "qkv_b", 192), (BPROJ, "proj_b", C),
                                     (G2, "ln2_g", C), (B2, "ln2_b", C), (FW1, "f_ln1", C), (FW2, "f_ln2", C)):
                    sp.dma_start(par[:, off:off + n], A[name].to_broadcast([P, n])).then_inc(s_w, 16)
                load_x(sp, 0, s_x)
                sp.wait_ge(s_ext, 48)
                sp.dma_start(rel[:, :], bass.AP(ext.tensor, 0, [[1, P], [1, BIAS_W]])).then_inc(s_rel, 16)
                sp.wait_ge(s_x, 64)

            @block.scalar
            def _(act):
                for d in range(2):
                    act.dma_start(w_a[64 * d:64 * d + 64, 0:192], A["qkv_w"]).then_inc(s_wa, 16)
                    act.dma_start(w_a[64 * d:64 * d + 64, 192:256], A["proj_w"]).then_inc(s_wa, 16)
                act.dma_start(c2[:, :].rearrange("c (e h) -> c e h", e=NE), A["w2"].rearrange("e c h -> c e h")).then_inc(s_c2, 16)
                for d in range(2):
                    cols = slice(64 * d, 64 * d + 64)
                    for h in range(NH):
                        slot = (h % 2) * 2 + h // 2
                        act.dma_start(nat[HD * slot:HD * slot + HD, W_QKV2, cols], A["wq"][HD * h:HD * h + HD, :]).then_inc(s_nat, 16)
                    act.dma_start(nat[64:96, W_QKV2, cols], A["wk"]).then_inc(s_nat, 16)
                    act.dma_start(nat[96:128, W_QKV2, cols], A["wv"]).then_inc(s_nat, 16)
                    act.dma_start(nat[0:C, W_WO, cols], A["wo"]).then_inc(s_nat, 16)
                    act.dma_start(nat[0:NE, W_ROUTER, cols], A["router_w"]).then_inc(s_nat, 16)
                    for first, name in ((W_ONE, "w1"), (W_THREE, "w3")):
                        w = A[name].rearrange("e h c -> (e h) c")
                        act.dma_start(nat[:, first:first + NC - 1, cols],
                                      w[0:(NC - 1) * P, :].rearrange("(k p) c -> p k c", p=P)).then_inc(s_nat, 16)
                        act.dma_start(nat[0:rows_of(NC - 1), first + NC - 1, cols],
                                      w[(NC - 1) * P:, :]).then_inc(s_nat, 16)
                for n, ks in enumerate(wt_banks):
                    act.wait_ge(s_trn, n + 1)
                    for k in ks:
                        r = nat_rows(k)
                        last = nc.scalar.copy(wt_hi[:, k * P:k * P + r], bank[n % 4][:, (k % 4) * P:(k % 4) * P + r])
                    last.then_inc(s_hi, 1)

            @block.gpsimd
            def _(pool):
                for t in (h0, hn, h1, xl, x1, ao, qkv, gate_l, sq, xc):
                    nc.gpsimd.memset(t[:, :, :], 0.0)
                for t in (hl, ql, ka, qb):
                    nc.gpsimd.memset(t[:, :, :], 0.0)
                nc.gpsimd.memset(rope[:, :, :, :], 0.0)
                nc.gpsimd.memset(rmax[:, :, :], 0.0)
                nc.gpsimd.memset(fqb[:, :, :, :], 0.0)
                for t, at in ((kb, C), (fkb, 3 * HD)):
                    v = t[:, :, :] if t is kb else t[:, :, :, :].rearrange("p t g c -> p (t g) c")
                    nc.gpsimd.memset(v, 0.0).then_inc(s_zero, 1)
                pool.wait_ge(s_zero, 2)
                for t, at in ((kb, C), (fkb, 3 * HD)):
                    v = t[:, :, :] if t is kb else t[:, :, :, :].rearrange("p t g c -> p (t g) c")
                    nc.gpsimd.memset(v[:, :, at:at + 1], 1.0)
                    nc.gpsimd.memset(v[:, :, at + 1:at + 2], -1.0)
                nc.gpsimd.memset(v1[:, :, :], 1.0)
                nc.gpsimd.memset(vf[:, :, :, :], 1.0)
                nc.gpsimd.memset(c2b[:, :, :], 0.0).then_inc(s_zero, 1)
                pool.wait_ge(s_zero, 3)
                pool.wait_ge(s_c2, 16)
                for c, e0, ne, blk in W2B:
                    for e in range(e0, e0 + ne):
                        a, z = max(c * P, e * HID), min(c * P + rows_of(c), (e + 1) * HID)
                        last = nc.gpsimd.tensor_copy(c2b[:, blk + e - e0, a - c * P:z - c * P], c2[:, a:z])
                last.then_inc(s_c2b, 1)

            @block.tensor
            def _(pe):
                pe.wait_ge(s_w, 16 * 12)
                for o in range(C):
                    last = nc.tensor.matmul(bank[4 + o // 32][:, (o % 32) * PATCH:(o % 32 + 1) * PATCH], w_raw[:, o, :], dft[:, :],
                                            start=True, stop=True)
                    if o % 32 == 31:
                        last.then_inc(s_tokw, 1)
                pe.wait_ge(s_const, 16)
                pe.wait_ge(s_nat, 16 * 24)
                for n, ks in enumerate(wt_banks):
                    if n >= 4:
                        pe.wait_ge(s_lo, n - 3)
                    for k in ks:
                        r = nat_rows(k)
                        last = nc.tensor.transpose(bank[n % 4][:, (k % 4) * P:(k % 4) * P + r], nat[0:r, k, :], ident[0:r, 0:r])
                    last.then_inc(s_trn, 1)
                pe.wait_ge(s_c2b, 1)
                pe.wait_ge(s_tokc, 4)
                for n, ks in enumerate(w2_banks):
                    for k in ks:
                        last = nc.tensor.transpose(bank[4 + n][:, (k % 8) * C:(k % 8 + 1) * C], c2b[:, k, :], ident[0:C, 0:C])
                    last.then_inc(s_trn, 1)

            @block.vector
            def _(dve):
                dve.wait_ge(s_const, 16)
                for dst, off in ((identb, K_ID), (flipb, K_FLIP), (mask_s, K_MS), (mask_t, K_MT)):
                    nc.vector.tensor_copy(dst[:, :], const[:, off:off + P])
                for n in range(2):
                    dve.wait_ge(s_tokw, n + 1)
                    src = bank[4 + n][:, :].rearrange("p (o l j q) -> p j q l o", l=2, j=2, q=HALF)
                    for j in range(2):
                        for late in range(2):
                            last = nc.vector.tensor_copy(w_tok[64 * j:64 * j + 64, :, late, 32 * n:32 * n + 32],
                                                         src[64 * j:64 * j + 64, j, :, late, :])
                        last.then_inc(s_tokc, 1)
                dve.wait_ge(s_wa, 64)
                nc.vector.tensor_copy(wa_hi[:, :], w_a[:, :]).then_inc(s_cast, 1)
                dve.wait_ge(s_cast, 1)
                nc.vector.tensor_tensor(wa_lo[:, :], w_a[:, :], wa_hi[:, :], ALU.subtract)
                dve.wait_ge(s_rel, 16)
                nc.vector.tensor_scalar(rel[:, 0:BIAS_W - 1], rel[:, 0:BIAS_W - 1], rel[:, BIAS_W - 1:BIAS_W], None,
                                        ALU.subtract).then_inc(s_cast, 1)
                dve.wait_ge(s_cast, 2)
                nc.vector.memset(rel[:, BIAS_W - 1:BIAS_W], 0.0).then_inc(s_cast, 1)
                dve.wait_ge(s_cast, 3)
                nc.vector.tensor_copy(rel_hi[:, :], rel[:, :]).then_inc(s_cast, 1)
                dve.wait_ge(s_cast, 4)
                nc.vector.tensor_tensor(rel_lo[:, :], rel[:, :], rel_hi[:, :], ALU.subtract)
                for n, ks in enumerate(wt_banks):
                    dve.wait_ge(s_hi, n + 1)
                    for k in ks:
                        r = nat_rows(k)
                        last = nc.vector.tensor_tensor(wt_lo[:, k * P:k * P + r], bank[n % 4][:, (k % 4) * P:(k % 4) * P + r],
                                                       wt_hi[:, k * P:k * P + r], ALU.subtract)
                    last.then_inc(s_lo, 1)
                for n, ks in enumerate(w2_banks):
                    dve.wait_ge(s_trn, len(wt_banks) + n + 1)
                    w = len(ks) * C
                    nc.vector.tensor_copy(w2s[:, ks[0] * C:ks[0] * C + w], bank[4 + n][:, 0:w])

        s_txt, s_tok, s_early, s_sum, s_tokT, s_xnext, s_out = (sem(n) for n in (
            "s_txt", "s_tok", "s_early", "s_sum", "s_tokT", "s_xnext", "s_out"))
        s_dve, s_pool, s_norm, s_hl, s_hlT, s_ht, s_proj = (sem(n) for n in (
            "s_dve", "s_pool", "s_norm", "s_hl", "s_hlT", "s_ht", "s_proj"))
        s_raw, s_split, s_splitA, s_splitD, s_stkT, s_stk = (sem(n) for n in (
            "s_raw", "s_split", "s_splitA", "s_splitD", "s_stkT", "s_stk"))
        s_sc, s_red, s_max, s_mrow, s_mT, s_m, s_st, s_exp, s_avg, s_av, s_ao = (sem(n) for n in (
            "s_sc", "s_red", "s_max", "s_mrow", "s_mT", "s_m", "s_st", "s_exp", "s_avg", "s_av", "s_ao"))
        s_rope, s_router, s_logit, s_gexp, s_ab, s_silu, s_u, s_w2, s_gated, s_res, s_h1 = (sem(n) for n in (
            "s_rope", "s_router", "s_logit", "s_gexp", "s_ab", "s_silu", "s_u", "s_w2", "s_gated", "s_res", "s_h1"))

        a1_s0 = [len(A1_S) * i for i in range(NT)]
        a1_k0 = [len(A1_K) * i for i in range(NT)]
        a2_s0, a2_k0 = [], []
        ns, nk = len(A1_S) * NT, len(A1_K) * NT
        for i in range(NT):
            a2_s0.append([ns + h * len(a2_s(i)) for h in range(NH)])
            a2_k0.append([nk + h * len(a2_k(i)) for h in range(NH)])
            ns += NH * len(a2_s(i))
            nk += NH * len(a2_k(i))

        N_AB = CHUNK_TILES * NC

        def chunk_cols(t):
            return t * CW, min((t + 1) * CW, TOK)

        W2_AFTER = {3: 0, 6: 1, 9: 2}

        with nc.Fori(0, B) as b:
            with nc.Block() as block:
                @block.sync
                def _(sp):
                    sp.dma_start(h0[0:TXT, FULL, :], A["txt"][b]).then_inc(s_txt, 16)
                    sp.wait_ge(s_tok, 3)
                    load_x(sp, (b + 1) % B, s_xnext)
                    sp.wait_ge(s_res, NT)
                    sp.dma_start(out[b][0:FULL * P, :].rearrange("(i p) c -> p i c", p=P), res[:, 0:FULL, :]).then_inc(s_out, 16)
                    sp.dma_start(out[b][FULL * P:, :], res[0:REST, FULL, :]).then_inc(s_out, 16)
                    sp.wait_ge(s_out, 32)
                    sp.wait_ge(s_xnext, 64)

                @block.tensor
                def _(pe):
                    for g in range(3):
                        for q in range(HALF):
                            if g < 2:
                                dst = bank[g][:, :].rearrange("p (u v) -> p u v", v=V)
                                src = xs[:, 8 * g:8 * g + 8, q, :]
                            else:
                                dst, src = bank[2][:, 0:V], xpad[:, :]
                            last = nc.tensor.matmul(dst, w_tok[:, q, :, :].rearrange("p l o -> p (l o)"), src,
                                                    start=(q == 0), stop=(q == HALF - 1))
                        last.then_inc(s_tok, 1)
                    pe.wait_ge(s_sum, 3)
                    hf = h_feat[:, :, :].rearrange("c v n -> c (v n)")
                    for i in range(FULL):
                        last = nc.tensor.transpose(bank[3][:, C * i:C * i + C], hf[:, P * i:P * i + P], ident[0:C, 0:C])
                    last.then_inc(s_tokT, 1)

                    def turn_hl(n):
                        pe.wait_ge(s_hl, n)
                        for i in range(NT):
                            w = tokens(i)
                            dst = bankb[0][:, P * i:P * i + w] if i < FULL else bankb[1][:, 0:w]
                            last = nc.tensor.transpose(dst, hl[0:w, i, :], identb[0:w, 0:w])
                        last.then_inc(s_hlT, 1)

                    def project(n, w_hi, w_lo, cols, per_bank, first_bank):
                        pe.wait_ge(s_ht, 2 * n)
                        for i in range(NT):
                            w = tokens(i)
                            dst = bank[first_bank + i // per_bank][0:w, (i % per_bank) * cols:(i % per_bank + 1) * cols]
                            nc.tensor.matmul(dst, ht[:, P * i:P * i + w], w_hi, start=True, stop=False)
                            last = nc.tensor.matmul(dst, ht[:, P * i:P * i + w], w_lo, start=False, stop=True)
                            if i % per_bank == per_bank - 1 or i == NT - 1:
                                last.then_inc(s_proj, 1)

                    def turn_stacks(n, parts):
                        for k, (src, rows) in enumerate(parts):
                            for i in range(FULL):
                                last = nc.tensor.transpose(bankb[(0, 2, 3)[k]][0:rows, P * i:P * i + P], src(i), identb[:, :])
                            last.then_inc(s_stkT, 1)
                        for k, (src, rows) in enumerate(parts):
                            last = nc.tensor.transpose(bankb[1][0:rows, P * k:P * k + REST], src(FULL)[0:REST], identb[0:REST, 0:REST])
                        last.then_inc(s_stkT, 1)

                    def score_bank(g):
                        if g >= 3:
                            pe.wait_ge(s_red, g - 2)
                        return bank[g % 3]

                    def exp_bank(g):
                        if g >= 3:
                            pe.wait_ge(s_exp, g - 2)
                        return bank[3 + g % 3]

                    turn_hl(1)
                    project(1, wa_hi[:, 0:192], wa_lo[:, 0:192], 192, 2, 2)
                    pe.wait_ge(s_split, 2)
                    pe.wait_ge(s_splitA, 2)
                    turn_stacks(1, [(lambda i: ql[:, i, :], P), (lambda i: ka[:, i, :], P), (lambda i: kb[:, i, :], C + 2)])
                    pe.wait_ge(s_stk, 6)

                    def a1_scores(i):
                        w, q0 = tokens(i), P * i
                        for n, (k0, k1) in enumerate(A1_S):
                            dst = score_bank(a1_s0[i] + n)
                            bend = min(k1, q0 + w)
                            nc.tensor.matmul(dst[0:w, 0:k1 - k0], qt[:, q0:q0 + w], kt1[:, k0:k1], start=True, stop=False)
                            last = nc.tensor.matmul(dst[0:w, 0:k1 - k0], qt[0:C, q0:q0 + w], kt2[0:C, k0:k1],
                                                    start=False, stop=(bend <= k0))
                            if bend > k0:
                                y = BIAS_W - P - q0 + k0
                                for r in (rel_hi, rel_lo):
                                    last = nc.tensor.matmul(dst[0:w, 0:bend - k0], flipb[:, 0:w], r[:, y:y + bend - k0],
                                                            start=False, stop=(r is rel_lo))
                            last.then_inc(s_sc, 1)

                    def a1_turn_max(i):
                        pe.wait_ge(s_mrow, i + 1)
                        if i >= 1:
                            pe.wait_ge(s_m, i)
                        w = tokens(i)
                        nc.tensor.transpose(bankb[7][0:C + 2, 0:w], qb[0:w, i, :], identb[0:w, 0:w]).then_inc(s_mT, 1)

                    def a1_exponents(i):
                        pe.wait_ge(s_m, i + 1)
                        w, q0 = tokens(i), P * i
                        for n, keys in enumerate(A1_K):
                            dst = exp_bank(a1_k0[i] + n)
                            for jj, j in enumerate(keys):
                                kw, o = tokens(j), dst[0:tokens(j), P * jj:P * jj + w]
                                nc.tensor.matmul(o, kt1[:, P * j:P * j + kw], qt[:, q0:q0 + w], start=True, stop=False)
                                last = nc.tensor.matmul(o, kt2[:, P * j:P * j + kw], qm[:, q0:q0 + w],
                                                        start=False, stop=(j > i))
                                if j <= i:
                                    y = BIAS_W - P - P * (i - j)
                                    for r in (rel_hi, rel_lo):
                                        last = nc.tensor.matmul(o, r[:, y:y + kw], flipb[:, 0:w], start=False, stop=(r is rel_lo))
                            last.then_inc(s_st, 1)

                    def a1_values(i):
                        if i >= 1:
                            pe.wait_ge(s_ao, i)
                        w = tokens(i)
                        for n, keys in enumerate(A1_K):
                            g = a1_k0[i] + n
                            pe.wait_ge(s_exp, g + 1)
                            for jj, j in enumerate(keys):
                                kw = tokens(j)
                                last = nc.tensor.matmul(bank[6][0:w, 0:C + 1], pt[0:kw, g % PT_RING, P * jj:P * jj + w],
                                                        v1[0:kw, j, :], start=(j == 0), stop=(j == NT - 1))
                            last.then_inc(s_avg, 1)

                    for i in range(NT + 2):
                        if i < NT:
                            a1_scores(i)
                        if 1 <= i <= NT:
                            a1_turn_max(i - 1)
                        if i >= 2:
                            a1_values(i - 2)
                        if 1 <= i <= NT:
                            a1_exponents(i - 1)

                    turn_hl(2)
                    project(2, wa_hi[:, 192:256], wa_lo[:, 192:256], C, 8, 2)

                    def wt(w, k, n):
                        return w[:, k * P:k * P + n]

                    turn_hl(3)
                    project(3, wt(wt_hi, W_QKV2, P), wt(wt_lo, W_QKV2, P), P, 4, 2)
                    pe.wait_ge(s_split, 4)
                    pe.wait_ge(s_splitA, 4)
                    turn_stacks(2, [(lambda i: fqb[:, i, 0:2, :].rearrange("p h c -> p (h c)"), P),
                                    (lambda i: fqb[:, i, 2:4, :].rearrange("p h c -> p (h c)"), P),
                                    (lambda i: fkb[:, i, :, :].rearrange("p h c -> p (h c)"), P)])
                    pe.wait_ge(s_stk, 12)

                    def a2_scores(i, h):
                        w, q0, pr, p0 = tokens(i), P * i, h // 2, FS * (h % 2)
                        groups = a2_s(i)
                        for n, (k0, k1) in enumerate(groups):
                            dst = score_bank(a2_s0[i][h] + n)
                            diag = n == len(groups) - 1
                            last = nc.tensor.matmul(dst[0:w, 0:k1 - k0], fq[p0:p0 + 3 * HD, pr, q0:q0 + w],
                                                    fk[p0:p0 + 3 * HD, k0:k1], start=True, stop=not diag)
                            if diag:
                                last = nc.tensor.matmul(dst[0:w, q0 - k0:q0 - k0 + w], identb[0:w, 0:w], mask_s[0:w, 0:w],
                                                        start=False, stop=True)
                            last.then_inc(s_sc, 1)

                    def a2_turn_max(i):
                        pe.wait_ge(s_mrow, NT + i + 1)
                        pe.wait_ge(s_m, NT + i)
                        w = tokens(i)
                        for pr in range(2):
                            last = nc.tensor.transpose(bankb[7][:, P * pr:P * pr + w],
                                                       fqb[0:w, i, 2 * pr:2 * pr + 2, :].rearrange("p h c -> p (h c)"),
                                                       identb[0:w, 0:w])
                        last.then_inc(s_mT, 1)

                    def a2_exponents(i, h):
                        pe.wait_ge(s_m, NT + i + 1)
                        w, q0, pr, p0, K = tokens(i), P * i, h // 2, FS * (h % 2), 3 * HD + 2
                        for n, keys in enumerate(a2_k(i)):
                            dst = exp_bank(a2_k0[i][h] + n)
                            for jj, j in enumerate(keys):
                                kw, o = tokens(j), dst[0:tokens(j), P * jj:P * jj + w]
                                last = nc.tensor.matmul(o, fk[p0:p0 + K, P * j:P * j + kw], fqm[p0:p0 + K, pr, q0:q0 + w],
                                                        start=True, stop=(j < i))
                                if j == i:
                                    last = nc.tensor.matmul(o, identb[0:kw, 0:kw], mask_t[0:kw, 0:w], start=False, stop=True)
                            last.then_inc(s_st, 1)

                    def a2_values(i, h):
                        if h == 0:
                            pe.wait_ge(s_ao, NT + i)
                        w = tokens(i)
                        for n, keys in enumerate(a2_k(i)):
                            g = a2_k0[i][h] + n
                            pe.wait_ge(s_exp, g + 1)
                            for jj, j in enumerate(keys):
                                kw = tokens(j)
                                last = nc.tensor.matmul(bank[6][0:w, (HD + 1) * h:(HD + 1) * (h + 1)],
                                                        pt[0:kw, g % PT_RING, P * jj:P * jj + w], vf[0:kw, j, h % 2, :],
                                                        start=(j == 0), stop=(j == i))
                            last.then_inc(s_avg, 1)

                    for i in range(NT + 2):
                        for h in range(NH):
                            if i < NT:
                                a2_scores(i, h)
                            if 1 <= i <= NT and h == 0:
                                a2_turn_max(i - 1)
                            if i >= 2:
                                a2_values(i - 2, h)
                            if 1 <= i <= NT:
                                a2_exponents(i - 1, h)

                    turn_hl(4)
                    project(4, wt(wt_hi, W_WO, C), wt(wt_lo, W_WO, C), C, 8, 2)

                    turn_hl(5)
                    pe.wait_ge(s_ht, 10)
                    for i in range(NT):
                        w = tokens(i)
                        for wgt in (wt_hi, wt_lo):
                            last = nc.tensor.matmul(bank[7][0:w, NE * i:NE * i + NE], ht[:, P * i:P * i + w],
                                                    wt(wgt, W_ROUTER, NE), start=(wgt is wt_hi), stop=(wgt is wt_lo))
                    last.then_inc(s_router, 1)

                    def up(t, c):
                        n, (a, z), r = t * NC + c, chunk_cols(t), rows_of(c)
                        if n >= 3:
                            pe.wait_ge(s_u, n - 2)
                        for k, first in ((0, W_ONE), (1, W_THREE)):
                            dst = bank[2 * (n % 3) + k][0:r, 0:z - a]
                            nc.tensor.matmul(dst, wt(wt_hi, first + c, r), ht[:, a:z], start=True, stop=False)
                            last = nc.tensor.matmul(dst, wt(wt_lo, first + c, r), ht[:, a:z], start=False, stop=True)
                        last.then_inc(s_ab, 1)

                    def down(i):
                        w, dst = tokens(i), bank[6 + i % 2]
                        pe.wait_ge(s_u, (i // CHUNK_TILES + 1) * NC)
                        if i == 1:
                            pe.wait_ge(s_logit, 2)
                        if i >= 2:
                            pe.wait_ge(s_gated, i - 1)
                        for c, e0, ne, blk in W2B:
                            r = rows_of(c)
                            last = nc.tensor.matmul(dst[0:w, C * e0:C * (e0 + ne)], hid[0:r, c, P * i:P * i + w],
                                                    w2s[0:r, C * blk:C * (blk + ne)], start=(c == 0), stop=(c == NC - 1),
                                                    skip_group_check=True)
                        last.then_inc(s_w2, 1)

                    for t in range(CHUNK_TILES):
                        for c in range(NC):
                            up(t, c)
                            if t >= 1 and c in W2_AFTER:
                                down(CHUNK_TILES * (t - 1) + W2_AFTER[c])
                    for k in range(CHUNK_TILES):
                        down(CHUNK_TILES * (CHUNK_TILES - 1) + k)

                @block.scalar
                def _(act):
                    for g in range(2):
                        act.wait_ge(s_tok, g + 1)
                        nc.scalar.copy(h_feat[:, :, 8 * g:8 * g + 8],
                                       bank[g][0:C, :].rearrange("p (u v) -> p v u", v=V)).then_inc(s_early, 1)

                    def take_ht(n):
                        act.wait_ge(s_hlT, n)
                        nc.scalar.copy(ht[:, 0:FULL * P], bankb[0][:, :]).then_inc(s_ht, 1)
                        nc.scalar.copy(ht[:, FULL * P:TOK], bankb[1][:, 0:REST]).then_inc(s_ht, 1)

                    take_ht(1)
                    act.wait_ge(s_raw, 5)
                    for dst in (ql, qb):
                        nc.scalar.copy(dst[:, :, 0:C], qkv[:, :, 0:C])
                    nc.scalar.copy(ka[:, :, 0:C], qkv[:, :, C:2 * C]).then_inc(s_splitA, 1)
                    nc.scalar.copy(ka[:, :, C:2 * C], qkv[:, :, C:2 * C]).then_inc(s_splitA, 1)
                    nc.scalar.copy(v1[:, 0:FULL, 0:C], qkv[:, 0:FULL, 2 * C:3 * C])
                    nc.scalar.copy(v1[0:REST, FULL, 0:C], qkv[0:REST, FULL, 2 * C:3 * C])
                    act.wait_ge(s_stkT, 1)
                    nc.scalar.copy(qt[:, 0:FULL * P], bankb[0][:, :]).then_inc(s_stk, 1)
                    act.wait_ge(s_stkT, 3)
                    nc.scalar.copy(kt2[:, 0:FULL * P], bankb[3][0:C + 2, :]).then_inc(s_stk, 1)

                    def exponent(g, rows, dst_of, scale_):
                        if g >= PT_RING:
                            act.wait_ge(s_avg, g - PT_RING + 1)
                        act.wait_ge(s_st, g + 1)
                        src = bank[3 + g % 3]
                        nc.scalar.activation(dst_of(pt[:, g % PT_RING, :]), dst_of(src[:, :]), ACT.Exp,
                                             scale=scale_).then_inc(s_exp, 1)

                    def block_view(keys, w):
                        kw, n = tokens(keys[-1]), len(keys)
                        return lambda t: t[0:kw, :].rearrange("p (j q) -> p j q", q=P)[:, 0:n, 0:w]

                    for i in range(NT):
                        w = tokens(i)
                        act.wait_ge(s_mT, i + 1)
                        nc.scalar.copy(qm[:, P * i:P * i + w], bankb[7][0:C + 2, 0:w]).then_inc(s_m, 1)
                        for n, keys in enumerate(A1_K):
                            exponent(a1_k0[i] + n, w, block_view(keys, w), 1.0)

                    take_ht(2)
                    take_ht(3)
                    act.wait_ge(s_proj, 5 + 2 + 1)
                    nc.scalar.copy(qkv[:, 0:4, 0:P], bank[2][:, :].rearrange("p (i n) -> p i n", n=P)).then_inc(s_raw, 1)
                    act.wait_ge(s_proj, 5 + 2 + 2)
                    nc.scalar.copy(qkv[:, 4:8, 0:P], bank[3][:, :].rearrange("p (i n) -> p i n", n=P)).then_inc(s_raw, 1)
                    act.wait_ge(s_proj, 5 + 2 + 3)
                    nc.scalar.copy(qkv[0:REST, 8, 0:P], bank[4][0:REST, 0:P]).then_inc(s_raw, 1)
                    act.wait_ge(s_raw, 8)
                    vv = qkv[:, :, 96:128].rearrange("p t (g c) -> p t g c", g=NKV)
                    for g in range(NKV):
                        nc.scalar.copy(vf[:, 0:FULL, g, 0:HD], vv[:, 0:FULL, g, :])
                        nc.scalar.copy(vf[0:REST, FULL, g, 0:HD], vv[0:REST, FULL, g, :])
                    act.wait_ge(s_rope, 2)
                    rq = rope[:, 0, :, 0:64].rearrange("p t (h c) -> p t h c", c=HD)
                    rk = rope[:, 0, :, 64:96].rearrange("p t (h c) -> p t h c", c=HD)
                    nc.scalar.copy(fqb[:, :, :, 0:HD], rq).then_inc(s_splitA, 1)
                    nc.scalar.copy(fkb[:, :, :, 0:HD], rk)
                    nc.scalar.copy(fqb[:, :, :, 2 * HD:3 * HD], rq)
                    nc.scalar.copy(fkb[:, :, :, HD:2 * HD], rk).then_inc(s_splitA, 1)
                    act.wait_ge(s_stkT, 5)
                    nc.scalar.copy(fq[:, 0, 0:FULL * P], bankb[0][:, :]).then_inc(s_stk, 1)
                    act.wait_ge(s_stkT, 7)
                    nc.scalar.copy(fk[:, 0:FULL * P], bankb[3][:, :]).then_inc(s_stk, 1)

                    for i in range(NT):
                        w = tokens(i)
                        act.wait_ge(s_mT, NT + i + 1)
                        nc.scalar.copy(fqm[:, :, P * i:P * i + w],
                                       bankb[7][:, 0:2 * P].rearrange("p (r q) -> p r q", q=P)[:, :, 0:w]).then_inc(s_m, 1)
                        for h in range(NH):
                            for n, keys in enumerate(a2_k(i)):
                                exponent(a2_k0[i][h] + n, w, block_view(keys, w), float(HD) ** -0.5)

                    take_ht(4)
                    take_ht(5)
                    act.wait_ge(s_logit, 3)
                    nc.scalar.activation(gate_e[:, :, :], gate_l[:, :, :], ACT.Exp).then_inc(s_gexp, 1)
                    for t in range(CHUNK_TILES):
                        a, z = chunk_cols(t)
                        for c in range(NC):
                            n, r = t * NC + c, rows_of(c)
                            act.wait_ge(s_ab, n + 1)
                            if n >= 4:
                                act.wait_ge(s_u, n - 3)
                            nc.scalar.activation(silu[0:r, n % 4, 0:z - a], bank[2 * (n % 3)][0:r, 0:z - a],
                                                 ACT.Silu).then_inc(s_silu, 1)

                @block.gpsimd
                def _(pool):
                    steps = [0]

                    def link(ins):
                        steps[0] += 1
                        ins.then_inc(s_pool, 1)
                        pool.wait_ge(s_pool, steps[0])

                    def split(src):
                        link(nc.gpsimd.tensor_copy(hl[:, :, 0:C], src[:, :, :]))
                        nc.gpsimd.tensor_tensor(hl[:, :, C:P], src[:, :, :], hl[:, :, 0:C], ALU.subtract).then_inc(s_hl, 1)

                    def normalize(dst, src, k):
                        half = const[:, K_HALF:K_HALF + 1].to_broadcast([P, NT])
                        link(nc.gpsimd.tensor_tensor(stat[:, 7, :], stat[:, k, :], half, ALU.pow))
                        link(nc.gpsimd.tensor_tensor(dst[:, :, :], src[:, :, :], per_token(stat[:, 7, :], C), ALU.mult))

                    pool.wait_ge(s_norm, 1)
                    normalize(hn, xc, 3)
                    link(nc.gpsimd.tensor_tensor(hn[:, :, :], hn[:, :, :], par_b(G1), ALU.mult))
                    link(nc.gpsimd.tensor_tensor(hn[:, :, :], hn[:, :, :], par_b(B1), ALU.add))
                    split(hn)
                    pool.wait_ge(s_splitA, 1)
                    nc.gpsimd.tensor_tensor(ql[:, :, C:P], qkv[:, :, 0:C], ql[:, :, 0:C], ALU.subtract).then_inc(s_split, 1)
                    nc.gpsimd.tensor_tensor(kb[:, :, 0:C], qkv[:, :, C:P], ka[:, :, 0:C], ALU.subtract).then_inc(s_split, 1)
                    for i in range(NT):
                        w = tokens(i)
                        pool.wait_ge(s_max, i + 1)
                        link(nc.gpsimd.tensor_scalar(qb[0:w, i, C:C + 1], rmax[0:w, i, 0:1], -1.0, None, ALU.mult))
                        nc.gpsimd.tensor_tensor(qb[0:w, i, C + 1:C + 2], rmax[0:w, i, 0:1], qb[0:w, i, C:C + 1],
                                                ALU.add).then_inc(s_mrow, 1)
                    pool.wait_ge(s_ao, NT)
                    split(ao)
                    pool.wait_ge(s_norm, 2)
                    normalize(hn, xc, 3)
                    link(nc.gpsimd.tensor_tensor(hn[:, :, :], hn[:, :, :], par_b(G2), ALU.mult))
                    link(nc.gpsimd.tensor_tensor(hn[:, :, :], hn[:, :, :], par_b(B2), ALU.add))
                    nc.gpsimd.tensor_tensor(h1[:, :, :], hn[:, :, :], h0[:, :, :], ALU.add).then_inc(s_h1, 1)
                    pool.wait_ge(s_norm, 3)
                    normalize(xl, xc, 3)
                    normalize(hn, xl, 5)
                    link(nc.gpsimd.tensor_tensor(hn[:, :, :], hn[:, :, :], par_b(FW1), ALU.mult))
                    split(hn)
                    pool.wait_ge(s_raw, 8)
                    qk = qkv[:, :, 0:96].rearrange("p t (h c) -> p t h c", c=HD)
                    rot = rope[:, 1, :, :].rearrange("p t (h c) -> p t h c", c=HD)
                    sin = const[:, K_SIN:K_SIN + NT * HD].rearrange("p (t c) -> p t c", c=HD)
                    for a, z in ((0, HD // 2), (HD // 2, HD)):
                        o = HD // 2 - a
                        last = nc.gpsimd.tensor_tensor(rot[:, :, :, a:z], qk[:, :, :, o:o + HD // 2],
                                                       sin[:, :, a:z].unsqueeze(2).to_broadcast([P, NT, 6, HD // 2]), ALU.mult)
                    last.then_inc(s_rope, 1)
                    pool.wait_ge(s_splitA, 4)
                    rq = rope[:, 0, :, 0:64].rearrange("p t (h c) -> p t h c", c=HD)
                    rk = rope[:, 0, :, 64:96].rearrange("p t (h c) -> p t h c", c=HD)
                    nc.gpsimd.tensor_tensor(fqb[:, :, :, HD:2 * HD], rq, fqb[:, :, :, 0:HD], ALU.subtract).then_inc(s_split, 1)
                    nc.gpsimd.tensor_tensor(fkb[:, :, :, 2 * HD:3 * HD], rk, fkb[:, :, :, 0:HD], ALU.subtract).then_inc(s_split, 1)
                    M = 3 * HD
                    for i in range(NT):
                        w = tokens(i)
                        pool.wait_ge(s_max, NT + i + 1)
                        link(nc.gpsimd.tensor_scalar(fqb[0:w, i, :, M], rmax[0:w, i, :], -1.0, None, ALU.mult))
                        nc.gpsimd.tensor_tensor(fqb[0:w, i, :, M + 1], rmax[0:w, i, :], fqb[0:w, i, :, M], ALU.add).then_inc(s_mrow, 1)
                    pool.wait_ge(s_ao, 2 * NT)
                    split(ao)
                    pool.wait_ge(s_norm, 4)
                    normalize(hn, x1, 3)
                    link(nc.gpsimd.tensor_tensor(hn[:, :, :], hn[:, :, :], par_b(FW2), ALU.mult))
                    split(hn)
                    link(nc.gpsimd.tensor_tensor(xl[:, :, :], h1[:, :, :], x1[:, :, :], ALU.add))
                    for i in range(NT):
                        w = tokens(i)
                        pool.wait_ge(s_gated, i + 1)
                        g = gated[0:w, i % 2, :]
                        for half in (4 * C, 2 * C, C):
                            link(nc.gpsimd.tensor_tensor(g[:, 0:half], g[:, 0:half], g[:, half:2 * half], ALU.add))
                        nc.gpsimd.tensor_tensor(res[0:w, i, :], g[:, 0:C], xl[0:w, i, :], ALU.add).then_inc(s_res, 1)

                @block.vector
                def _(dve):
                    steps = [0]

                    def link(ins):
                        steps[0] += 1
                        ins.then_inc(s_dve, 1)
                        dve.wait_ge(s_dve, steps[0])

                    def st(k):
                        return stat[:, k, :]

                    def center(src):
                        link(nc.vector.tensor_reduce(st(0), src[:, :, :], AX.X, ALU.add))
                        link(nc.vector.tensor_scalar(st(1), st(0), 1.0 / C, None, ALU.mult))
                        link(nc.vector.tensor_tensor(xc[:, :, :], src[:, :, :], per_token(st(1), C), ALU.subtract))
                        mean_square(xc)

                    def mean_square(src):
                        link(nc.vector.tensor_tensor(sq[:, :, :], src[:, :, :], src[:, :, :], ALU.mult))
                        link(nc.vector.tensor_reduce(st(0), sq[:, :, :], AX.X, ALU.add))
                        link(nc.vector.tensor_scalar(st(2), st(0), 1.0 / C, None, ALU.mult))

                    for g, (n0, n1, u0) in enumerate(((0, 7, 1), (7, 15, 0), (15, 16, 0))):
                        dve.wait_ge(s_tok, g + 1)
                        dve.wait_ge(s_early, min(g + 1, 2) if g else 1)
                        late = bank[g][C:P, :].rearrange("p (u v) -> p v u", v=V)[:, :, u0:u0 + n1 - n0]
                        nc.vector.tensor_tensor(h_feat[:, :, n0:n1], late, h_feat[:, :, n0:n1], ALU.add).then_inc(s_sum, 1)
                    dve.wait_ge(s_tokT, 1)
                    link(nc.vector.tensor_copy(h0[:, 0:FULL, :], bank[3][:, :].rearrange("p (i c) -> p i c", c=C)))
                    dve.wait_ge(s_txt, 16)
                    center(h0)
                    nc.vector.tensor_scalar(st(3), st(2), 1.0 + LN_EPS, LN_EPS * LN_EPS, ALU.mult, ALU.add).then_inc(s_norm, 1)
                    for k in range(5):
                        dve.wait_ge(s_proj, k + 1)
                        n, w = (2, P) if k < 4 else (1, REST)
                        nc.vector.tensor_tensor(qkv[0:w, 2 * k:2 * k + n, :],
                                                bank[2 + k][0:w, 0:192 * n].rearrange("p (i n) -> p i n", n=192),
                                                par_b(BQKV, 192, n, w), ALU.add).then_inc(s_raw, 1)

                    def take_stacks(n, a, bk, c):
                        dve.wait_ge(s_stkT, 4 * n - 2)
                        nc.vector.tensor_copy(bk[:, 0:FULL * P], bankb[2][0:bk.shape[0], :]).then_inc(s_stk, 1)
                        dve.wait_ge(s_stkT, 4 * n)
                        for k, dst in enumerate((a, bk, c)):
                            nc.vector.tensor_copy(dst[:, FULL * P:TOK], bankb[1][0:dst.shape[0], P * k:P * k + REST]).then_inc(s_stk, 1)

                    take_stacks(1, qt, kt1, kt2)

                    def a1_out(i):
                        w = tokens(i)
                        dve.wait_ge(s_avg, a1_k0[i] + len(A1_K))
                        link(nc.vector.reciprocal(rec[0:w, 0:1], bank[6][0:w, C:C + 1]))
                        nc.vector.tensor_scalar(ao[0:w, i, :], bank[6][0:w, 0:C], rec[0:w, 0:1], scale[0:w, 0:1],
                                                ALU.mult, ALU.mult).then_inc(s_ao, 1)

                    for i in range(NT + 2):
                        if i < NT:
                            w = tokens(i)
                            for n, (k0, k1) in enumerate(A1_S):
                                dve.wait_ge(s_sc, a1_s0[i] + n + 1)
                                nc.vector.tensor_reduce(pmax[0:w, 0, n:n + 1], bank[(a1_s0[i] + n) % 3][0:w, 0:k1 - k0],
                                                        AX.X, ALU.max).then_inc(s_red, 1)
                            dve.wait_ge(s_red, a1_s0[i] + len(A1_S))
                            nc.vector.tensor_reduce(rmax[0:w, i, 0:1], pmax[0:w, 0, 0:len(A1_S)], AX.X, ALU.max).then_inc(s_max, 1)
                            dve.wait_ge(s_max, i + 1)
                        if i >= 2:
                            a1_out(i - 2)

                    def from_project(dst, add, first):
                        dve.wait_ge(s_proj, first + 1)
                        nc.vector.tensor_tensor(dst[:, 0:FULL, :], bank[2][:, :].rearrange("p (i c) -> p i c", c=C),
                                                add[:, 0:FULL, :], ALU.add)
                        dve.wait_ge(s_proj, first + 2)
                        link(nc.vector.tensor_tensor(dst[0:REST, FULL, :], bank[3][0:REST, 0:C], add[0:REST, FULL, :], ALU.add))

                    from_project(x1, par_b(BPROJ), 5)
                    center(x1)
                    nc.vector.tensor_scalar(st(3), st(2), LN_EPS, None, ALU.add).then_inc(s_norm, 1)
                    dve.wait_ge(s_h1, 1)
                    center(h1)
                    link(nc.vector.tensor_scalar(st(3), st(2), LN_EPS, None, ALU.add))
                    link(nc.vector.reciprocal(st(5), st(3)))
                    link(nc.vector.tensor_tensor(st(5), st(2), st(5), ALU.mult))
                    nc.vector.tensor_scalar(st(5), st(5), RMS_EPS, None, ALU.add).then_inc(s_norm, 1)
                    dve.wait_ge(s_raw, 8)
                    cos = const[:, K_COS:K_COS + NT * HD].rearrange("p (t c) -> p t c", c=HD)
                    link(nc.vector.tensor_tensor(rope[:, 0, :, :].rearrange("p t (h c) -> p t h c", c=HD),
                                                 qkv[:, :, 0:96].rearrange("p t (h c) -> p t h c", c=HD),
                                                 cos.unsqueeze(2).to_broadcast([P, NT, 6, HD]), ALU.mult))
                    dve.wait_ge(s_rope, 1)
                    nc.vector.tensor_tensor(rope[:, 0, :, :], rope[:, 0, :, :], rope[:, 1, :, :], ALU.add).then_inc(s_rope, 1)
                    take_stacks(2, fq[:, 0, :], fq[:, 1, :], fk)

                    def a2_out(i):
                        w = tokens(i)
                        dve.wait_ge(s_avg, a2_k0[i][NH - 1] + len(a2_k(i)))
                        o = bank[6][0:w, 0:NH * (HD + 1)].rearrange("p (h c) -> p h c", c=HD + 1)
                        link(nc.vector.reciprocal(rec[0:w, :], o[:, :, HD]))
                        nc.vector.tensor_tensor(ao[0:w, i, :].rearrange("p (g r c) -> p r g c", g=2, r=2),
                                                o[:, :, 0:HD].rearrange("p (r g) c -> p r g c", r=2),
                                                rec[0:w, :].rearrange("p (r g) -> p r g", r=2).unsqueeze(3).to_broadcast([w, 2, 2, HD]),
                                                ALU.mult).then_inc(s_ao, 1)

                    for i in range(NT + 2):
                        if i < NT:
                            w, groups = tokens(i), a2_s(i)
                            for h in range(NH):
                                for n, (k0, k1) in enumerate(groups):
                                    g = a2_s0[i][h] + n
                                    dve.wait_ge(s_sc, g + 1)
                                    dst = rmax[0:w, i, h:h + 1] if len(groups) == 1 else pmax[0:w, h, n:n + 1]
                                    last = nc.vector.tensor_reduce(dst, bank[g % 3][0:w, 0:k1 - k0], AX.X, ALU.max).then_inc(s_red, 1)
                            dve.wait_ge(s_red, a2_s0[i][NH - 1] + len(groups))
                            if len(groups) > 1:
                                nc.vector.tensor_reduce(rmax[0:w, i, :], pmax[0:w, :, 0:len(groups)], AX.X, ALU.max).then_inc(s_max, 1)
                            else:
                                nc.vector.tensor_copy(rmax[0:w, i, :], rmax[0:w, i, :]).then_inc(s_max, 1)
                            dve.wait_ge(s_max, NT + i + 1)
                        if i >= 2:
                            a2_out(i - 2)

                    from_project(x1, xl, 5 + 2 + 3)
                    mean_square(x1)
                    nc.vector.tensor_scalar(st(3), st(2), RMS_EPS, None, ALU.add).then_inc(s_norm, 1)

                    dve.wait_ge(s_router, 1)
                    nc.vector.tensor_copy(gate_l[:, 0:FULL, :], bank[7][:, 0:FULL * NE].rearrange("p (i e) -> p i e", e=NE)).then_inc(s_logit, 1)
                    nc.vector.tensor_copy(gate_l[0:REST, FULL, :], bank[7][0:REST, FULL * NE:NT * NE]).then_inc(s_logit, 1)
                    dve.wait_ge(s_logit, 2)
                    link(nc.vector.tensor_reduce(gate_s[:, 0, :], gate_l[:, :, :], AX.X, ALU.max))
                    nc.vector.tensor_tensor(gate_l[:, :, :], gate_l[:, :, :], per_token(gate_s[:, 0, :], NE), ALU.subtract).then_inc(s_logit, 1)

                    def pick(m, sel):
                        desc = const[:, K_DESC:K_DESC + NE].unsqueeze(1).to_broadcast([P, NT, NE])
                        link(nc.vector.tensor_reduce(gate_s[:, m, :], gate_p[:, :, :], AX.X, ALU.max))
                        link(nc.vector.tensor_tensor(sel[:, :, :], gate_p[:, :, :], per_token(gate_s[:, m, :], NE), ALU.is_equal))
                        link(nc.vector.tensor_tensor(sel[:, :, :], sel[:, :, :], desc, ALU.mult))
                        link(nc.vector.tensor_reduce(gate_s[:, 3, :], sel[:, :, :], AX.X, ALU.max))
                        link(nc.vector.tensor_tensor(sel[:, :, :], sel[:, :, :], per_token(gate_s[:, 3, :], NE), ALU.is_equal))

                    def gates():
                        dve.wait_ge(s_gexp, 1)
                        link(nc.vector.tensor_reduce(gate_s[:, 0, :], gate_e[:, :, :], AX.X, ALU.add))
                        link(nc.vector.reciprocal(gate_s[:, 5, :], gate_s[:, 0, :]))
                        link(nc.vector.tensor_tensor(gate_e[:, :, :], gate_e[:, :, :], per_token(gate_s[:, 5, :], NE), ALU.mult))
                        link(nc.vector.tensor_copy(gate_p[:, :, :], gate_e[:, :, :]))
                        pick(1, gate_m)
                        link(nc.vector.scalar_tensor_tensor(gate_p[:, :, :], gate_m[:, :, :], -2.0, gate_p[:, :, :], ALU.mult, ALU.add))
                        pick(2, gate_w)
                        link(nc.vector.tensor_tensor(gate_m[:, :, :], gate_m[:, :, :], gate_w[:, :, :], ALU.add))
                        link(nc.vector.tensor_tensor(gate_m[:, :, :], gate_m[:, :, :], gate_e[:, :, :], ALU.mult))
                        link(nc.vector.tensor_tensor(gate_s[:, 4, :], gate_s[:, 1, :], gate_s[:, 2, :], ALU.add))
                        link(nc.vector.tensor_scalar(gate_s[:, 4, :], gate_s[:, 4, :], 1e-9, None, ALU.add))
                        link(nc.vector.reciprocal(gate_s[:, 5, :], gate_s[:, 4, :]))
                        link(nc.vector.tensor_tensor(gate_w[:, :, :], gate_m[:, :, :], per_token(gate_s[:, 5, :], NE), ALU.mult))

                    def gate_tile(i):
                        w = tokens(i)
                        dve.wait_ge(s_w2, i + 1)
                        if i >= 2:
                            dve.wait_ge(s_res, i - 1)
                        nc.vector.tensor_tensor(gated[0:w, i % 2, :].rearrange("p (e c) -> p e c", c=C),
                                                bank[6 + i % 2][0:w, :].rearrange("p (e c) -> p e c", c=C),
                                                per_token(gate_w[0:w, i, :], C), ALU.mult).then_inc(s_gated, 1)

                    for t in range(CHUNK_TILES):
                        a, z = chunk_cols(t)
                        for c in range(NC):
                            n, r = t * NC + c, rows_of(c)
                            dve.wait_ge(s_silu, n + 1)
                            nc.vector.tensor_tensor(hid[0:r, c, a:z], bank[2 * (n % 3) + 1][0:r, 0:z - a],
                                                    silu[0:r, n % 4, 0:z - a], ALU.mult).then_inc(s_u, 1)
                            if t >= 1 and c in W2_AFTER:
                                gate_tile(CHUNK_TILES * (t - 1) + W2_AFTER[c])
                        if t == 0:
                            gates()
                    for k in range(CHUNK_TILES):
                        gate_tile(CHUNK_TILES * (CHUNK_TILES - 1) + k)

            nums = [s.num for s in sems]
            nc.gpsimd.sem_clear(range(min(nums), max(nums) + 1))
            nc.all_engine_barrier()


def constants():
    import numpy as np
    k = np.arange(P)
    c = np.zeros((P, NCONST), np.float32)
    c[:, K_ID:K_ID + P] = np.eye(P)
    c[:, K_FLIP:K_FLIP + P] = np.eye(P)[::-1]
    c[:, K_MS:K_MS + P] = np.where(k[None, :] > k[:, None], -1e30, 0)
    c[:, K_MT:K_MT + P] = np.where(k[:, None] > k[None, :], -1e30, 0)
    inv = 1.0 / 10000.0 ** (np.arange(0, HD, 2, dtype=np.float32) / HD)
    fr = np.outer(np.arange(NT * P, dtype=np.float32), inv)
    emb = np.concatenate([fr, fr], axis=-1)
    sign = np.concatenate([-np.ones(HD // 2), np.ones(HD // 2)])
    for off, t in ((K_COS, np.cos(emb)), (K_SIN, np.sin(emb) * sign)):
        c[:, off:off + NT * HD] = t.reshape(NT, P, HD).transpose(1, 0, 2).reshape(P, NT * HD)
    c[:, K_DESC:K_DESC + NE] = np.arange(NE, 0, -1)
    c[:, K_HALF] = -0.5
    f, p = np.arange(NFREQ)[:, None], np.arange(PATCH)[None, :]
    ang = 2 * np.pi * f * p / PATCH
    dft = np.concatenate([np.cos(ang), -np.sin(ang)]) / np.sqrt(PATCH)
    return c, dft.astype(np.float32)


_INS = {
    'x': ('x', None), 'txt': ('txt', None), 'tok_w': ('L0_tok_W', None),
    'ln1_g': ('L0_attn_ln1_g', (1, -1)), 'ln1_b': ('L0_attn_ln1_b', (1, -1)), 'qkv_w': ('L0_attn_qkv_w', None),
    'qkv_b': ('L0_attn_qkv_b', (1, -1)), 'bias_table': ('L0_attn_bias_table', (1, -1)),
    'attn_scale': ('L0_attn_scale', (1, 1)), 'proj_w': ('L0_attn_proj_w', None), 'proj_b': ('L0_attn_proj_b', (1, -1)),
    'ln2_g': ('L0_attn_ln2_g', (1, -1)), 'ln2_b': ('L0_attn_ln2_b', (1, -1)), 'f_ln1': ('L0_ffn_ln1_w', (1, -1)),
    'f_ln2': ('L0_ffn_ln2_w', (1, -1)), 'wq': ('L0_ffn_wq', None), 'wk': ('L0_ffn_wk', None), 'wv': ('L0_ffn_wv', None),
    'wo': ('L0_ffn_wo', None), 'router_w': ('L0_ffn_router_w', None), 'w1': ('L0_ffn_w1', None),
    'w2': ('L0_ffn_w2', None), 'w3': ('L0_ffn_w3', None),
}


def kernel(**inputs):
    import numpy as np
    import concourse.bacc as bacc
    from concourse.bass_utils import run_bass_kernel_spmd as run

    nc = bacc.Bacc("TRN2", target_bir_lowering=False, num_devices=1)
    arrays, aps = {}, {}

    def give(name, a):
        arrays[f"in_{name}"] = a
        aps[name] = nc.dram_tensor(f"in_{name}", a.shape, mybir.dt.from_np(a.dtype), kind="ExternalInput").ap()

    for name, (key, shape) in _INS.items():
        a = np.ascontiguousarray(inputs[key])
        give(name, a if shape is None else a.reshape(shape))
    const, dft = constants()
    give("const", const)
    give("dft", dft)
    out = nc.dram_tensor("out_dram", (B, TOK, C), F32, kind="ExternalOutput").ap()
    program(nc, aps, out)
    r = run(nc, [arrays], core_ids=[0])
    return r.results[0]["out_dram"]
```

```python
from contextlib import ExitStack

import concourse.bass as bass
from concourse import mybir

F32 = mybir.dt.float32
BF16 = mybir.dt.bfloat16
ALU = mybir.AluOpType
ACT = mybir.ActivationFunctionType
AX = mybir.AxisListType

B, C, TIME, V = 4, 64, 128, 64
TXT = 32
PATCH, STRIDE = 16, 8
NPATCH = TIME // STRIDE
NFREQ = PATCH // 2 + 1
TOK = V * NPATCH + TXT
P = 128
NT = (TOK + P - 1) // P
FULL = TOK // P
REST = TOK - FULL * P
SPAN = 1023
LN_EPS, RMS_EPS = 1e-5, 1e-6
NH, NKV, HD = 4, 2, 16
NE, HID = 8, 170
ROWS = NE * HID
NC = (ROWS + P - 1) // P
FS = 64
HALF = 4
G1, B1, BQKV, BPROJ, G2, B2, FW1, FW2 = 0, 64, 128, 320, 384, 448, 512, 576
NPAR = 640
K_ID, K_FLIP, K_MS, K_MT, K_COS, K_SIN, K_DESC, K_HALF = 0, 128, 256, 384, 512, 656, 800, 808
NCONST = 809
W_QKV2, W_WO, W_ROUTER, W_ONE, W_THREE = 0, 1, 2, 3, 3 + NC
NWT = 3 + 2 * NC
BIAS_PAD = 96
BIAS_W = NT * P
BIAS_LEN = BIAS_W + P - 1
PT_RING = 12
CUT = 5
PARTS = (range(0, CUT), range(CUT, NT))
CHUNK_TILES = 3
CW = CHUNK_TILES * P


def tokens(i):
    return P if i < FULL else REST


def rows_of(c):
    return min(P, ROWS - c * P)


def w2_blocks():
    out, blk = [], 0
    for c in range(NC):
        e0, e1 = c * P // HID, (c * P + rows_of(c) - 1) // HID
        out.append((c, e0, e1 - e0 + 1, blk))
        blk += e1 - e0 + 1
    return out, blk


W2B, NBLK = w2_blocks()

A1_S = [(0, 384), (384, 768), (768, TOK)]
A1_K = [range(0, 4), range(4, 8), range(8, 9)]


def a2_s(i):
    n = min(TOK, (i + 1) * P)
    parts = (n + 511) // 512
    return [(n * g // parts, n * (g + 1) // parts) for g in range(parts)]


def a2_k(i):
    return [range(a, min(a + 4, i + 1)) for a in range(0, i + 1, 4)]


def weave(main, side, every=1, first=0):
    out, side = [], list(side)
    for n, steps in enumerate(main):
        out += steps
        if n >= first and (n - first) % every == every - 1 and side:
            out += side.pop(0)
    for steps in side:
        out += steps
    return out


X_TOKENS = [[("tok", g) for g in range(3)], [("tokT", 0)], [("ln1a", 0)], [("ln1b", 0)], [("turn1", 0)],
            [("qkv1", k) for k in range(3)], [("qkv1", 3), ("qkv1", 4)], [("split1", 0)],
            [("stack1", k) for k in range(3)], [("stack1", k) for k in range(3, 6)]]
Y_HEADS = [[("ystart", 0)], [("turn3", 0)], [("qkv2", k) for k in range(3)], [("rope", 0)], [("split2", 0)],
           [("stack2", k) for k in range(6)]]


def a1_steps(k):
    out = []
    for kind, lag in (("S1", 0), ("T1", 1), ("V1", 2), ("E1", 1), ("O1", 2)):
        if 0 <= k - lag < NT:
            out.append((kind, k - lag))
    return out


def a2_steps(k):
    out = []
    for kind, lag, h in (("S2", 0, 0), ("V2", 2, 0), ("S2", 0, 1), ("T2", 1, 0), ("S2", 0, 2), ("E2", 1, 0), ("X2", 2, 0),
                         ("E2", 1, 1), ("S2", 0, 3), ("E2", 1, 2), ("O2", 2, 0), ("E2", 1, 3)):
        if 0 <= k - lag < NT:
            out.append((kind, k - lag, h))
    return out


A1 = [a1_steps(k) for k in range(NT + 2)]
A2 = [a2_steps(k) for k in range(NT + 2)]
X_END = [[("aosplit1", 0)], [("turn2", 0)], [("proj", 0), ("proj", 1)], [("ln2a", 0)], [("ln2b", 0)], [("ln3a", 0)], [("ln3b", 0)]]
Y_MID = [[("aosplit2", 0)], [("turn4", 0)], [("wo", 0), ("wo", 1)], [("rms", 0)], [("turn5", 0)], [("router", 0)]]
MOE = [[("up", t, c)] for t in range(3) for c in range(NC)]
MOE_END = [[("down", m)] for m in range(3 * NC)]

ORDER_X = sum(X_TOKENS + A1 + X_END, [])
ORDER_XY = (weave(Y_HEADS, X_TOKENS[:4]) + weave(A2, X_TOKENS[4:]) + weave(A1, Y_MID)
            + weave(MOE, X_END, every=4, first=1) + sum(MOE_END, []))
ORDER_Y = sum(Y_HEADS + A2 + Y_MID + MOE + MOE_END, [])


class Plan:

    JOBS = {"tok", "tokT", "qkv1", "proj", "qkv2", "wo", "router", "stack1", "stack2"}
    TURNS = {"turn1", "turn2", "turn3", "turn4", "turn5"}

    def __init__(self, order):
        self.order, self.names = order, {s[0] for s in order}
        self.score, self.exp, self.unit, self.job = {}, {}, {}, {}
        ns = nk = 0
        for s in order:
            kind, i = s[0], s[1]
            if kind in ("S1", "S2"):
                self.score[s] = ns
                ns += len(A1_S if kind == "S1" else a2_s(i))
                self.unit.setdefault((kind[1], i), len(self.unit))
            if kind in ("E1", "E2"):
                self.exp[s] = nk
                nk += len(A1_K if kind == "E1" else a2_k(i))
            if kind in self.JOBS:
                self.job[kind, i] = len(self.job)
            if kind in self.TURNS:
                for p in range(2):
                    self.job[kind, p] = len(self.job)
        self.scores, self.exps, self.units = ns, nk, len(self.unit)


def program(nc, A, out):
    ctx = ExitStack()
    with ctx:
        def sb(name, shape, dt=F32):
            return ctx.enter_context(nc.sbuf_tensor(name, shape, dt))

        sems = []

        def sem(name):
            s = ctx.enter_context(nc.semaphore(name))
            sems.append(s)
            return s

        bank = [ctx.enter_context(nc.psum_tensor(f"bank{i}", [P, 512], F32)) for i in range(8)]
        bankb = [b[:, :].bitcast(BF16) for b in bank]

        const = sb("const", [P, NCONST])
        ident = const[:, K_ID:K_ID + P]
        identb = sb("identb", [P, P], BF16)
        flipb = sb("flipb", [P, P], BF16)
        mask_s = sb("mask_s", [P, P], BF16)
        mask_t = sb("mask_t", [P, P], BF16)
        par = sb("par", [P, NPAR])
        scale = sb("scale", [P, 1])
        dft = sb("dft", [2 * NFREQ, PATCH])
        w_tok = sb("w_tok", [P, HALF, 2, C])
        wa_hi, wa_lo = sb("wa_hi", [P, 256], BF16), sb("wa_lo", [P, 256], BF16)
        wt_hi, wt_lo = sb("wt_hi", [P, NWT * P], BF16), sb("wt_lo", [P, NWT * P], BF16)
        w2s = sb("w2s", [P, NBLK * C])
        rel_hi, rel_lo = sb("rel_hi", [P, BIAS_W], BF16), sb("rel_lo", [P, BIAS_W], BF16)

        xs = sb("xs", [P, NPATCH, HALF, V])
        xpad = sb("xpad", [P, V])
        h0, xc, sq, hn, xt = (sb(n, [P, NT, C]) for n in ("h0", "xc", "sq", "hn", "xt"))
        h1_next, xl_next = sb("h1_next", [P, NT, C]), sb("xl_next", [P, NT, C])
        stat_x = sb("stat_x", [P, 8, NT])
        hl_x, ht_x = sb("hl_x", [P, NT, P], BF16), sb("ht_x", [P, TOK], BF16)
        qkv = sb("qkv", [P, NT, 192])
        h_feat = qkv[0:C, :, :].rearrange("p t c -> p (t c)")[:, 0:V * NPATCH].rearrange("p (v n) -> p v n", n=NPATCH)
        ql = sb("ql", [P, NT, P], BF16)
        qb = sb("qb", [P, NT, C + 2], BF16)
        ka = sb("ka", [P, NT, P], BF16)
        kb = sb("kb", [P, NT, C + 2], BF16)
        qt, qm = sb("qt", [P, TOK], BF16), sb("qm", [C + 2, TOK], BF16)
        kt1, kt2 = sb("kt1", [P, TOK], BF16), sb("kt2", [C + 2, TOK], BF16)
        v1 = sb("v1", [P, NT, C + 1])
        ao_x = sb("ao_x", [P, NT, C])

        h1, xl, x1, hn_y, ao_y, res = (sb(n, [P, NT, C]) for n in ("h1", "xl", "x1", "hn_y", "ao_y", "res"))
        stat_y = sb("stat_y", [P, 8, NT])
        hl_y, ht_y = sb("hl_y", [P, NT, P], BF16), sb("ht_y", [P, TOK], BF16)
        qkv_y = sb("qkv_y", [P, NT, P])
        rope = sb("rope", [P, 2, NT, 96])
        fqb = sb("fqb", [P, NT, 4, FS], BF16)
        fkb = sb("fkb", [P, NT, 2, FS], BF16)
        fq, fqm = sb("fq", [P, 2, TOK], BF16), sb("fqm", [P, 2, TOK], BF16)
        fk = sb("fk", [P, 2, TOK], BF16)
        vf = sb("vf", [P, NT, NKV, 32])
        ot = sb("ot", [P, P])
        gate_l, gate_p, gate_e, gate_m, gate_w = (sb(n, [P, NT, NE]) for n in ("gate_l", "gate_p", "gate_e", "gate_m", "gate_w"))
        gate_s = sb("gate_s", [P, 6, NT])
        silu = rope[:, :, :, :].rearrange("p a t c -> p (a t c)")[:, 0:3 * CW].rearrange("p (s n) -> p s n", s=3)
        gated = fq[:, :, :].rearrange("p a n -> p (a n)").bitcast(F32)[:, 0:2 * NE * C].rearrange("p (s n) -> p s n", s=2)
        hid = sb("hid", [P, 2, NC, CW])

        pmax = sb("pmax", [P, 4, 4])
        rmax = sb("rmax", [P, NT, 4])
        rec = sb("rec", [P, 4])
        pt = sb("pt", [P, PT_RING, 512])

        hidf = hid[:, :, :, :].rearrange("p s a b -> p (s a b)")
        w_raw = hidf[0:2 * NFREQ, 0:C * C].rearrange("p (o c) -> p o c", o=C)
        nat = hidf[:, C * C:C * C + NWT * P].rearrange("p (k c) -> p k c", k=NWT)
        ptf = pt[:, :, :].rearrange("p a b -> p (a b)")
        c2 = ptf[0:C, 0:ROWS]
        c2b = ptf[0:C, ROWS:ROWS + NBLK * P].rearrange("p (k c) -> p k c", k=NBLK)
        used = ROWS + NBLK * P
        rel = ptf[:, used:used + BIAS_W]
        w_a = ptf[:, used + BIAS_W:used + BIAS_W + 256]
        ext = nc.dram_tensor("bias_ext", (1, BIAS_LEN), F32, kind="Internal").ap()

        def par_b(off, n=C, tiles=NT, np_=P):
            return par[0:np_, off:off + n].unsqueeze(1).to_broadcast([np_, tiles, n])

        def per_token(ap, n):
            return ap.unsqueeze(2).to_broadcast([ap.shape[0], ap.shape[1], n])

        def load_x(sp, b, s):
            v = A["x"][b].rearrange("c (u j q) v -> j c u (q v)", j=2, q=HALF)
            for j in range(2):
                sp.dma_start(xs[64 * j:64 * j + 64, :, :, :].rearrange("p u q v -> p u (q v)"),
                             v[j]).then_inc(s, 16)
                sp.dma_start(xpad[64 * j:64 * j + 64, :], A["x"][b][:, TIME - 1, :]).then_inc(s, 16)

        s_const, s_w, s_nat, s_c2, s_ext, s_x = (sem(n) for n in (
            "s_const", "s_w", "s_nat", "s_c2", "s_ext", "s_x"))
        s_rel, s_cast, s_zero, s_c2b = sem("s_rel"), sem("s_cast"), sem("s_zero"), sem("s_c2b")
        s_tokw, s_tokc, s_trn, s_hi, s_lo, s_wa = (sem(n) for n in (
            "s_tokw", "s_tokc", "s_trn", "s_hi", "s_lo", "s_wa"))
        wt_banks = [range(a, min(a + 4, NWT)) for a in range(0, NWT, 4)]
        w2_banks = [range(a, min(a + 8, NBLK)) for a in range(0, NBLK, 8)]

        def nat_rows(k):
            return {W_QKV2: P, W_WO: C, W_ROUTER: NE}.get(k) or rows_of((k - W_ONE) % NC)

        with nc.Block() as block:
            @block.sync
            def _(sp):
                tab = A["bias_table"]
                sp.dma_start(ext[:, 0:BIAS_PAD], tab[:, 0:BIAS_PAD]).then_inc(s_ext, 16)
                sp.dma_start(ext[:, BIAS_PAD:BIAS_PAD + SPAN], tab).then_inc(s_ext, 16)
                tail = BIAS_LEN - BIAS_PAD - SPAN
                sp.dma_start(ext[:, BIAS_PAD + SPAN:].unsqueeze(2),
                             tab[:, SPAN - 1:SPAN].unsqueeze(1).to_broadcast([1, tail, 1])).then_inc(s_ext, 16)
                sp.dma_start(const[:, :], A["const"]).then_inc(s_const, 16)
                sp.dma_start(dft[:, :], A["dft"]).then_inc(s_w, 16)
                sp.dma_start(scale[:, :], A["attn_scale"].to_broadcast([P, 1])).then_inc(s_w, 16)
                wv = A["tok_w"].rearrange("o (f c) -> f o c", c=C)
                sp.dma_start(w_raw[:, :, :], wv).then_inc(s_w, 16)
                for off, name, n in ((G1, "ln1_g", C), (B1, "ln1_b", C), (BQKV, "qkv_b", 192), (BPROJ, "proj_b", C),
                                     (G2, "ln2_g", C), (B2, "ln2_b", C), (FW1, "f_ln1", C), (FW2, "f_ln2", C)):
                    sp.dma_start(par[:, off:off + n], A[name].to_broadcast([P, n])).then_inc(s_w, 16)
                load_x(sp, 0, s_x)
                sp.wait_ge(s_ext, 48)
                sp.dma_start(rel[:, :], bass.AP(ext.tensor, 0, [[1, P], [1, BIAS_W]])).then_inc(s_rel, 16)
                sp.wait_ge(s_x, 64)

            @block.scalar
            def _(act):
                for d in range(2):
                    act.dma_start(w_a[64 * d:64 * d + 64, 0:192], A["qkv_w"]).then_inc(s_wa, 16)
                    act.dma_start(w_a[64 * d:64 * d + 64, 192:256], A["proj_w"]).then_inc(s_wa, 16)
                act.dma_start(c2[:, :].rearrange("c (e h) -> c e h", e=NE), A["w2"].rearrange("e c h -> c e h")).then_inc(s_c2, 16)
                for d in range(2):
                    cols = slice(64 * d, 64 * d + 64)
                    for h in range(NH):
                        slot = (h % 2) * 2 + h // 2
                        act.dma_start(nat[HD * slot:HD * slot + HD, W_QKV2, cols], A["wq"][HD * h:HD * h + HD, :]).then_inc(s_nat, 16)
                    act.dma_start(nat[64:96, W_QKV2, cols], A["wk"]).then_inc(s_nat, 16)
                    act.dma_start(nat[96:128, W_QKV2, cols], A["wv"]).then_inc(s_nat, 16)
                    act.dma_start(nat[0:C, W_WO, cols], A["wo"]).then_inc(s_nat, 16)
                    act.dma_start(nat[0:NE, W_ROUTER, cols], A["router_w"]).then_inc(s_nat, 16)
                    for first, name in ((W_ONE, "w1"), (W_THREE, "w3")):
                        w = A[name].rearrange("e h c -> (e h) c")
                        act.dma_start(nat[:, first:first + NC - 1, cols],
                                      w[0:(NC - 1) * P, :].rearrange("(k p) c -> p k c", p=P)).then_inc(s_nat, 16)
                        act.dma_start(nat[0:rows_of(NC - 1), first + NC - 1, cols],
                                      w[(NC - 1) * P:, :]).then_inc(s_nat, 16)
                for n, ks in enumerate(wt_banks):
                    act.wait_ge(s_trn, n + 1)
                    for k in ks:
                        r = nat_rows(k)
                        last = nc.scalar.copy(wt_hi[:, k * P:k * P + r], bank[n % 4][:, (k % 4) * P:(k % 4) * P + r])
                    last.then_inc(s_hi, 1)

            @block.gpsimd
            def _(pool):
                for t in (h0, xt, x1, ao_x, ao_y, qkv, qkv_y, gate_l, qb):
                    nc.gpsimd.memset(t[:, FULL, :], 0.0)
                nc.gpsimd.memset(fk[:, :, :], 0.0)
                nc.gpsimd.memset(fqb[:, :, :, :], 0.0)
                for t, at in ((kb, C), (fkb, 3 * HD)):
                    v = t[:, :, :] if t is kb else t[:, :, :, :].rearrange("p t g c -> p (t g) c")
                    nc.gpsimd.memset(v, 0.0).then_inc(s_zero, 1)
                pool.wait_ge(s_zero, 2)
                for t, at in ((kb, C), (fkb, 3 * HD)):
                    v = t[:, :, :] if t is kb else t[:, :, :, :].rearrange("p t g c -> p (t g) c")
                    nc.gpsimd.memset(v[:, :, at:at + 1], 1.0)
                    nc.gpsimd.memset(v[:, :, at + 1:at + 2], -1.0)
                nc.gpsimd.memset(v1[:, :, C:C + 1], 1.0)
                nc.gpsimd.memset(vf[:, :, :, HD:HD + 1], 1.0)
                nc.gpsimd.memset(vf[:, :, :, HD + 1:32], 0.0)
                nc.gpsimd.memset(c2b[:, :, :], 0.0).then_inc(s_zero, 1)
                pool.wait_ge(s_zero, 3)
                pool.wait_ge(s_c2, 16)
                for c, e0, ne, blk in W2B:
                    for e in range(e0, e0 + ne):
                        a, z = max(c * P, e * HID), min(c * P + rows_of(c), (e + 1) * HID)
                        last = nc.gpsimd.tensor_copy(c2b[:, blk + e - e0, a - c * P:z - c * P], c2[:, a:z])
                last.then_inc(s_c2b, 1)

            @block.tensor
            def _(pe):
                pe.wait_ge(s_w, 16 * 11)
                for o in range(C):
                    for j in range(2):
                        last = nc.tensor.matmul(bank[4 + o // 32][64 * j:64 * j + 64, (o % 32) * PATCH:(o % 32 + 1) * PATCH],
                                                w_raw[:, o, :], dft[:, :], start=True, stop=True)
                    if o % 32 == 31:
                        last.then_inc(s_tokw, 1)
                pe.wait_ge(s_const, 16)
                pe.wait_ge(s_nat, 16 * 24)
                for n, ks in enumerate(wt_banks):
                    if n >= 4:
                        pe.wait_ge(s_lo, n - 3)
                    for k in ks:
                        r = nat_rows(k)
                        last = nc.tensor.transpose(bank[n % 4][:, (k % 4) * P:(k % 4) * P + r], nat[0:r, k, :], ident[0:r, 0:r])
                    last.then_inc(s_trn, 1)
                pe.wait_ge(s_c2b, 1)
                pe.wait_ge(s_tokc, 4)
                for n, ks in enumerate(w2_banks):
                    for k in ks:
                        last = nc.tensor.transpose(bank[4 + n][:, (k % 8) * C:(k % 8 + 1) * C], c2b[:, k, :], ident[0:C, 0:C])
                    last.then_inc(s_trn, 1)

            @block.vector
            def _(dve):
                dve.wait_ge(s_const, 16)
                for dst, off in ((identb, K_ID), (flipb, K_FLIP), (mask_s, K_MS), (mask_t, K_MT)):
                    nc.vector.tensor_copy(dst[:, :], const[:, off:off + P])
                for n in range(2):
                    dve.wait_ge(s_tokw, n + 1)
                    src = bank[4 + n][:, :].rearrange("p (o l j q) -> p j q l o", l=2, j=2, q=HALF)
                    for j in range(2):
                        for late in range(2):
                            last = nc.vector.tensor_copy(w_tok[64 * j:64 * j + 64, :, late, 32 * n:32 * n + 32],
                                                         src[64 * j:64 * j + 64, j, :, late, :])
                        last.then_inc(s_tokc, 1)
                dve.wait_ge(s_wa, 64)
                nc.vector.tensor_copy(wa_hi[:, :], w_a[:, :]).then_inc(s_cast, 1)
                dve.wait_ge(s_cast, 1)
                nc.vector.tensor_tensor(wa_lo[:, :], w_a[:, :], wa_hi[:, :], ALU.subtract)
                dve.wait_ge(s_rel, 16)
                nc.vector.tensor_scalar(rel[:, 0:BIAS_W - 1], rel[:, 0:BIAS_W - 1], rel[:, BIAS_W - 1:BIAS_W], None,
                                        ALU.subtract).then_inc(s_cast, 1)
                dve.wait_ge(s_cast, 2)
                nc.vector.memset(rel[:, BIAS_W - 1:BIAS_W], 0.0).then_inc(s_cast, 1)
                dve.wait_ge(s_cast, 3)
                nc.vector.tensor_copy(rel_hi[:, :], rel[:, :]).then_inc(s_cast, 1)
                dve.wait_ge(s_cast, 4)
                nc.vector.tensor_tensor(rel_lo[:, :], rel[:, :], rel_hi[:, :], ALU.subtract)
                for n, ks in enumerate(wt_banks):
                    dve.wait_ge(s_hi, n + 1)
                    for k in ks:
                        r = nat_rows(k)
                        last = nc.vector.tensor_tensor(wt_lo[:, k * P:k * P + r], bank[n % 4][:, (k % 4) * P:(k % 4) * P + r],
                                                       wt_hi[:, k * P:k * P + r], ALU.subtract)
                    last.then_inc(s_lo, 1)
                for n, ks in enumerate(w2_banks):
                    dve.wait_ge(s_trn, len(wt_banks) + n + 1)
                    w = len(ks) * C
                    nc.vector.tensor_copy(w2s[:, ks[0] * C:ks[0] * C + w], bank[4 + n][:, 0:w])

        s_txt, s_xload, s_out = sem("s_txt"), sem("s_xload"), sem("s_out")
        s_dve, s_pool = sem("s_dve"), sem("s_pool")
        s_job = sem("s_job")
        s_taken = [sem("s_taken0"), sem("s_taken1")]
        s_early = sem("s_early")
        s_norm_x, s_gain_x, s_hi_x, s_hl_x, s_h1 = (sem(n) for n in ("s_norm_x", "s_gain_x", "s_hi_x", "s_hl_x", "s_h1"))
        s_norm_y, s_gain_y, s_hi_y, s_hl_y = (sem(n) for n in ("s_norm_y", "s_gain_y", "s_hi_y", "s_hl_y"))
        s_qk_hi, s_qk_lo, s_fqk_hi, s_fqk_lo = (sem(n) for n in ("s_qk_hi", "s_qk_lo", "s_fqk_hi", "s_fqk_lo"))
        s_rot, s_rope, s_copy = sem("s_rot"), sem("s_rope"), sem("s_copy")
        s_sc, s_red, s_max, s_mrow, s_mT, s_m, s_st, s_exp, s_used, s_av, s_ot, s_oT, s_ao = (sem(n) for n in (
            "s_sc", "s_red", "s_max", "s_mrow", "s_mT", "s_m", "s_st", "s_exp", "s_used", "s_av", "s_ot", "s_oT", "s_ao"))
        s_logit, s_gexp, s_ab, s_silu, s_u, s_w2, s_gated, s_res = (sem(n) for n in (
            "s_logit", "s_gexp", "s_ab", "s_silu", "s_u", "s_w2", "s_gated", "s_res"))

        def chunk_cols(t):
            return t * CW, min((t + 1) * CW, TOK)

        def run_pass(plan, bx, by, b_load):
            has_x, has_y = "tok" in plan.names, "up" in plan.names

            def taken(eng, name, k):
                n = plan.job[name, k]
                eng.wait_ge(s_taken[n % 2], n // 2 + 1)

            def job_bank(name, k):
                return 6 + plan.job[name, k] % 2

            with nc.Block() as block:
                @block.sync
                def _(sp):
                    if has_x:
                        sp.dma_start(h0[0:TXT, FULL, :], A["txt"][bx]).then_inc(s_txt, 16)
                        sp.wait_ge(s_job, plan.job["tok", 2] + 1)
                        load_x(sp, b_load, s_xload)
                    if has_y:
                        sp.wait_ge(s_res, NT)
                        sp.dma_start(out[by][0:FULL * P, :].rearrange("(i p) c -> p i c", p=P), res[:, 0:FULL, :]).then_inc(s_out, 16)
                        sp.dma_start(out[by][FULL * P:, :], res[0:REST, FULL, :]).then_inc(s_out, 16)
                        sp.wait_ge(s_out, 32)
                    if has_x:
                        sp.wait_ge(s_xload, 64)

                @block.tensor
                def _(pe):
                    def job(name, k):
                        n = plan.job[name, k]
                        if n >= 2:
                            pe.wait_ge(s_taken[n % 2], n // 2)
                        return bank[6 + n % 2], bankb[6 + n % 2]

                    def tok(g):
                        o, _ = job("tok", g)
                        for q in range(HALF):
                            dst = o[:, :].rearrange("p (u v) -> p u v", v=V) if g < 2 else o[:, 0:V]
                            src = xs[:, 8 * g:8 * g + 8, q, :] if g < 2 else xpad[:, :]
                            last = nc.tensor.matmul(dst, w_tok[:, q, :, :].rearrange("p l o -> p (l o)"), src,
                                                    start=(q == 0), stop=(q == HALF - 1))
                        last.then_inc(s_job, 1)

                    def tokT(_):
                        for g in range(3):
                            taken(pe, "tok", g)
                        o, _ = job("tokT", 0)
                        hf = h_feat[:, :, :].rearrange("c v n -> c (v n)")
                        for i in range(FULL):
                            last = nc.tensor.transpose(o[:, C * i:C * i + C], hf[:, P * i:P * i + P], ident[0:C, 0:C])
                        last.then_inc(s_job, 1)

                    def turn(name, hl, s_hl, n):
                        pe.wait_ge(s_hl, n)
                        for part, tiles in enumerate(PARTS):
                            _, o = job(name, part)
                            for k, i in enumerate(tiles):
                                w = tokens(i)
                                last = nc.tensor.transpose(o[:, P * k:P * k + w], hl[0:w, i, :], identb[0:w, 0:w])
                            last.then_inc(s_job, 1)

                    def project(name, k, tiles, turned, ht, w_hi, w_lo, cols):
                        for part in range(2):
                            taken(pe, turned, part)
                        o, _ = job(name, k)
                        for n, i in enumerate(tiles):
                            w = tokens(i)
                            dst = o[0:w, n * cols:(n + 1) * cols]
                            nc.tensor.matmul(dst, ht[:, P * i:P * i + w], w_hi, start=True, stop=False)
                            last = nc.tensor.matmul(dst, ht[:, P * i:P * i + w], w_lo, start=False, stop=True)
                        last.then_inc(s_job, 1)

                    def stack(name, k, src, rows):
                        _, o = job(name, k)
                        for n, i in enumerate(PARTS[k % 2]):
                            w = tokens(i)
                            last = nc.tensor.transpose(o[0:rows, P * n:P * n + w], src(i)[0:w], identb[0:w, 0:w])
                        last.then_inc(s_job, 1)

                    def stack1(k):
                        pe.wait_ge(s_qk_hi, 2)
                        pe.wait_ge(s_qk_lo, 1)
                        src, rows = ((ql, P), (ka, P), (kb, C + 2))[k // 2]
                        stack("stack1", k, lambda i: src[:, i, :], rows)

                    def stack2(k):
                        pe.wait_ge(s_fqk_hi, 2)
                        pe.wait_ge(s_fqk_lo, 1)
                        src = (fqb[:, :, 0:2, :], fqb[:, :, 2:4, :], fkb[:, :, :, :])[k // 2]
                        stack("stack2", k, lambda i: src[:, i, :, :].rearrange("p h c -> p (h c)"), P)

                    def score_bank(g):
                        if g >= 2:
                            pe.wait_ge(s_red, g - 1)
                        return bank[g % 2]

                    def exp_bank(g):
                        if g >= 2:
                            pe.wait_ge(s_exp, g - 1)
                        return bank[2 + g % 2]

                    def S1(i):
                        if i == 0:
                            for k in range(6):
                                taken(pe, "stack1", k)
                        w, q0 = tokens(i), P * i
                        for n, (k0, k1) in enumerate(A1_S):
                            dst = score_bank(plan.score["S1", i] + n)
                            bend = min(k1, q0 + w)
                            nc.tensor.matmul(dst[0:w, 0:k1 - k0], qt[:, q0:q0 + w], kt1[:, k0:k1], start=True, stop=False)
                            last = nc.tensor.matmul(dst[0:w, 0:k1 - k0], qt[0:C, q0:q0 + w], kt2[0:C, k0:k1],
                                                    start=False, stop=(bend <= k0))
                            if bend > k0:
                                y = BIAS_W - P - q0 + k0
                                for r in (rel_hi, rel_lo):
                                    last = nc.tensor.matmul(dst[0:w, 0:bend - k0], flipb[:, 0:w], r[:, y:y + bend - k0],
                                                            start=False, stop=(r is rel_lo))
                            last.then_inc(s_sc, 1)

                    def max_bank(u):
                        pe.wait_ge(s_mrow, u + 1)
                        if u >= 1:
                            pe.wait_ge(s_m, u)
                        return bankb[5]

                    def T1(i):
                        o, w = max_bank(plan.unit["1", i]), tokens(i)
                        nc.tensor.transpose(o[0:C + 2, 0:w], qb[0:w, i, :], identb[0:w, 0:w]).then_inc(s_mT, 1)

                    def E1(i):
                        pe.wait_ge(s_m, plan.unit["1", i] + 1)
                        w, q0 = tokens(i), P * i
                        for n, keys in enumerate(A1_K):
                            dst = exp_bank(plan.exp["E1", i] + n)
                            for jj, j in enumerate(keys):
                                kw, o = tokens(j), dst[0:tokens(j), P * jj:P * jj + w]
                                nc.tensor.matmul(o, kt1[:, P * j:P * j + kw], qt[:, q0:q0 + w], start=True, stop=False)
                                last = nc.tensor.matmul(o, kt2[:, P * j:P * j + kw], qm[:, q0:q0 + w],
                                                        start=False, stop=(j > i))
                                if j <= i:
                                    y = BIAS_W - P - P * (i - j)
                                    for r in (rel_hi, rel_lo):
                                        last = nc.tensor.matmul(o, r[:, y:y + kw], flipb[:, 0:w], start=False, stop=(r is rel_lo))
                            last.then_inc(s_st, 1)

                    def V1(i):
                        if plan.unit["1", i] >= 1:
                            pe.wait_ge(s_ao, plan.unit["1", i])
                        w = tokens(i)
                        for n, keys in enumerate(A1_K):
                            g = plan.exp["E1", i] + n
                            pe.wait_ge(s_exp, g + 1)
                            for jj, j in enumerate(keys):
                                kw = tokens(j)
                                last = nc.tensor.matmul(bank[4][0:w, 0:C + 1], pt[0:kw, g % PT_RING, P * jj:P * jj + w],
                                                        v1[0:kw, j, :], start=(j == 0), stop=(j == NT - 1))
                            last.then_inc(s_used, 1)

                    def wt(w, k, n):
                        return w[:, k * P:k * P + n]

                    def S2(i, h):
                        if i == 0 and h == 0:
                            for k in range(6):
                                taken(pe, "stack2", k)
                        w, q0 = tokens(i), P * i
                        groups = a2_s(i)
                        for n, (k0, k1) in enumerate(groups):
                            dst = score_bank(plan.score["S2", i, h] + n)
                            diag = n == len(groups) - 1
                            last = nc.tensor.matmul(dst[0:w, 0:k1 - k0], fq[:, h // 2, q0:q0 + w], fk[:, h % 2, k0:k1],
                                                    start=True, stop=not diag)
                            if diag:
                                last = nc.tensor.matmul(dst[0:w, q0 - k0:q0 - k0 + w], identb[0:w, 0:w], mask_s[0:w, 0:w],
                                                        start=False, stop=True)
                            last.then_inc(s_sc, 1)

                    def T2(i):
                        o, w = max_bank(plan.unit["2", i]), tokens(i)
                        for pr in range(2):
                            last = nc.tensor.transpose(o[:, P * pr:P * pr + w],
                                                       fqb[0:w, i, 2 * pr:2 * pr + 2, :].rearrange("p h c -> p (h c)"),
                                                       identb[0:w, 0:w])
                        last.then_inc(s_mT, 1)

                    def E2(i, h):
                        pe.wait_ge(s_m, plan.unit["2", i] + 1)
                        w, q0 = tokens(i), P * i
                        for n, keys in enumerate(a2_k(i)):
                            dst = exp_bank(plan.exp["E2", i, h] + n)
                            for jj, j in enumerate(keys):
                                kw, o = tokens(j), dst[0:tokens(j), P * jj:P * jj + w]
                                last = nc.tensor.matmul(o, fk[:, h % 2, P * j:P * j + kw], fqm[:, h // 2, q0:q0 + w],
                                                        start=True, stop=(j < i))
                                if j == i:
                                    last = nc.tensor.matmul(o, identb[0:kw, 0:kw], mask_t[0:kw, 0:w], start=False, stop=True)
                            last.then_inc(s_st, 1)

                    def V2(i):
                        if plan.unit["2", i] >= 1:
                            pe.wait_ge(s_ao, plan.unit["2", i])
                        w = tokens(i)
                        for n, keys in enumerate(a2_k(i)):
                            for h in range(NH):
                                pe.wait_ge(s_exp, plan.exp["E2", i, h] + n + 1)
                            for jj, j in enumerate(keys):
                                kw = tokens(j)
                                for h in range(NH):
                                    g = plan.exp["E2", i, h] + n
                                    last = nc.tensor.matmul(bank[4][32 * h:32 * h + 32, 0:w], vf[0:kw, j, h % 2, :],
                                                            pt[0:kw, g % PT_RING, P * jj:P * jj + w],
                                                            start=(j == 0), stop=(j == i))
                        last.then_inc(s_used, NH * len(a2_k(i)))

                    def X2(i):
                        pe.wait_ge(s_ot, i + 1)
                        w = tokens(i)
                        nc.tensor.transpose(bank[4][0:w, P:2 * P], ot[:, 0:w], ident[:, :]).then_inc(s_oT, 1)

                    def router(_):
                        for part in range(2):
                            taken(pe, "turn5", part)
                        o, _ = job("router", 0)
                        for i in range(NT):
                            w = tokens(i)
                            for wgt in (wt_hi, wt_lo):
                                last = nc.tensor.matmul(o[0:w, NE * i:NE * i + NE], ht_y[:, P * i:P * i + w],
                                                        wt(wgt, W_ROUTER, NE), start=(wgt is wt_hi), stop=(wgt is wt_lo))
                        last.then_inc(s_job, 1)

                    def up(t, c):
                        n, (a, z), r = t * NC + c, chunk_cols(t), rows_of(c)
                        if n == 0:
                            pe.wait_ge(s_red, plan.scores)
                            pe.wait_ge(s_exp, plan.exps)
                        if n >= 2:
                            pe.wait_ge(s_u, n - 1)
                        for k, first in ((0, W_ONE), (1, W_THREE)):
                            dst = bank[2 * (n % 2) + k][0:r, 0:z - a]
                            nc.tensor.matmul(dst, wt(wt_hi, first + c, r), ht_y[:, a:z], start=True, stop=False)
                            last = nc.tensor.matmul(dst, wt(wt_lo, first + c, r), ht_y[:, a:z], start=False, stop=True)
                        last.then_inc(s_ab, 1)
                        if t >= 1:
                            for m in range(3 * c, 3 * c + 3):
                                down_piece(t - 1, m)

                    def down_piece(t, m):
                        i, (c, e0, ne, blk) = CHUNK_TILES * t + m // NC, W2B[m % NC]
                        w, dst, r = tokens(i), bank[4 + i % 2], rows_of(c)
                        if m == 0:
                            pe.wait_ge(s_u, (t + 1) * NC)
                        if c == 0:
                            if i < 2:
                                pe.wait_ge((s_ao, s_m)[i], plan.units)
                            else:
                                pe.wait_ge(s_gated, i - 1)
                        q0 = P * (i % CHUNK_TILES)
                        last = nc.tensor.matmul(dst[0:w, C * e0:C * (e0 + ne)], hid[0:r, t % 2, c, q0:q0 + w],
                                                w2s[0:r, C * blk:C * (blk + ne)], start=(c == 0), stop=(c == NC - 1),
                                                skip_group_check=True)
                        if c == NC - 1:
                            last.then_inc(s_w2, 1)

                    steps = {
                        "tok": tok, "tokT": tokT, "stack1": stack1, "stack2": stack2, "S1": S1, "T1": T1, "E1": E1, "V1": V1,
                        "S2": S2, "T2": lambda i, h: T2(i), "E2": E2, "V2": lambda i, h: V2(i), "X2": lambda i, h: X2(i),
                        "router": router, "up": up, "down": lambda m: down_piece(2, m),
                        "turn1": lambda _: turn("turn1", hl_x, s_hl_x, 1), "turn2": lambda _: turn("turn2", hl_x, s_hl_x, 2),
                        "turn3": lambda _: turn("turn3", hl_y, s_hl_y, 1), "turn4": lambda _: turn("turn4", hl_y, s_hl_y, 2),
                        "turn5": lambda _: turn("turn5", hl_y, s_hl_y, 3),
                        "qkv1": lambda k: project("qkv1", k, range(2 * k, min(2 * k + 2, NT)), "turn1", ht_x,
                                                  wa_hi[:, 0:192], wa_lo[:, 0:192], 192),
                        "proj": lambda k: project("proj", k, (range(FULL), [FULL])[k], "turn2", ht_x,
                                                  wa_hi[:, 192:256], wa_lo[:, 192:256], C),
                        "qkv2": lambda k: project("qkv2", k, range(4 * k, min(4 * k + 4, NT)), "turn3", ht_y,
                                                  wt(wt_hi, W_QKV2, P), wt(wt_lo, W_QKV2, P), P),
                        "wo": lambda k: project("wo", k, (range(FULL), [FULL])[k], "turn4", ht_y,
                                                wt(wt_hi, W_WO, C), wt(wt_lo, W_WO, C), C),
                    }
                    for s in plan.order:
                        if s[0] in steps:
                            steps[s[0]](*s[1:])

                @block.scalar
                def _(act):
                    def job(name, k):
                        n = plan.job[name, k]
                        act.wait_ge(s_job, n + 1)
                        return bank[6 + n % 2], bankb[6 + n % 2], s_taken[n % 2]

                    def tok(g):
                        if g < 2:
                            o, _, _ = job("tok", g)
                            nc.scalar.copy(h_feat[:, :, 8 * g:8 * g + 8],
                                           o[0:C, :].rearrange("p (u v) -> p v u", v=V)).then_inc(s_early, 1)

                    def hi(src, ready, n, hl, s_hi):
                        if ready is not None:
                            act.wait_ge(ready, n)
                        nc.scalar.copy(hl[:, :, 0:C], src[:, :, :]).then_inc(s_hi, 1)

                    def turn(name, ht):
                        for part, tiles in enumerate(PARTS):
                            _, o, s = job(name, part)
                            c0, n = P * tiles[0], sum(tokens(i) for i in tiles)
                            nc.scalar.copy(ht[:, c0:c0 + n], o[:, 0:n]).then_inc(s, 1)

                    def split1(_):
                        for k in range(5):
                            taken(act, "qkv1", k)
                        nc.scalar.copy(ql[:, :, 0:C], qkv[:, :, 0:C])
                        nc.scalar.copy(ka[:, :, 0:C], qkv[:, :, C:2 * C]).then_inc(s_qk_hi, 1)
                        nc.scalar.copy(qb[:, :, 0:C], qkv[:, :, 0:C])
                        nc.scalar.copy(ka[:, :, C:2 * C], qkv[:, :, C:2 * C])
                        nc.scalar.copy(v1[:, 0:FULL, 0:C], qkv[:, 0:FULL, 2 * C:3 * C])
                        nc.scalar.copy(v1[0:REST, FULL, 0:C], qkv[0:REST, FULL, 2 * C:3 * C]).then_inc(s_qk_hi, 1)

                    def take(name, k, dst, rows):
                        _, o, s = job(name, k)
                        c0, n = P * PARTS[k % 2][0], sum(tokens(i) for i in PARTS[k % 2])
                        nc.scalar.copy(dst[:, c0:c0 + n], o[0:rows, 0:n]).then_inc(s, 1)

                    def stack1(k):
                        if k % 2 == 0:
                            take("stack1", k, (qt, kt1, kt2)[k // 2], (P, P, C + 2)[k // 2])

                    def qkv2(k):
                        o, _, s = job("qkv2", k)
                        if k < 2:
                            nc.scalar.copy(qkv_y[:, 4 * k:4 * k + 4, :], o[:, :].rearrange("p (i n) -> p i n", n=P)).then_inc(s, 1)
                        else:
                            nc.scalar.copy(qkv_y[0:REST, FULL, :], o[0:REST, 0:P]).then_inc(s, 1)

                    def split2(_):
                        act.wait_ge(s_rope, 1)
                        rq = rope[:, 0, :, 0:64].rearrange("p t (h c) -> p t h c", c=HD)
                        rk = rope[:, 0, :, 64:96].rearrange("p t (h c) -> p t h c", c=HD)
                        nc.scalar.copy(fqb[:, :, :, 0:HD], rq)
                        nc.scalar.copy(fkb[:, :, :, 0:HD], rk).then_inc(s_fqk_hi, 1)
                        nc.scalar.copy(fqb[:, :, :, 2 * HD:3 * HD], rq)
                        nc.scalar.copy(fkb[:, :, :, HD:2 * HD], rk)
                        for k in range(3):
                            taken(act, "qkv2", k)
                        vv = qkv_y[:, :, 96:128].rearrange("p t (g c) -> p t g c", g=NKV)
                        nc.scalar.copy(vf[:, 0:FULL, :, 0:HD], vv[:, 0:FULL, :, :])
                        nc.scalar.copy(vf[0:REST, FULL, :, 0:HD], vv[0:REST, FULL, :, :]).then_inc(s_fqk_hi, 1)

                    def stack2(k):
                        if k < 4 and k % 2 == 0:
                            take("stack2", k, fq[:, k // 2, :], P)

                    def exponents(g0, groups, w, scale_):
                        for n, keys in enumerate(groups):
                            g = g0 + n
                            if g >= PT_RING:
                                act.wait_ge(s_used, g - PT_RING + 1)
                            act.wait_ge(s_st, g + 1)
                            kw, m = tokens(keys[-1]), len(keys)

                            def view(t):
                                return t[0:kw, :].rearrange("p (j q) -> p j q", q=P)[:, 0:m, 0:w]

                            nc.scalar.activation(view(pt[:, g % PT_RING, :]), view(bank[2 + g % 2][:, :]), ACT.Exp,
                                                 scale=scale_).then_inc(s_exp, 1)

                    def T1(i):
                        w = tokens(i)
                        act.wait_ge(s_mT, plan.unit["1", i] + 1)
                        nc.scalar.copy(qm[:, P * i:P * i + w], bankb[5][0:C + 2, 0:w]).then_inc(s_m, 1)

                    def T2(i, _):
                        w = tokens(i)
                        act.wait_ge(s_mT, plan.unit["2", i] + 1)
                        nc.scalar.copy(fqm[:, :, P * i:P * i + w],
                                       bankb[5][:, 0:2 * P].rearrange("p (r q) -> p r q", q=P)[:, :, 0:w]).then_inc(s_m, 1)

                    def V2(i, _):
                        w = tokens(i)
                        act.wait_ge(s_used, plan.exp["E2", i, NH - 1] + len(a2_k(i)))
                        if i >= 1:
                            act.wait_ge(s_oT, i)
                        nc.scalar.copy(ot[:, 0:w], bank[4][:, 0:w]).then_inc(s_ot, 1)

                    def router(_):
                        act.wait_ge(s_logit, 3)
                        nc.scalar.activation(gate_e[:, :, :], gate_l[:, :, :], ACT.Exp).then_inc(s_gexp, 1)

                    def up(t, c):
                        n, r, (a, z) = t * NC + c, rows_of(c), chunk_cols(t)
                        act.wait_ge(s_ab, n + 1)
                        if n >= 3:
                            act.wait_ge(s_u, n - 2)
                        nc.scalar.activation(silu[0:r, n % 3, 0:z - a], bank[2 * (n % 2)][0:r, 0:z - a],
                                             ACT.Silu).then_inc(s_silu, 1)

                    steps = {
                        "tok": tok, "split1": split1, "stack1": stack1, "qkv2": qkv2, "split2": split2, "stack2": stack2,
                        "T1": T1, "T2": T2, "V2": V2, "router": router, "up": up,
                        "ln1b": lambda _: hi(hn, s_gain_x, 1, hl_x, s_hi_x),
                        "aosplit1": lambda _: hi(ao_x, s_ao, plan.units, hl_x, s_hi_x),
                        "ystart": lambda _: hi(hn, None, 0, hl_y, s_hi_y),
                        "aosplit2": lambda _: hi(ao_y, s_ao, plan.unit["2", NT - 1] + 1, hl_y, s_hi_y),
                        "rms": lambda _: hi(hn_y, s_gain_y, 1, hl_y, s_hi_y),
                        "turn1": lambda _: turn("turn1", ht_x), "turn2": lambda _: turn("turn2", ht_x),
                        "turn3": lambda _: turn("turn3", ht_y), "turn4": lambda _: turn("turn4", ht_y),
                        "turn5": lambda _: turn("turn5", ht_y),
                        "E1": lambda i: exponents(plan.exp["E1", i], A1_K, tokens(i), 1.0),
                        "E2": lambda i, h: exponents(plan.exp["E2", i, h], a2_k(i), tokens(i), float(HD) ** -0.5),
                    }
                    for s in plan.order:
                        if s[0] in steps:
                            steps[s[0]](*s[1:])

                @block.gpsimd
                def _(pool):
                    count = [0]

                    def link(ins):
                        count[0] += 1
                        ins.then_inc(s_pool, 1)
                        pool.wait_ge(s_pool, count[0])

                    def normalize(dst, src, stat, k):
                        half = const[:, K_HALF:K_HALF + 1].to_broadcast([P, NT])
                        link(nc.gpsimd.tensor_tensor(stat[:, 7, :], stat[:, k, :], half, ALU.pow))
                        link(nc.gpsimd.tensor_tensor(dst[:, :, :], src[:, :, :], per_token(stat[:, 7, :], C), ALU.mult))

                    def lo(src, hl, s_hi, n, s_hl):
                        pool.wait_ge(s_hi, n)
                        nc.gpsimd.tensor_tensor(hl[:, :, C:P], src[:, :, :], hl[:, :, 0:C], ALU.subtract).then_inc(s_hl, 1)

                    def ln1b(_):
                        pool.wait_ge(s_norm_x, 1)
                        normalize(hn, xc, stat_x, 3)
                        link(nc.gpsimd.tensor_tensor(hn[:, :, :], hn[:, :, :], par_b(G1), ALU.mult))
                        nc.gpsimd.tensor_tensor(hn[:, :, :], hn[:, :, :], par_b(B1), ALU.add).then_inc(s_gain_x, 1)
                        pool.wait_ge(s_gain_x, 1)
                        lo(hn, hl_x, s_hi_x, 1, s_hl_x)

                    def split1(_):
                        pool.wait_ge(s_qk_hi, 1)
                        nc.gpsimd.tensor_tensor(ql[:, :, C:P], qkv[:, :, 0:C], ql[:, :, 0:C], ALU.subtract)
                        nc.gpsimd.tensor_tensor(kb[:, :, 0:C], qkv[:, :, C:P], ka[:, :, 0:C], ALU.subtract).then_inc(s_qk_lo, 1)

                    def ln2b(_):
                        pool.wait_ge(s_norm_x, 2)
                        normalize(hn, xc, stat_x, 3)
                        link(nc.gpsimd.tensor_tensor(hn[:, :, :], hn[:, :, :], par_b(G2), ALU.mult))
                        link(nc.gpsimd.tensor_tensor(hn[:, :, :], hn[:, :, :], par_b(B2), ALU.add))
                        nc.gpsimd.tensor_tensor(h1_next[:, :, :], hn[:, :, :], h0[:, :, :], ALU.add).then_inc(s_h1, 1)

                    def ln3b(_):
                        pool.wait_ge(s_norm_x, 3)
                        normalize(xl_next, xc, stat_x, 3)
                        normalize(hn, xl_next, stat_x, 5)
                        link(nc.gpsimd.tensor_tensor(hn[:, :, :], hn[:, :, :], par_b(FW1), ALU.mult))

                    def rope_(_):
                        for k in range(3):
                            taken(pool, "qkv2", k)
                        nc.gpsimd.memset(fqb[:, :, :, 3 * HD:3 * HD + 2], 0.0)
                        qk = qkv_y[:, :, 0:96].rearrange("p t (h c) -> p t h c", c=HD)
                        rot = rope[:, 1, :, :].rearrange("p t (h c) -> p t h c", c=HD)
                        sin = const[:, K_SIN:K_SIN + NT * HD].rearrange("p (t c) -> p t c", c=HD)
                        for a, z in ((0, HD // 2), (HD // 2, HD)):
                            o = HD // 2 - a
                            last = nc.gpsimd.tensor_tensor(rot[:, :, :, a:z], qk[:, :, :, o:o + HD // 2],
                                                           sin[:, :, a:z].unsqueeze(2).to_broadcast([P, NT, 6, HD // 2]), ALU.mult)
                        last.then_inc(s_rot, 1)

                    def split2(_):
                        pool.wait_ge(s_fqk_hi, 1)
                        rq = rope[:, 0, :, 0:64].rearrange("p t (h c) -> p t h c", c=HD)
                        rk = rope[:, 0, :, 64:96].rearrange("p t (h c) -> p t h c", c=HD)
                        nc.gpsimd.tensor_tensor(fqb[:, :, :, HD:2 * HD], rq, fqb[:, :, :, 0:HD], ALU.subtract)
                        nc.gpsimd.tensor_tensor(fkb[:, :, :, 2 * HD:3 * HD], rk, fkb[:, :, :, 0:HD], ALU.subtract).then_inc(s_fqk_lo, 1)

                    def rms(_):
                        pool.wait_ge(s_norm_y, 1)
                        normalize(hn_y, x1, stat_y, 3)
                        nc.gpsimd.tensor_tensor(hn_y[:, :, :], hn_y[:, :, :], par_b(FW2), ALU.mult).then_inc(s_gain_y, 1)
                        pool.wait_ge(s_gain_y, 1)
                        lo(hn_y, hl_y, s_hi_y, 3, s_hl_y)
                        link(nc.gpsimd.tensor_tensor(xl[:, :, :], h1[:, :, :], x1[:, :, :], ALU.add))

                    def add_experts(i):
                        w = tokens(i)
                        pool.wait_ge(s_gated, i + 1)
                        g = gated[0:w, i % 2, :]
                        for half in (4 * C, 2 * C, C):
                            link(nc.gpsimd.tensor_tensor(g[:, 0:half], g[:, 0:half], g[:, half:2 * half], ALU.add))
                        nc.gpsimd.tensor_tensor(res[0:w, i, :], g[:, 0:C], xl[0:w, i, :], ALU.add).then_inc(s_res, 1)

                    def aosplit(n, ao, hl, s_hi, s_hl):
                        pool.wait_ge(s_ao, n)
                        lo(ao, hl, s_hi, 2, s_hl)

                    def finished(t, m):
                        return CHUNK_TILES * t + m // NC - 1 if m and m % NC == 0 else None

                    def up(t, c):
                        if t >= 1:
                            for m in range(3 * c + 1, 3 * c + 4):
                                if finished(t - 1, m) is not None:
                                    add_experts(finished(t - 1, m))

                    def down(m):
                        if finished(2, m + 1) is not None:
                            add_experts(finished(2, m + 1))

                    steps = {
                        "ln1b": ln1b, "split1": split1, "ln2b": ln2b, "ln3b": ln3b, "rope": rope_, "split2": split2, "rms": rms,
                        "up": up, "down": down,
                        "aosplit1": lambda _: aosplit(plan.units, ao_x, hl_x, s_hi_x, s_hl_x),
                        "ystart": lambda _: lo(hn, hl_y, s_hi_y, 1, s_hl_y),
                        "aosplit2": lambda _: aosplit(plan.unit["2", NT - 1] + 1, ao_y, hl_y, s_hi_y, s_hl_y),
                    }
                    for s in plan.order:
                        if s[0] in steps:
                            steps[s[0]](*s[1:])

                @block.vector
                def _(dve):
                    count = [0]

                    def link(ins):
                        count[0] += 1
                        ins.then_inc(s_dve, 1)
                        dve.wait_ge(s_dve, count[0])

                    def job(name, k):
                        n = plan.job[name, k]
                        dve.wait_ge(s_job, n + 1)
                        return bank[6 + n % 2], bankb[6 + n % 2], s_taken[n % 2]

                    def center(src):
                        link(nc.vector.tensor_reduce(stat_x[:, 0, :], src[:, :, :], AX.X, ALU.add))
                        link(nc.vector.tensor_scalar(stat_x[:, 1, :], stat_x[:, 0, :], 1.0 / C, None, ALU.mult))
                        link(nc.vector.tensor_tensor(xc[:, :, :], src[:, :, :], per_token(stat_x[:, 1, :], C), ALU.subtract))

                    def mean_square(src, stat):
                        link(nc.vector.tensor_tensor(sq[:, :, :], src[:, :, :], src[:, :, :], ALU.mult))
                        link(nc.vector.tensor_reduce(stat[:, 0, :], sq[:, :, :], AX.X, ALU.add))
                        link(nc.vector.tensor_scalar(stat[:, 2, :], stat[:, 0, :], 1.0 / C, None, ALU.mult))

                    def tok(g):
                        n0, n1, u0 = ((0, 7, 1), (7, 15, 0), (15, 16, 0))[g]
                        o, _, s = job("tok", g)
                        dve.wait_ge(s_early, min(g, 1) + 1)
                        late = o[C:P, :].rearrange("p (u v) -> p v u", v=V)[:, :, u0:u0 + n1 - n0]
                        nc.vector.tensor_tensor(h_feat[:, :, n0:n1], late, h_feat[:, :, n0:n1], ALU.add).then_inc(s, 1)

                    def tokT(_):
                        o, _, s = job("tokT", 0)
                        nc.vector.tensor_copy(h0[:, 0:FULL, :], o[:, :].rearrange("p (i c) -> p i c", c=C)).then_inc(s, 1)

                    def ln1a(_):
                        taken(dve, "tokT", 0)
                        dve.wait_ge(s_txt, 16)
                        center(h0)

                    def ln1b(_):
                        mean_square(xc, stat_x)
                        nc.vector.tensor_scalar(stat_x[:, 3, :], stat_x[:, 2, :], 1.0 + LN_EPS, LN_EPS * LN_EPS,
                                                ALU.mult, ALU.add).then_inc(s_norm_x, 1)

                    def qkv1(k):
                        o, _, s = job("qkv1", k)
                        n, w = (2, P) if k < 4 else (1, REST)
                        nc.vector.tensor_tensor(qkv[0:w, 2 * k:2 * k + n, :], o[0:w, 0:192 * n].rearrange("p (i n) -> p i n", n=192),
                                                par_b(BQKV, 192, n, w), ALU.add).then_inc(s, 1)

                    def take(name, k, dst, rows):
                        _, o, s = job(name, k)
                        c0, n = P * PARTS[k % 2][0], sum(tokens(i) for i in PARTS[k % 2])
                        nc.vector.tensor_copy(dst[:, c0:c0 + n], o[0:rows, 0:n]).then_inc(s, 1)

                    def stack1(k):
                        if k % 2:
                            take("stack1", k, (qt, kt1, kt2)[k // 2], (P, P, C + 2)[k // 2])

                    def stack2(k):
                        if k < 4:
                            if k % 2:
                                take("stack2", k, fq[:, k // 2, :], P)
                            return
                        _, o, s = job("stack2", k)
                        c0, n = P * PARTS[k % 2][0], sum(tokens(i) for i in PARTS[k % 2])
                        for g in range(NKV):
                            last = nc.vector.tensor_copy(fk[FS * g:FS * g + FS, g, c0:c0 + n], o[FS * g:FS * g + FS, 0:n])
                        last.then_inc(s, 1)

                    def reduce_groups(g0, groups, w, h):
                        for n, (k0, k1) in enumerate(groups):
                            dve.wait_ge(s_sc, g0 + n + 1)
                            nc.vector.tensor_reduce(pmax[0:w, h, n:n + 1], bank[(g0 + n) % 2][0:w, 0:k1 - k0],
                                                    AX.X, ALU.max).then_inc(s_red, 1)
                        return g0 + len(groups)

                    def max_row(u, done, parts, mx, hi_, lo_):
                        dve.wait_ge(s_red, done)
                        nc.vector.tensor_reduce(mx, parts, AX.X, ALU.max).then_inc(s_max, 1)
                        dve.wait_ge(s_max, u + 1)
                        link(nc.vector.tensor_scalar(hi_, mx, -1.0, None, ALU.mult))
                        nc.vector.tensor_tensor(lo_, mx, hi_, ALU.add).then_inc(s_mrow, 1)

                    def S1(i):
                        w = tokens(i)
                        done = reduce_groups(plan.score["S1", i], A1_S, w, 0)
                        max_row(plan.unit["1", i], done, pmax[0:w, 0, 0:len(A1_S)], rmax[0:w, i, 0:1],
                                qb[0:w, i, C:C + 1], qb[0:w, i, C + 1:C + 2])

                    def O1(i):
                        w = tokens(i)
                        dve.wait_ge(s_used, plan.exp["E1", i] + len(A1_K))
                        link(nc.vector.reciprocal(rec[0:w, 0:1], bank[4][0:w, C:C + 1]))
                        nc.vector.tensor_scalar(ao_x[0:w, i, :], bank[4][0:w, 0:C], rec[0:w, 0:1], scale[0:w, 0:1],
                                                ALU.mult, ALU.mult).then_inc(s_ao, 1)

                    def S2(i, h):
                        w, groups, M = tokens(i), a2_s(i), 3 * HD
                        done = reduce_groups(plan.score["S2", i, h], groups, w, h)
                        if h == NH - 1:
                            max_row(plan.unit["2", i], done, pmax[0:w, :, 0:len(groups)], rmax[0:w, i, :],
                                    fqb[0:w, i, :, M], fqb[0:w, i, :, M + 1])

                    def O2(i, _):
                        w = tokens(i)
                        dve.wait_ge(s_oT, i + 1)
                        o = bank[4][0:w, P:2 * P].rearrange("p (h c) -> p h c", c=32)
                        link(nc.vector.reciprocal(rec[0:w, :], o[:, :, HD]))
                        nc.vector.tensor_tensor(ao_y[0:w, i, :].rearrange("p (g r c) -> p r g c", g=2, r=2),
                                                o[:, :, 0:HD].rearrange("p (r g) c -> p r g c", r=2),
                                                rec[0:w, :].rearrange("p (r g) -> p r g", r=2).unsqueeze(3).to_broadcast([w, 2, 2, HD]),
                                                ALU.mult).then_inc(s_ao, 1)

                    def from_project(name, k, dst, add):
                        o, _, s = job(name, k)
                        if k == 0:
                            nc.vector.tensor_tensor(dst[:, 0:FULL, :], o[:, :].rearrange("p (i c) -> p i c", c=C),
                                                    add[:, 0:FULL, :], ALU.add).then_inc(s, 1)
                        else:
                            nc.vector.tensor_tensor(dst[0:REST, FULL, :], o[0:REST, 0:C], add[0:REST, FULL, :], ALU.add).then_inc(s, 1)

                    def ln2a(_):
                        for k in range(2):
                            taken(dve, "proj", k)
                        center(xt)

                    def ln2b(_):
                        mean_square(xc, stat_x)
                        nc.vector.tensor_scalar(stat_x[:, 3, :], stat_x[:, 2, :], LN_EPS, None, ALU.add).then_inc(s_norm_x, 1)

                    def ln3a(_):
                        dve.wait_ge(s_h1, 1)
                        center(h1_next)

                    def ln3b(_):
                        mean_square(xc, stat_x)
                        link(nc.vector.tensor_scalar(stat_x[:, 3, :], stat_x[:, 2, :], LN_EPS, None, ALU.add))
                        link(nc.vector.reciprocal(stat_x[:, 5, :], stat_x[:, 3, :]))
                        link(nc.vector.tensor_tensor(stat_x[:, 5, :], stat_x[:, 2, :], stat_x[:, 5, :], ALU.mult))
                        nc.vector.tensor_scalar(stat_x[:, 5, :], stat_x[:, 5, :], RMS_EPS, None, ALU.add).then_inc(s_norm_x, 1)

                    def ystart(_):
                        nc.vector.tensor_copy(h1[:, :, :], h1_next[:, :, :])
                        nc.vector.tensor_copy(xl[:, :, :], xl_next[:, :, :]).then_inc(s_copy, 1)

                    def rope_(_):
                        for k in range(3):
                            taken(dve, "qkv2", k)
                        cos = const[:, K_COS:K_COS + NT * HD].rearrange("p (t c) -> p t c", c=HD)
                        link(nc.vector.tensor_tensor(rope[:, 0, :, :].rearrange("p t (h c) -> p t h c", c=HD),
                                                     qkv_y[:, :, 0:96].rearrange("p t (h c) -> p t h c", c=HD),
                                                     cos.unsqueeze(2).to_broadcast([P, NT, 6, HD]), ALU.mult))
                        dve.wait_ge(s_rot, 1)
                        nc.vector.tensor_tensor(rope[:, 0, :, :], rope[:, 0, :, :], rope[:, 1, :, :], ALU.add).then_inc(s_rope, 1)

                    def rms(_):
                        for k in range(2):
                            taken(dve, "wo", k)
                        mean_square(x1, stat_y)
                        nc.vector.tensor_scalar(stat_y[:, 3, :], stat_y[:, 2, :], RMS_EPS, None, ALU.add).then_inc(s_norm_y, 1)

                    def router(_):
                        o, _, s = job("router", 0)
                        nc.vector.tensor_copy(gate_l[:, 0:FULL, :], o[:, 0:FULL * NE].rearrange("p (i e) -> p i e", e=NE)).then_inc(s_logit, 1)
                        nc.vector.tensor_copy(gate_l[0:REST, FULL, :], o[0:REST, FULL * NE:NT * NE]).then_inc(s, 1)
                        dve.wait_ge(s_logit, 1)
                        taken(dve, "router", 0)
                        nc.vector.tensor_reduce(gate_s[:, 0, :], gate_l[:, :, :], AX.X, ALU.max).then_inc(s_logit, 1)
                        dve.wait_ge(s_logit, 2)
                        nc.vector.tensor_tensor(gate_l[:, :, :], gate_l[:, :, :], per_token(gate_s[:, 0, :], NE), ALU.subtract).then_inc(s_logit, 1)

                    def pick(m, sel):
                        desc = const[:, K_DESC:K_DESC + NE].unsqueeze(1).to_broadcast([P, NT, NE])
                        link(nc.vector.tensor_reduce(gate_s[:, m, :], gate_p[:, :, :], AX.X, ALU.max))
                        link(nc.vector.tensor_tensor(sel[:, :, :], gate_p[:, :, :], per_token(gate_s[:, m, :], NE), ALU.is_equal))
                        link(nc.vector.tensor_tensor(sel[:, :, :], sel[:, :, :], desc, ALU.mult))
                        link(nc.vector.tensor_reduce(gate_s[:, 3, :], sel[:, :, :], AX.X, ALU.max))
                        link(nc.vector.tensor_tensor(sel[:, :, :], sel[:, :, :], per_token(gate_s[:, 3, :], NE), ALU.is_equal))

                    def gates(part):
                        if part == 0:
                            dve.wait_ge(s_gexp, 1)
                            link(nc.vector.tensor_reduce(gate_s[:, 0, :], gate_e[:, :, :], AX.X, ALU.add))
                            link(nc.vector.reciprocal(gate_s[:, 5, :], gate_s[:, 0, :]))
                            link(nc.vector.tensor_tensor(gate_e[:, :, :], gate_e[:, :, :], per_token(gate_s[:, 5, :], NE), ALU.mult))
                            link(nc.vector.tensor_copy(gate_p[:, :, :], gate_e[:, :, :]))
                        if part == 1:
                            pick(1, gate_m)
                            link(nc.vector.scalar_tensor_tensor(gate_p[:, :, :], gate_m[:, :, :], -2.0, gate_p[:, :, :], ALU.mult, ALU.add))
                        if part == 2:
                            pick(2, gate_w)
                            link(nc.vector.tensor_tensor(gate_m[:, :, :], gate_m[:, :, :], gate_w[:, :, :], ALU.add))
                        if part == 3:
                            link(nc.vector.tensor_tensor(gate_m[:, :, :], gate_m[:, :, :], gate_e[:, :, :], ALU.mult))
                            link(nc.vector.tensor_tensor(gate_s[:, 4, :], gate_s[:, 1, :], gate_s[:, 2, :], ALU.add))
                            link(nc.vector.tensor_scalar(gate_s[:, 4, :], gate_s[:, 4, :], 1e-9, None, ALU.add))
                            link(nc.vector.reciprocal(gate_s[:, 5, :], gate_s[:, 4, :]))
                            link(nc.vector.tensor_tensor(gate_w[:, :, :], gate_m[:, :, :], per_token(gate_s[:, 5, :], NE), ALU.mult))

                    def gate_tile(i):
                        w = tokens(i)
                        dve.wait_ge(s_w2, i + 1)
                        if i >= 2:
                            dve.wait_ge(s_res, i - 1)
                        nc.vector.tensor_tensor(gated[0:w, i % 2, :].rearrange("p (e c) -> p e c", c=C),
                                                bank[4 + i % 2][0:w, :].rearrange("p (e c) -> p e c", c=C),
                                                per_token(gate_w[0:w, i, :], C), ALU.mult).then_inc(s_gated, 1)

                    def up(t, c):
                        n, r, (a, z) = t * NC + c, rows_of(c), chunk_cols(t)
                        dve.wait_ge(s_silu, n + 1)
                        if t == 2 and c == 0:
                            dve.wait_ge(s_w2, CHUNK_TILES)
                        nc.vector.tensor_tensor(hid[0:r, t % 2, c, 0:z - a], bank[2 * (n % 2) + 1][0:r, 0:z - a],
                                                silu[0:r, n % 3, 0:z - a], ALU.mult).then_inc(s_u, 1)
                        if t == 0 and 2 <= c < 6:
                            gates(c - 2)
                        if t >= 1:
                            for m in range(3 * c + 1, 3 * c + 4):
                                if m % NC == 0:
                                    gate_tile(CHUNK_TILES * (t - 1) + m // NC - 1)

                    def down(m):
                        if (m + 1) % NC == 0:
                            gate_tile(CHUNK_TILES * 2 + m // NC)

                    steps = {
                        "tok": tok, "tokT": tokT, "ln1a": ln1a, "ln1b": ln1b, "qkv1": qkv1, "stack1": stack1, "stack2": stack2,
                        "S1": S1, "O1": O1, "S2": S2, "O2": O2, "ln2a": ln2a, "ln2b": ln2b, "ln3a": ln3a, "ln3b": ln3b,
                        "ystart": ystart, "rope": rope_, "rms": rms, "router": router, "up": up, "down": down,
                        "proj": lambda k: from_project("proj", k, xt, par_b(BPROJ)),
                        "wo": lambda k: from_project("wo", k, x1, xl),
                    }
                    for s in plan.order:
                        if s[0] in steps:
                            steps[s[0]](*s[1:])

            nums = [s.num for s in sems]
            nc.gpsimd.sem_clear(range(min(nums), max(nums) + 1))
            nc.all_engine_barrier()

        run_pass(Plan(ORDER_X), 0, None, 1)
        with nc.Fori(0, B - 1) as b:
            run_pass(Plan(ORDER_XY), b + 1, b, (b + 2) % B)
        run_pass(Plan(ORDER_Y), None, B - 1, None)


def constants():
    import numpy as np
    k = np.arange(P)
    c = np.zeros((P, NCONST), np.float32)
    c[:, K_ID:K_ID + P] = np.eye(P)
    c[:, K_FLIP:K_FLIP + P] = np.eye(P)[::-1]
    c[:, K_MS:K_MS + P] = np.where(k[None, :] > k[:, None], -1e30, 0)
    c[:, K_MT:K_MT + P] = np.where(k[:, None] > k[None, :], -1e30, 0)
    inv = 1.0 / 10000.0 ** (np.arange(0, HD, 2, dtype=np.float32) / HD)
    fr = np.outer(np.arange(NT * P, dtype=np.float32), inv)
    emb = np.concatenate([fr, fr], axis=-1)
    sign = np.concatenate([-np.ones(HD // 2), np.ones(HD // 2)])
    for off, t in ((K_COS, np.cos(emb)), (K_SIN, np.sin(emb) * sign)):
        c[:, off:off + NT * HD] = t.reshape(NT, P, HD).transpose(1, 0, 2).reshape(P, NT * HD)
    c[:, K_DESC:K_DESC + NE] = np.arange(NE, 0, -1)
    c[:, K_HALF] = -0.5
    f, p = np.arange(NFREQ)[:, None], np.arange(PATCH)[None, :]
    ang = 2 * np.pi * f * p / PATCH
    dft = np.concatenate([np.cos(ang), -np.sin(ang)]) / np.sqrt(PATCH)
    return c, dft.astype(np.float32)


_INS = {
    'x': ('x', None), 'txt': ('txt', None), 'tok_w': ('L0_tok_W', None),
    'ln1_g': ('L0_attn_ln1_g', (1, -1)), 'ln1_b': ('L0_attn_ln1_b', (1, -1)), 'qkv_w': ('L0_attn_qkv_w', None),
    'qkv_b': ('L0_attn_qkv_b', (1, -1)), 'bias_table': ('L0_attn_bias_table', (1, -1)),
    'attn_scale': ('L0_attn_scale', (1, 1)), 'proj_w': ('L0_attn_proj_w', None), 'proj_b': ('L0_attn_proj_b', (1, -1)),
    'ln2_g': ('L0_attn_ln2_g', (1, -1)), 'ln2_b': ('L0_attn_ln2_b', (1, -1)), 'f_ln1': ('L0_ffn_ln1_w', (1, -1)),
    'f_ln2': ('L0_ffn_ln2_w', (1, -1)), 'wq': ('L0_ffn_wq', None), 'wk': ('L0_ffn_wk', None), 'wv': ('L0_ffn_wv', None),
    'wo': ('L0_ffn_wo', None), 'router_w': ('L0_ffn_router_w', None), 'w1': ('L0_ffn_w1', None),
    'w2': ('L0_ffn_w2', None), 'w3': ('L0_ffn_w3', None),
}


def kernel(**inputs):
    import numpy as np
    import concourse.bacc as bacc
    from concourse.bass_utils import run_bass_kernel_spmd as run

    nc = bacc.Bacc("TRN2", target_bir_lowering=False, num_devices=1)
    arrays, aps = {}, {}

    def give(name, a):
        arrays[f"in_{name}"] = a
        aps[name] = nc.dram_tensor(f"in_{name}", a.shape, mybir.dt.from_np(a.dtype), kind="ExternalInput").ap()

    for name, (key, shape) in _INS.items():
        a = np.ascontiguousarray(inputs[key])
        give(name, a if shape is None else a.reshape(shape))
    const, dft = constants()
    give("const", const)
    give("dft", dft)
    out = nc.dram_tensor("out_dram", (B, TOK, C), F32, kind="ExternalOutput").ap()
    program(nc, aps, out)
    r = run(nc, [arrays], core_ids=[0])
    return r.results[0]["out_dram"]
```

```python
from contextlib import ExitStack

import concourse.bass as bass
from concourse import mybir

F32 = mybir.dt.float32
BF16 = mybir.dt.bfloat16
ALU = mybir.AluOpType
ACT = mybir.ActivationFunctionType
AX = mybir.AxisListType

B, C, TIME, V = 4, 64, 128, 64
TXT = 32
PATCH, STRIDE = 16, 8
NPATCH = TIME // STRIDE
NFREQ = PATCH // 2 + 1
TOK = V * NPATCH + TXT
P = 128
NT = (TOK + P - 1) // P
FULL = TOK // P
REST = TOK - FULL * P
SPAN = 1023
LN_EPS, RMS_EPS = 1e-5, 1e-6
NH, NKV, HD = 4, 2, 16
NE, HID = 8, 170
ROWS = NE * HID
NC = (ROWS + P - 1) // P
FS = 64
HALF = 4
G1, B1, BQKV, BPROJ, G2, B2, FW1, FW2 = 0, 64, 128, 320, 384, 448, 512, 576
NPAR = 640
K_ID, K_FLIP, K_MS, K_MT, K_COS, K_SIN, K_DESC, K_HALF = 0, 128, 256, 384, 512, 656, 800, 808
NCONST = 809
W_QKV2, W_WO, W_ROUTER, W_ONE, W_THREE = 0, 1, 2, 3, 3 + NC
NWT = 3 + 2 * NC
BIAS_PAD = 96
BIAS_W = NT * P
BIAS_LEN = BIAS_W + P - 1
PT_RING = 12
CUT = 5
PARTS = (range(0, CUT), range(CUT, NT))
CHUNK_TILES = 3
CW = CHUNK_TILES * P


def pair(n):
    return n % 3 if n < NC else n % 2


def tokens(i):
    return P if i < FULL else REST


def rows_of(c):
    return min(P, ROWS - c * P)


def w2_blocks():
    out, blk = [], 0
    for c in range(NC):
        e0, e1 = c * P // HID, (c * P + rows_of(c) - 1) // HID
        out.append((c, e0, e1 - e0 + 1, blk))
        blk += e1 - e0 + 1
    return out, blk


W2B, NBLK = w2_blocks()

A1_S = [(0, 384), (384, 768), (768, TOK)]


def a2_s(i):
    n = min(TOK, (i + 1) * P)
    parts = (n + 511) // 512
    return [(n * g // parts, n * (g + 1) // parts) for g in range(parts)]


def key_groups(i, last):
    n = 512 // tokens(i)
    return [range(a, min(a + n, last + 1, FULL)) for a in range(0, min(last + 1, FULL), n)] + (
        [range(FULL, NT)] if last == FULL else [])


def a1_k(i):
    return key_groups(i, NT - 1)


def a2_k(i):
    return key_groups(i, i)


def spread(main, side):
    at = [(n + 0.5, 0, n) for n in range(len(main))]
    at += [((n + 0.5) * len(main) / len(side), 1, n) for n in range(len(side))]
    return [(main, side)[which][n] for _, which, n in sorted(at)]


def place(main, *sides):
    at = [(n, -1, n, e) for n, e in enumerate(main)]
    for c, (steps, places) in enumerate(sides):
        assert len(steps) == len(places)
        at += [(n - 0.5, c, k, e) for k, (e, n) in enumerate(zip(steps, places))]
    return [e for *_, e in sorted(at, key=lambda a: a[:3])]


TOK_X = [[("tok", 0)], [("tok", 1)], [("tok", 2)]]
TOK_HEAD = [[("tokT", 0)], [("ln1a", 0)], [("ln1b", 0)], [("ln1c", 0)]]
TOK_TAIL = [[("turn1", 0)], [("qkv1", k) for k in range(3)], [("qkv1", 3), ("qkv1", 4)], [("split1", 0)],
            [("stack1", k) for k in range(3)], [("stack1", k) for k in range(3, 6)]]
HEADS = [[("ystart", 0)], [("turn3", 0)], [("qkv2", k) for k in range(3)], [("rope", 0)], [("split2", 0)],
         [("stack2", k) for k in range(3)], [("stack2", k) for k in range(3, 6)]]
X_END = [[("aosplit1", 0)], [("turn2", 0)], [("proj", 0), ("proj", 1)], [("ln2a", 0)], [("ln2b", 0)],
         [("ln2c", 0)], [("ln3a", 0)], [("ln3b", 0)], [("ln3c", 0)]]
Y_MID = [[("aosplit2", 0)], [("turn4", 0)], [("wo", 0), ("wo", 1)], [("rmsa", 0)], [("rmsb", 0)], [("turn5", 0)], [("router", 0)]]
MOE = [[("up", t, c)] for t in range(3) for c in range(NC)]
MOE_END = [[("down", m) for m in range(a, a + 3)] for a in range(0, 3 * NC, 3)]
WEIGHTS = [[("wa", 0)], [("wt", 0), ("wt", 1)], [("wt", 2), ("wt", 3)], [("w2blocks", 0)], [("rel", 0)],
           [("wt", 4), ("wt", 5)], [("wt", 6)], [("w2", 0)], [("w2", 1)], [("w2", 2)]]

A1_LATE = 5
A2_TILES = list(range(NT))[::-1]
PLACE = {i: n for n, i in enumerate(A2_TILES)}


def attention_order(one, two, late=0):
    def tile1(k):
        return k - late if one and 0 <= k - late < NT else None

    def tile2(k):
        return A2_TILES[k] if two and 0 <= k < NT else None

    def step(kind, i, *part):
        return [(kind, i, *part)] if i is not None else []

    def parts(kind, i, groups, *head):
        return [(kind, i, *head, n) for n in range(len(groups(i)))] if i is not None else []

    out = []
    for k in range(NT + 2 + late):
        i0, i1, i2, j0, j1, j2 = tile2(k), tile2(k - 1), tile2(k - 2), tile1(k), tile1(k - 1), tile1(k - 2)
        scores = sum((parts("S2", i0, a2_s, h) for h in range(NH)), []) + parts("S1", j0, lambda _: A1_S)
        e2 = [parts("E2", i1, a2_k, h) for h in range(NH)]
        v2, v1, e1 = parts("V2", i2, a2_k), parts("V1", j2, a1_k), parts("E1", j1, a1_k)
        if i1 is not None:
            rest = (v2 + step("T2", i1) + step("X2", i2) + step("T1", j1) + spread(e2[0] + e2[1] + e2[2], v1)
                    + step("O1", j2) + step("O2", i2) + spread(e2[3], e1))
        else:
            rest = v1 + step("T1", j1) + step("O1", j2) + v2 + step("X2", i2) + step("O2", i2) + e1
        out += spread(rest, scores) if scores and rest else rest + scores
    return [[s] for s in out]


A1, A2 = attention_order(True, False), attention_order(False, True)
A12 = attention_order(True, True, A1_LATE)
LAST_A2 = A12.index([("O2", A2_TILES[-1])]) + 1
MID_AT = [2, 6, 14, 18, 24, 30, 36]
TOK_AT = [0, 16, 30]
X_AT = [0, 2, 4, 4, 5, 11, 12, 14, 17, 18, 20, 22, 24, 27, 30, 33]
NEXT_AT = [19, 21, 25, 28, 30, 32, 32, 35, 39, 43]
WEIGHTS_AT = [0, 2, 3, 4, 4, 5, 6, 8, 9, 10]
START_AT = [2, 5, 8, 10, 12, 13, 15, 16, 16, 16, 16, 16, 16]
A12_END = A12[:LAST_A2] + place(A12[LAST_A2:], (Y_MID, MID_AT))
A12_TOK = A12[:LAST_A2] + place(A12[LAST_A2:], (Y_MID, MID_AT), (TOK_X, TOK_AT))

ORDER_FIRST = [[("fold", 0)]] + TOK_X + place(TOK_HEAD + TOK_TAIL, (WEIGHTS, WEIGHTS_AT))
ORDER_START = A1 + place(X_END + HEADS, (TOK_X + TOK_HEAD + TOK_TAIL, START_AT))
ORDER_FULL = A12_TOK + place(MOE + MOE_END, (X_END + HEADS, X_AT), (TOK_HEAD + TOK_TAIL, NEXT_AT))
ORDER_LAST1 = A12_END + place(MOE + MOE_END, (X_END + HEADS, X_AT))
ORDER_END = A2 + Y_MID + MOE + MOE_END


class Plan:

    JOBS = {"tok", "tokT", "qkv1", "proj", "qkv2", "wo", "router", "stack1", "stack2", "T1", "T2"}
    TURNS = {"turn1", "turn2", "turn3", "turn4", "turn5"}

    def __init__(self, order):
        order = sum(order, [])
        self.order, self.names = order, {s[0] for s in order}
        self.first = {}
        self.score, self.exp, self.job, self.used, self.output = {}, {}, {}, {}, {}
        ns = nk = nv = 0
        for at, s in enumerate(order):
            kind, i = s[0], s[1]
            self.first.setdefault(kind, at)
            if kind in ("S1", "S2"):
                self.score[s] = ns
                ns += 1
            if kind in ("E1", "E2"):
                self.exp[s] = nk
                assert nk < PT_RING or nk - PT_RING in self.used, "the ring of exponentials is too short"
                nk += 1
            if kind in ("V1", "V2"):
                nv += 1
                for e in [("E1", i, s[2])] if kind == "V1" else [("E2", i, h, s[2]) for h in range(NH)]:
                    self.used[self.exp[e]] = nv
                self.output[kind, i] = nv
            if kind in self.JOBS:
                self.job[kind, i] = len(self.job)
            if kind in self.TURNS:
                for p in range(2):
                    self.job[kind, p] = len(self.job)
        self.scores, self.exps = ns, nk

    def before(self, a, b):
        return a in self.first and (b not in self.first or self.first[a] < self.first[b])

    def count(self, step, among):
        return 1 + sum(self.before(a, step) for a in among if a != step)


CENTER, NORM_X, GAIN_X, SPLIT_X, SPLIT_Y = ("ln1a", "ln2a", "ln3a"), ("ln1b", "ln2b", "ln3b"), ("ln1c", "ln3c"), ("ln1c", "aosplit1"), ("ystart", "aosplit2", "rmsb")


def program(nc, A, out):
    ctx = ExitStack()
    with ctx:
        def sb(name, shape, dt=F32):
            return ctx.enter_context(nc.sbuf_tensor(name, shape, dt))

        sems = []

        def sem(name):
            s = ctx.enter_context(nc.semaphore(name))
            sems.append(s)
            return s

        bank = [ctx.enter_context(nc.psum_tensor(f"bank{i}", [P, 512], F32)) for i in range(8)]
        bankb = [b[:, :].bitcast(BF16) for b in bank]

        const = sb("const", [P, NCONST])
        ident = const[:, K_ID:K_ID + P]
        identb = sb("identb", [P, P], BF16)
        flipb = sb("flipb", [P, P], BF16)
        mask_s = sb("mask_s", [P, P], BF16)
        mask_t = sb("mask_t", [P, P], BF16)
        par = sb("par", [P, NPAR])
        scale = sb("scale", [P, 1])
        dft = sb("dft", [2 * NFREQ, PATCH])
        w_tok = sb("w_tok", [P, HALF, 2, C])
        wa_hi, wa_lo = sb("wa_hi", [P, 256], BF16), sb("wa_lo", [P, 256], BF16)
        wt_hi, wt_lo = sb("wt_hi", [P, NWT * P], BF16), sb("wt_lo", [P, NWT * P], BF16)
        w2s = sb("w2s", [P, NBLK * C])
        rel_hi, rel_lo = sb("rel_hi", [P, BIAS_W], BF16), sb("rel_lo", [P, BIAS_W], BF16)

        xs = sb("xs", [P, NPATCH, HALF, V])
        xpad = sb("xpad", [P, V])
        h_feat = sb("h_feat", [C, V, NPATCH])
        h0, xc, sq, hn = (sb(n, [P, NT, C]) for n in ("h0", "xc", "sq", "hn"))
        stat_x = sb("stat_x", [P, 8, NT])
        hl_x, ht_x = sb("hl_x", [P, NT, P], BF16), sb("ht_x", [P, TOK], BF16)
        qkv = sb("qkv", [P, NT, 192])
        ql = sb("ql", [P, NT, P], BF16)
        qb = sb("qb", [P, NT, C + 2], BF16)
        ka = sb("ka", [P, NT, P], BF16)
        kb = sb("kb", [P, NT, C + 2], BF16)
        qt, qm = sb("qt", [P, TOK], BF16), sb("qm", [P, TOK], BF16)
        kt1, kt2 = sb("kt1", [P, TOK], BF16), sb("kt2", [P, TOK], BF16)
        v1 = sb("v1", [P, NT, C + 1])
        xt, ao_x = qkv[:, :, 0:C], qkv[:, :, C:2 * C]

        h1, xl, x1, base, res = (sb(n, [P, NT, C]) for n in ("h1", "xl", "x1", "base", "res"))
        stat_y = sb("stat_y", [P, 8, NT])
        hl_y, ht_y = sb("hl_y", [P, NT, P], BF16), sb("ht_y", [P, TOK], BF16)
        ht_m = sb("ht_m", [P, TOK], BF16)
        qkv_y = sb("qkv_y", [P, NT, P])
        ao_y, hn_y = qkv_y[:, :, 0:C], qkv_y[:, :, C:2 * C]
        rope = sb("rope", [P, 2, NT, 96])
        fqb = sb("fqb", [P, NT, 4, FS], BF16)
        fkb = sb("fkb", [P, NT, 2, FS], BF16)
        fq, fqm = sb("fq", [P, 2, TOK], BF16), sb("fqm", [P, 2, TOK], BF16)
        fk = sb("fk", [P, 2, TOK], BF16)
        vf = sb("vf", [P, NT, NKV, 32])
        ot = sb("ot", [P, P])
        gate_l, gate_p, gate_e, gate_m, gate_w = (sb(n, [P, NT, NE]) for n in ("gate_l", "gate_p", "gate_e", "gate_m", "gate_w"))
        gate_s = sb("gate_s", [P, 6, NT])
        silu = sb("silu", [P, 3, CW])
        gated, gsum = sb("gated", [P, NE * C]), sb("gsum", [P, C])
        hid = sb("hid", [P, 2, NC, CW])

        pmax, pmax1 = sb("pmax", [P, 2, 4, 4]), sb("pmax1", [P, 2, 3])
        rmax1, rec1 = sb("rmax1", [P, NT]), sb("rec1", [P, 1])
        rmax = sb("rmax", [P, NT, 4])
        rec = sb("rec", [P, 4])
        pt = sb("pt", [P, PT_RING, 512])

        hidf = hid[:, :, :, :].rearrange("p s a b -> p (s a b)")
        w_raw = hidf[0:2 * NFREQ, 0:C * C].rearrange("p (o c) -> p o c", o=C)
        nat = hidf[:, C * C:C * C + NWT * P].rearrange("p (k c) -> p k c", k=NWT)
        ptf = pt[:, :, :].rearrange("p a b -> p (a b)")
        c2 = ptf[0:C, 0:ROWS]
        c2b = ptf[0:C, ROWS:ROWS + NBLK * P].rearrange("p (k c) -> p k c", k=NBLK)
        used = ROWS + NBLK * P
        rel = ptf[:, used:used + BIAS_W]
        w_a = ptf[:, used + BIAS_W:used + BIAS_W + 256]
        ext = nc.dram_tensor("bias_ext", (1, BIAS_LEN), F32, kind="Internal").ap()

        def par_b(off, n=C, tiles=NT, np_=P):
            return par[0:np_, off:off + n].unsqueeze(1).to_broadcast([np_, tiles, n])

        def per_token(ap, n):
            return ap.unsqueeze(2).to_broadcast([ap.shape[0], ap.shape[1], n])

        def load_x(sp, b, s):
            v = A["x"][b].rearrange("c (u j q) v -> j c u (q v)", j=2, q=HALF)
            for j in range(2):
                sp.dma_start(xs[64 * j:64 * j + 64, :, :, :].rearrange("p u q v -> p u (q v)"),
                             v[j]).then_inc(s, 16)
                sp.dma_start(xpad[64 * j:64 * j + 64, :], A["x"][b][:, TIME - 1, :]).then_inc(s, 16)

        s_const, s_w, s_par, s_nat, s_c2, s_ext = (sem(n) for n in (
            "s_const", "s_w", "s_par", "s_nat", "s_c2", "s_ext"))
        s_rel, s_cast, s_zero, s_c2b = sem("s_rel"), sem("s_cast"), sem("s_zero"), sem("s_c2b")
        s_tokw, s_tokc, s_trn, s_hi, s_lo, s_wa = (sem(n) for n in (
            "s_tokw", "s_tokc", "s_trn", "s_hi", "s_lo", "s_wa"))
        wt_banks = [range(a, min(a + 4, NWT)) for a in range(0, NWT, 4)]
        w2_banks = [range(a, min(a + 8, NBLK)) for a in range(0, NBLK, 8)]

        def nat_rows(k):
            return {W_QKV2: P, W_WO: C, W_ROUTER: NE}.get(k) or rows_of((k - W_ONE) % NC)

        s_txt, s_xload = sem("s_txt"), sem("s_xload")
        s_dve, s_pool = sem("s_dve"), sem("s_pool")
        s_job = sem("s_job")
        s_taken = [sem("s_taken0"), sem("s_taken1")]
        s_early = sem("s_early")
        s_cent, s_sq_x, s_sq_y = sem("s_cent"), sem("s_sq_x"), sem("s_sq_y")
        s_norm_x, s_rstd_x, s_gain_x, s_hi_x, s_hl_x, s_h0, s_h1, s_xl = (sem(n) for n in (
            "s_norm_x", "s_rstd_x", "s_gain_x", "s_hi_x", "s_hl_x", "s_h0", "s_h1", "s_xl"))
        s_norm_y, s_rstd_y, s_gain_y, s_hi_y, s_hl_y, s_base = (sem(n) for n in (
            "s_norm_y", "s_rstd_y", "s_gain_y", "s_hi_y", "s_hl_y", "s_base"))
        s_qk_hi, s_qk_lo, s_fqk_hi, s_fqk_lo = (sem(n) for n in ("s_qk_hi", "s_qk_lo", "s_fqk_hi", "s_fqk_lo"))
        s_rot, s_rope = sem("s_rot"), sem("s_rope")
        s_sc, s_red, s_st, s_exp, s_used = (sem(n) for n in ("s_sc", "s_red", "s_st", "s_exp", "s_used"))
        s_max1, s_mrow1, s_ao1 = (sem(n) for n in ("s_max1", "s_mrow1", "s_ao1"))
        s_max2, s_mrow2, s_ot, s_oT, s_ao2 = (sem(n) for n in ("s_max2", "s_mrow2", "s_ot", "s_oT", "s_ao2"))
        s_logit, s_gexp, s_ab, s_silu, s_u, s_w2, s_res = (sem(n) for n in (
            "s_logit", "s_gexp", "s_ab", "s_silu", "s_u", "s_w2", "s_res"))

        s_out = ctx.enter_context(nc.semaphore("s_out"))

        def chunk_cols(t):
            return t * CW, min((t + 1) * CW, TOK)

        def run_pass(plan, by, b_tok):
            has_tok, has_y, has_end = "tok" in plan.names, "up" in plan.names, "ln2a" in plan.names
            is_first, is_last = "fold" in plan.names, "ln2a" not in plan.names

            def taken(eng, name, k):
                n = plan.job[name, k]
                eng.wait_ge(s_taken[n % 2], n // 2 + 1)

            def job_bank(name, k):
                return 6 + plan.job[name, k] % 2

            with nc.Block() as block:
                @block.sync
                def _(sp):
                    if is_first:
                        wv = A["tok_w"].rearrange("o (f c) -> f o c", c=C)
                        sp.dma_start(dft[:, :], A["dft"]).then_inc(s_w, 16)
                        sp.dma_start(w_raw[:, :, :], wv).then_inc(s_w, 16)
                    if has_tok:
                        load_x(sp, b_tok, s_xload)
                        if has_end:
                            sp.wait_ge(s_h1, 1)
                        if is_first:
                            sp.wait_ge(s_zero, 1)
                        sp.dma_start(h0[0:TXT, FULL, :], A["txt"][b_tok]).then_inc(s_txt, 16)
                    if is_first:
                        for off, name, n in ((G1, "ln1_g", C), (B1, "ln1_b", C), (BQKV, "qkv_b", 192), (BPROJ, "proj_b", C),
                                             (G2, "ln2_g", C), (B2, "ln2_b", C), (FW1, "f_ln1", C), (FW2, "f_ln2", C)):
                            sp.dma_start(par[:, off:off + n], A[name].to_broadcast([P, n])).then_inc(s_par, 16)
                        sp.dma_start(scale[:, :], A["attn_scale"].to_broadcast([P, 1])).then_inc(s_par, 16)
                        tab = A["bias_table"]
                        sp.dma_start(ext[:, 0:BIAS_PAD], tab[:, 0:BIAS_PAD]).then_inc(s_ext, 16)
                        sp.dma_start(ext[:, BIAS_PAD:BIAS_PAD + SPAN], tab).then_inc(s_ext, 16)
                        tail = BIAS_LEN - BIAS_PAD - SPAN
                        sp.dma_start(ext[:, BIAS_PAD + SPAN:].unsqueeze(2),
                                     tab[:, SPAN - 1:SPAN].unsqueeze(1).to_broadcast([1, tail, 1])).then_inc(s_ext, 16)
                        sp.wait_ge(s_ext, 48)
                        sp.dma_start(rel[:, :], bass.AP(ext.tensor, 0, [[1, P], [1, BIAS_W]])).then_inc(s_rel, 16)
                    if has_y:
                        sp.wait_ge(s_res, 6)
                        sp.dma_start(out[by][0:6 * P, :].rearrange("(i p) c -> p i c", p=P), res[:, 0:6, :]).then_inc(s_out, 16)
                        sp.wait_ge(s_res, NT)
                        sp.dma_start(out[by][6 * P:FULL * P, :].rearrange("(i p) c -> p i c", p=P), res[:, 6:FULL, :]).then_inc(s_out, 16)
                        sp.dma_start(out[by][FULL * P:, :], res[0:REST, FULL, :]).then_inc(s_out, 16)
                        if is_last:
                            sp.wait_ge(s_out, 48)

                @block.tensor
                def _(pe):
                    def job(name, k):
                        n = plan.job[name, k]
                        if n >= 2:
                            pe.wait_ge(s_taken[n % 2], n // 2)
                        return bank[6 + n % 2], bankb[6 + n % 2]

                    def fold(_):
                        pe.wait_ge(s_w, 32)
                        for o in range(0, C, 2):
                            last = nc.tensor.matmul(bank[4][:, o // 2 * PATCH:(o // 2 + 1) * PATCH],
                                                    w_raw[:, o:o + 2, :].rearrange("f o c -> f (o c)"), dft[:, :],
                                                    start=True, stop=True)
                        last.then_inc(s_tokw, 1)

                    def weights(n):
                        if n == 0:
                            pe.wait_ge(s_const, 16)
                            pe.wait_ge(s_nat, 16 * 24)
                        if n >= 4:
                            pe.wait_ge(s_lo, n - 3)
                        for k in wt_banks[n]:
                            r = nat_rows(k)
                            last = nc.tensor.transpose(bank[n % 4][:, (k % 4) * P:(k % 4) * P + r], nat[0:r, k, :], ident[0:r, 0:r])
                        last.then_inc(s_trn, 1)

                    def w2_weights(n):
                        pe.wait_ge(s_c2b, 1)
                        for k in w2_banks[n]:
                            last = nc.tensor.transpose(bank[3 + n][:, (k % 8) * C:(k % 8 + 1) * C], c2b[:, k, :], ident[0:C, 0:C])
                        last.then_inc(s_trn, 1)

                    def tok(g):
                        if g == 0:
                            pe.wait_ge(s_xload, 64)
                            if is_first:
                                pe.wait_ge(s_tokc, 1)
                        o, _ = job("tok", g)
                        for q in range(HALF):
                            dst = o[:, :].rearrange("p (u v) -> p u v", v=V) if g < 2 else o[:, 0:V]
                            src = xs[:, 8 * g:8 * g + 8, q, :] if g < 2 else xpad[:, :]
                            last = nc.tensor.matmul(dst, w_tok[:, q, :, :].rearrange("p l o -> p (l o)"), src,
                                                    start=(q == 0), stop=(q == HALF - 1))
                        last.then_inc(s_job, 1)

                    def tokT(_):
                        for g in range(3):
                            taken(pe, "tok", g)
                        o, _ = job("tokT", 0)
                        hf = h_feat[:, :, :].rearrange("c v n -> c (v n)")
                        for i in range(FULL):
                            last = nc.tensor.transpose(o[:, C * i:C * i + C], hf[:, P * i:P * i + P], ident[0:C, 0:C])
                        last.then_inc(s_job, 1)

                    def turn(name, hl, s_hl, n):
                        pe.wait_ge(s_hl, n)
                        for part, tiles in enumerate(PARTS):
                            _, o = job(name, part)
                            for k, i in enumerate(tiles):
                                w = tokens(i)
                                last = nc.tensor.transpose(o[:, P * k:P * k + w], hl[0:w, i, :], identb[0:w, 0:w])
                            last.then_inc(s_job, 1)

                    def project(name, k, tiles, turned, ht, w_hi, w_lo, cols):
                        for part in range(2):
                            taken(pe, turned, part)
                        if is_first and k == 0:
                            pe.wait_ge(s_cast, 2)
                        o, _ = job(name, k)
                        for n, i in enumerate(tiles):
                            w = tokens(i)
                            dst = o[0:w, n * cols:(n + 1) * cols]
                            nc.tensor.matmul(dst, ht[:, P * i:P * i + w], w_hi, start=True, stop=False)
                            last = nc.tensor.matmul(dst, ht[:, P * i:P * i + w], w_lo, start=False, stop=True)
                        last.then_inc(s_job, 1)

                    def stack(name, k, src, rows):
                        _, o = job(name, k)
                        for n, i in enumerate(PARTS[k % 2]):
                            w = tokens(i)
                            last = nc.tensor.transpose(o[0:rows, P * n:P * n + w], src(i)[0:w], identb[0:w, 0:w])
                        last.then_inc(s_job, 1)

                    def stack1(k):
                        pe.wait_ge(s_qk_hi, 2)
                        pe.wait_ge(s_qk_lo, 1)
                        src, rows = ((ql, P), (ka, P), (kb, C + 2))[k // 2]
                        stack("stack1", k, lambda i: src[:, i, :], rows)

                    def stack2(k):
                        pe.wait_ge(s_fqk_hi, 2)
                        pe.wait_ge(s_fqk_lo, 1)
                        src = (fqb[:, :, 0:2, :], fqb[:, :, 2:4, :], fkb[:, :, :, :])[k // 2]
                        stack("stack2", k, lambda i: src[:, i, :, :].rearrange("p h c -> p (h c)"), P)

                    def score_bank(g):
                        if g >= 2:
                            pe.wait_ge(s_red, g - 1)
                        return bank[g % 2]

                    def exp_bank(g):
                        if g >= 2:
                            pe.wait_ge(s_exp, g - 1)
                        return bank[2 + g % 2]

                    def S1(i, n):
                        if i == n == 0 and plan.before("stack1", "S1"):
                            for k in range(6):
                                taken(pe, "stack1", k)
                        w, q0, (k0, k1) = tokens(i), P * i, A1_S[n]
                        dst = score_bank(plan.score["S1", i, n])
                        bend = min(k1, q0 + w)
                        nc.tensor.matmul(dst[0:w, 0:k1 - k0], qt[:, q0:q0 + w], kt1[:, k0:k1], start=True, stop=False)
                        last = nc.tensor.matmul(dst[0:w, 0:k1 - k0], qt[0:C, q0:q0 + w], kt2[0:C, k0:k1],
                                                start=False, stop=(bend <= k0))
                        if bend > k0:
                            y = BIAS_W - P - q0 + k0
                            for r in (rel_hi, rel_lo):
                                last = nc.tensor.matmul(dst[0:w, 0:bend - k0], flipb[:, 0:w], r[:, y:y + bend - k0],
                                                        start=False, stop=(r is rel_lo))
                        last.then_inc(s_sc, 1)

                    def T1(i):
                        pe.wait_ge(s_mrow1, i + 1)
                        (_, o), w = job("T1", i), tokens(i)
                        nc.tensor.transpose(o[0:C + 2, 0:w], qb[0:w, i, :], identb[0:w, 0:w]).then_inc(s_job, 1)

                    def E1(i, n):
                        taken(pe, "T1", i)
                        w, q0, dst = tokens(i), P * i, exp_bank(plan.exp["E1", i, n])
                        for jj, j in enumerate(a1_k(i)[n]):
                            kw, o = tokens(j), dst[0:tokens(j), w * jj:w * jj + w]
                            nc.tensor.matmul(o, kt1[:, P * j:P * j + kw], qt[:, q0:q0 + w], start=True, stop=False)
                            last = nc.tensor.matmul(o, kt2[:, P * j:P * j + kw], qm[:, q0:q0 + w],
                                                    start=False, stop=(j > i))
                            if j <= i:
                                y = BIAS_W - P - P * (i - j)
                                for r in (rel_hi, rel_lo):
                                    last = nc.tensor.matmul(o, r[:, y:y + kw], flipb[:, 0:w], start=False, stop=(r is rel_lo))
                        last.then_inc(s_st, 1)

                    def V1(i, n):
                        if i >= 1 and n == 0:
                            pe.wait_ge(s_ao1, i)
                        w, g = tokens(i), plan.exp["E1", i, n]
                        pe.wait_ge(s_exp, g + 1)
                        for jj, j in enumerate(a1_k(i)[n]):
                            kw = tokens(j)
                            last = nc.tensor.matmul(bank[5][0:w, 0:C + 1], pt[0:kw, g % PT_RING, w * jj:w * jj + w],
                                                    v1[0:kw, j, :], start=(j == 0), stop=(j == NT - 1))
                        last.then_inc(s_used, 1)

                    def wt(w, k, n):
                        return w[:, k * P:k * P + n]

                    def S2(i, h, n):
                        if PLACE[i] == h == n == 0 and plan.before("stack2", "S2"):
                            for k in range(6):
                                taken(pe, "stack2", k)
                        w, q0, (k0, k1) = tokens(i), P * i, a2_s(i)[n]
                        dst, diag = score_bank(plan.score["S2", i, h, n]), n == len(a2_s(i)) - 1
                        last = nc.tensor.matmul(dst[0:w, 0:k1 - k0], fq[:, h // 2, q0:q0 + w], fk[:, h % 2, k0:k1],
                                                start=True, stop=not diag)
                        if diag:
                            last = nc.tensor.matmul(dst[0:w, q0 - k0:q0 - k0 + w], identb[0:w, 0:w], mask_s[0:w, 0:w],
                                                    start=False, stop=True)
                        last.then_inc(s_sc, 1)

                    def T2(i):
                        pe.wait_ge(s_mrow2, PLACE[i] + 1)
                        (_, o), w = job("T2", i), tokens(i)
                        for pr in range(2):
                            last = nc.tensor.transpose(o[:, P * pr:P * pr + w],
                                                       fqb[0:w, i, 2 * pr:2 * pr + 2, :].rearrange("p h c -> p (h c)"),
                                                       identb[0:w, 0:w])
                        last.then_inc(s_job, 1)

                    def E2(i, h, n):
                        taken(pe, "T2", i)
                        w, q0, dst = tokens(i), P * i, exp_bank(plan.exp["E2", i, h, n])
                        for jj, j in enumerate(a2_k(i)[n]):
                            kw, o = tokens(j), dst[0:tokens(j), w * jj:w * jj + w]
                            last = nc.tensor.matmul(o, fk[:, h % 2, P * j:P * j + kw], fqm[:, h // 2, q0:q0 + w],
                                                    start=True, stop=(j < i))
                            if j == i:
                                last = nc.tensor.matmul(o, identb[0:kw, 0:kw], mask_t[0:kw, 0:w], start=False, stop=True)
                        last.then_inc(s_st, 1)

                    def V2(i, n):
                        if PLACE[i] >= 1 and n == 0:
                            pe.wait_ge(s_ao2, PLACE[i])
                        pe.wait_ge(s_exp, plan.exp["E2", i, NH - 1, n] + 1)
                        w = tokens(i)
                        for jj, j in enumerate(a2_k(i)[n]):
                            kw = tokens(j)
                            for h in range(NH):
                                g = plan.exp["E2", i, h, n]
                                last = nc.tensor.matmul(bank[4][32 * h:32 * h + 32, 0:w], vf[0:kw, j, h % 2, :],
                                                        pt[0:kw, g % PT_RING, w * jj:w * jj + w],
                                                        start=(j == 0), stop=(j == i))
                        last.then_inc(s_used, 1)

                    def X2(i):
                        pe.wait_ge(s_ot, PLACE[i] + 1)
                        w = tokens(i)
                        nc.tensor.transpose(bank[4][0:w, P:2 * P], ot[:, 0:w], ident[:, :]).then_inc(s_oT, 1)

                    def router(_):
                        for part in range(2):
                            taken(pe, "turn5", part)
                        o, _ = job("router", 0)
                        for i in range(NT):
                            w = tokens(i)
                            for wgt in (wt_hi, wt_lo):
                                last = nc.tensor.matmul(o[0:w, NE * i:NE * i + NE], ht_m[:, P * i:P * i + w],
                                                        wt(wgt, W_ROUTER, NE), start=(wgt is wt_hi), stop=(wgt is wt_lo))
                        last.then_inc(s_job, 1)

                    def up(t, c):
                        n, (a, z), r = t * NC + c, chunk_cols(t), rows_of(c)
                        if n == 0:
                            pe.wait_ge(s_red, plan.scores)
                            pe.wait_ge(s_exp, plan.exps)
                        if n == 2:
                            pe.wait_ge(s_ao2, NT)
                            if "S1" in plan.names:
                                pe.wait_ge(s_ao1, NT)
                        last_use = max((m for m in range(n) if pair(m) == pair(n)), default=None)
                        if last_use is not None:
                            pe.wait_ge(s_u, last_use + 1)
                        for k, first in ((0, W_ONE), (1, W_THREE)):
                            dst = bank[2 * pair(n) + k][0:r, 0:z - a]
                            nc.tensor.matmul(dst, wt(wt_hi, first + c, r), ht_m[:, a:z], start=True, stop=False)
                            last = nc.tensor.matmul(dst, wt(wt_lo, first + c, r), ht_m[:, a:z], start=False, stop=True)
                        last.then_inc(s_ab, 1)
                        if t >= 1:
                            for m in range(3 * c, 3 * c + 3):
                                down_piece(t - 1, m)

                    def down_piece(t, m):
                        i, (c, e0, ne, blk) = CHUNK_TILES * t + m // NC, W2B[m % NC]
                        w, dst, r = tokens(i), bank[4 + i % 2], rows_of(c)
                        if m == 0:
                            pe.wait_ge(s_u, (t + 1) * NC)
                        if c == 0:
                            if i >= 2:
                                pe.wait_ge(s_res, i - 1)
                        q0 = P * (i % CHUNK_TILES)
                        last = nc.tensor.matmul(dst[0:w, C * e0:C * (e0 + ne)], hid[0:r, t % 2, c, q0:q0 + w],
                                                w2s[0:r, C * blk:C * (blk + ne)], start=(c == 0), stop=(c == NC - 1),
                                                skip_group_check=True)
                        if c == NC - 1:
                            last.then_inc(s_w2, 1)

                    steps = {
                        "fold": fold, "wt": weights, "w2": w2_weights,
                        "tok": tok, "tokT": tokT, "stack1": stack1, "stack2": stack2, "S1": S1, "T1": T1, "E1": E1, "V1": V1,
                        "S2": S2, "T2": T2, "E2": E2, "V2": V2, "X2": X2,
                        "router": router, "up": up, "down": lambda m: down_piece(2, m),
                        "turn1": lambda _: turn("turn1", hl_x, s_hl_x, plan.count("ln1c", SPLIT_X)),
                        "turn2": lambda _: turn("turn2", hl_x, s_hl_x, plan.count("aosplit1", SPLIT_X)),
                        "turn3": lambda _: turn("turn3", hl_y, s_hl_y, plan.count("ystart", SPLIT_Y)),
                        "turn4": lambda _: turn("turn4", hl_y, s_hl_y, plan.count("aosplit2", SPLIT_Y)),
                        "turn5": lambda _: turn("turn5", hl_y, s_hl_y, plan.count("rmsb", SPLIT_Y)),
                        "qkv1": lambda k: project("qkv1", k, range(2 * k, min(2 * k + 2, NT)), "turn1", ht_x,
                                                  wa_hi[:, 0:192], wa_lo[:, 0:192], 192),
                        "proj": lambda k: project("proj", k, (range(FULL), [FULL])[k], "turn2", ht_x,
                                                  wa_hi[:, 192:256], wa_lo[:, 192:256], C),
                        "qkv2": lambda k: project("qkv2", k, range(4 * k, min(4 * k + 4, NT)), "turn3", ht_y,
                                                  wt(wt_hi, W_QKV2, P), wt(wt_lo, W_QKV2, P), P),
                        "wo": lambda k: project("wo", k, (range(FULL), [FULL])[k], "turn4", ht_y,
                                                wt(wt_hi, W_WO, C), wt(wt_lo, W_WO, C), C),
                    }
                    for s in plan.order:
                        if s[0] in steps:
                            steps[s[0]](*s[1:])

                @block.scalar
                def _(act):
                    def job(name, k):
                        n = plan.job[name, k]
                        act.wait_ge(s_job, n + 1)
                        return bank[6 + n % 2], bankb[6 + n % 2], s_taken[n % 2]

                    def load_weights():
                        act.dma_start(const[:, :], A["const"]).then_inc(s_const, 16)
                        for d in range(2):
                            act.dma_start(w_a[64 * d:64 * d + 64, 0:192], A["qkv_w"]).then_inc(s_wa, 16)
                            act.dma_start(w_a[64 * d:64 * d + 64, 192:256], A["proj_w"]).then_inc(s_wa, 16)
                        act.dma_start(c2[:, :].rearrange("c (e h) -> c e h", e=NE), A["w2"].rearrange("e c h -> c e h")).then_inc(s_c2, 16)
                        for d in range(2):
                            cols = slice(64 * d, 64 * d + 64)
                            for h in range(NH):
                                slot = (h % 2) * 2 + h // 2
                                act.dma_start(nat[HD * slot:HD * slot + HD, W_QKV2, cols], A["wq"][HD * h:HD * h + HD, :]).then_inc(s_nat, 16)
                            act.dma_start(nat[64:96, W_QKV2, cols], A["wk"]).then_inc(s_nat, 16)
                            act.dma_start(nat[96:128, W_QKV2, cols], A["wv"]).then_inc(s_nat, 16)
                            act.dma_start(nat[0:C, W_WO, cols], A["wo"]).then_inc(s_nat, 16)
                            act.dma_start(nat[0:NE, W_ROUTER, cols], A["router_w"]).then_inc(s_nat, 16)
                            for first, name in ((W_ONE, "w1"), (W_THREE, "w3")):
                                w = A[name].rearrange("e h c -> (e h) c")
                                act.dma_start(nat[:, first:first + NC - 1, cols],
                                              w[0:(NC - 1) * P, :].rearrange("(k p) c -> p k c", p=P)).then_inc(s_nat, 16)
                                act.dma_start(nat[0:rows_of(NC - 1), first + NC - 1, cols],
                                              w[(NC - 1) * P:, :]).then_inc(s_nat, 16)

                    def weights(n):
                        act.wait_ge(s_trn, n + 1)
                        for k in wt_banks[n]:
                            r = nat_rows(k)
                            last = nc.scalar.copy(wt_hi[:, k * P:k * P + r], bank[n % 4][:, (k % 4) * P:(k % 4) * P + r])
                        last.then_inc(s_hi, 1)

                    def tokT(_):
                        o, _, s = job("tokT", 0)
                        if has_end:
                            act.wait_ge(s_h1, 1)
                        nc.scalar.copy(h0[:, 0:FULL, :], o[:, :].rearrange("p (i c) -> p i c", c=C)).then_inc(s, 1)

                    def tok(g):
                        if g < 2:
                            o, _, _ = job("tok", g)
                            nc.scalar.copy(h_feat[:, :, 8 * g:8 * g + 8],
                                           o[0:C, :].rearrange("p (u v) -> p v u", v=V)).then_inc(s_early, 1)

                    def hi(src, ready, n, hl, s_hi):
                        if ready is not None:
                            act.wait_ge(ready, n)
                        nc.scalar.copy(hl[:, :, 0:C], src[:, :, :]).then_inc(s_hi, 1)

                    def turn(name, ht):
                        for part, tiles in enumerate(PARTS):
                            _, o, s = job(name, part)
                            c0, n = P * tiles[0], sum(tokens(i) for i in tiles)
                            nc.scalar.copy(ht[:, c0:c0 + n], o[:, 0:n]).then_inc(s, 1)

                    def square(src, ready, n, s):
                        act.wait_ge(ready, n)
                        nc.scalar.activation(sq[:, :, :], src[:, :, :], ACT.Square).then_inc(s, 1)

                    def square_y(_):
                        for k in range(2):
                            taken(act, "wo", k)
                        nc.scalar.activation(sq[:, :, :], x1[:, :, :], ACT.Square).then_inc(s_sq_y, 1)

                    def split1(_):
                        for k in range(5):
                            taken(act, "qkv1", k)
                        nc.scalar.copy(ql[:, :, 0:C], qkv[:, :, 0:C])
                        nc.scalar.copy(ka[:, :, 0:C], qkv[:, :, C:2 * C]).then_inc(s_qk_hi, 1)
                        nc.scalar.copy(qb[:, :, 0:C], qkv[:, :, 0:C])
                        nc.scalar.copy(ka[:, :, C:2 * C], qkv[:, :, C:2 * C])
                        nc.scalar.copy(v1[:, 0:FULL, 0:C], qkv[:, 0:FULL, 2 * C:3 * C])
                        nc.scalar.copy(v1[0:REST, FULL, 0:C], qkv[0:REST, FULL, 2 * C:3 * C]).then_inc(s_qk_hi, 1)

                    def take(name, k, dst, rows):
                        _, o, s = job(name, k)
                        c0, n = P * PARTS[k % 2][0], sum(tokens(i) for i in PARTS[k % 2])
                        nc.scalar.copy(dst[0:rows, c0:c0 + n], o[0:rows, 0:n]).then_inc(s, 1)

                    def stack1(k):
                        take("stack1", k, (qt, kt1, kt2)[k // 2], (P, P, C + 2)[k // 2])

                    def qkv2(k):
                        o, _, s = job("qkv2", k)
                        if k < 2:
                            nc.scalar.copy(qkv_y[:, 4 * k:4 * k + 4, :], o[:, :].rearrange("p (i n) -> p i n", n=P)).then_inc(s, 1)
                        else:
                            nc.scalar.copy(qkv_y[0:REST, FULL, :], o[0:REST, 0:P]).then_inc(s, 1)

                    def split2(_):
                        act.wait_ge(s_rope, 1)
                        rq = rope[:, 0, :, 0:64].rearrange("p t (h c) -> p t h c", c=HD)
                        rk = rope[:, 0, :, 64:96].rearrange("p t (h c) -> p t h c", c=HD)
                        nc.scalar.copy(fqb[:, :, :, 0:HD], rq)
                        nc.scalar.copy(fkb[:, :, :, 0:HD], rk).then_inc(s_fqk_hi, 1)
                        nc.scalar.copy(fqb[:, :, :, 2 * HD:3 * HD], rq)
                        nc.scalar.copy(fkb[:, :, :, HD:2 * HD], rk)
                        for k in range(3):
                            taken(act, "qkv2", k)
                        vv = qkv_y[:, :, 96:128].rearrange("p t (g c) -> p t g c", g=NKV)
                        nc.scalar.copy(vf[:, 0:FULL, :, 0:HD], vv[:, 0:FULL, :, :])
                        nc.scalar.copy(vf[0:REST, FULL, :, 0:HD], vv[0:REST, FULL, :, :]).then_inc(s_fqk_hi, 1)

                    def stack2(k):
                        if k < 4:
                            take("stack2", k, fq[:, k // 2, :], P)

                    def exponents(g, keys, w, scale_):
                        if g >= PT_RING:
                            act.wait_ge(s_used, plan.used[g - PT_RING])
                        act.wait_ge(s_st, g + 1)
                        kw, m = tokens(keys[-1]), len(keys)
                        nc.scalar.activation(pt[0:kw, g % PT_RING, 0:m * w], bank[2 + g % 2][0:kw, 0:m * w], ACT.Exp,
                                             scale=scale_).then_inc(s_exp, 1)

                    def T1(i):
                        w = tokens(i)
                        _, o, s = job("T1", i)
                        nc.scalar.copy(qm[0:C + 2, P * i:P * i + w], o[0:C + 2, 0:w]).then_inc(s, 1)

                    def T2(i):
                        w = tokens(i)
                        _, o, s = job("T2", i)
                        nc.scalar.copy(fqm[:, :, P * i:P * i + w],
                                       o[:, 0:2 * P].rearrange("p (r q) -> p r q", q=P)[:, :, 0:w]).then_inc(s, 1)

                    def V2(i, n):
                        if n < len(a2_k(i)) - 1:
                            return
                        w = tokens(i)
                        act.wait_ge(s_used, plan.output["V2", i])
                        if PLACE[i] >= 1:
                            act.wait_ge(s_oT, PLACE[i])
                        nc.scalar.copy(ot[:, 0:w], bank[4][:, 0:w]).then_inc(s_ot, 1)

                    def router(_):
                        act.wait_ge(s_logit, 3)
                        nc.scalar.activation(gate_e[:, :, :], gate_l[:, :, :], ACT.Exp).then_inc(s_gexp, 1)

                    def up(t, c):
                        n, r, (a, z) = t * NC + c, rows_of(c), chunk_cols(t)
                        act.wait_ge(s_ab, n + 1)
                        if n >= 3:
                            act.wait_ge(s_u, n - 2)
                        nc.scalar.activation(silu[0:r, n % 3, 0:z - a], bank[2 * pair(n)][0:r, 0:z - a],
                                             ACT.Silu).then_inc(s_silu, 1)

                    steps = {
                        "tok": tok, "tokT": tokT, "split1": split1, "stack1": stack1, "qkv2": qkv2, "split2": split2, "stack2": stack2,
                        "T1": T1, "T2": T2, "V2": V2, "router": router, "up": up,
                        "wt": weights, "rmsa": square_y,
                        "ln1b": lambda _: square(xc, s_cent, plan.count("ln1a", CENTER), s_sq_x),
                        "ln2b": lambda _: square(xc, s_cent, plan.count("ln2a", CENTER), s_sq_x),
                        "ln3b": lambda _: square(xc, s_cent, plan.count("ln3a", CENTER), s_sq_x),
                        "ln1c": lambda _: hi(hn, s_gain_x, plan.count("ln1c", GAIN_X), hl_x, s_hi_x),
                        "aosplit1": lambda _: hi(ao_x, s_ao1, NT, hl_x, s_hi_x),
                        "ystart": lambda _: hi(hn, s_gain_x, plan.count("ln3c", GAIN_X), hl_y, s_hi_y),
                        "aosplit2": lambda _: hi(ao_y, s_ao2, NT, hl_y, s_hi_y),
                        "rmsb": lambda _: hi(hn_y, s_gain_y, 1, hl_y, s_hi_y),
                        "turn1": lambda _: turn("turn1", ht_x), "turn2": lambda _: turn("turn2", ht_x),
                        "turn3": lambda _: turn("turn3", ht_y), "turn4": lambda _: turn("turn4", ht_y),
                        "turn5": lambda _: turn("turn5", ht_m),
                        "E1": lambda i, n: exponents(plan.exp["E1", i, n], a1_k(i)[n], tokens(i), 1.0),
                        "E2": lambda i, h, n: exponents(plan.exp["E2", i, h, n], a2_k(i)[n], tokens(i), float(HD) ** -0.5),
                    }
                    if is_first:
                        load_weights()
                    for s in plan.order:
                        if s[0] in steps:
                            steps[s[0]](*s[1:])

                @block.gpsimd
                def _(pool):
                    count = [0]

                    def link(ins):
                        count[0] += 1
                        ins.then_inc(s_pool, 1)
                        pool.wait_ge(s_pool, count[0])

                    def rstd(stat, k, n, dst):
                        half = const[:, K_HALF:K_HALF + 1].unsqueeze(1).to_broadcast([P, n, NT])
                        return nc.gpsimd.tensor_tensor(stat[:, dst:dst + n, :], stat[:, k:k + n, :], half, ALU.pow)

                    def set_up():
                        for t in (h0, x1, qkv, qkv_y, gate_l, qb):
                            last = nc.gpsimd.memset(t[:, FULL, :], 0.0)
                        last.then_inc(s_zero, 1)
                        nc.gpsimd.memset(fk[:, :, :], 0.0)
                        for t in (qm, kt2):
                            nc.gpsimd.memset(t[:, :], 0.0)
                        nc.gpsimd.memset(fqb[:, :, :, :], 0.0)
                        both = ((kb[:, :, :], C), (fkb[:, :, :, :].rearrange("p t g c -> p (t g) c"), 3 * HD))
                        for v, at in both:
                            nc.gpsimd.memset(v, 0.0).then_inc(s_zero, 1)
                        pool.wait_ge(s_zero, 3)
                        for v, at in both:
                            nc.gpsimd.memset(v[:, :, at:at + 1], 1.0)
                            nc.gpsimd.memset(v[:, :, at + 1:at + 2], -1.0)
                        nc.gpsimd.memset(v1[:, :, C:C + 1], 1.0)
                        nc.gpsimd.memset(vf[:, :, :, HD:HD + 1], 1.0)
                        nc.gpsimd.memset(vf[:, :, :, HD + 1:32], 0.0)
                        nc.gpsimd.memset(c2b[:, :, :], 0.0).then_inc(s_zero, 1)

                    def w2_blocks_(_):
                        pool.wait_ge(s_zero, 4)
                        pool.wait_ge(s_c2, 16)
                        for c, e0, ne, blk in W2B:
                            for e in range(e0, e0 + ne):
                                a, z = max(c * P, e * HID), min(c * P + rows_of(c), (e + 1) * HID)
                                last = nc.gpsimd.tensor_copy(c2b[:, blk + e - e0, a - c * P:z - c * P], c2[:, a:z])
                        last.then_inc(s_c2b, 1)

                    def max_row(mx, hi_, lo_, s_mrow):
                        link(nc.gpsimd.tensor_scalar(hi_, mx, -1.0, None, ALU.mult))
                        nc.gpsimd.tensor_tensor(lo_, mx, hi_, ALU.add).then_inc(s_mrow, 1)

                    def S1(i, n):
                        if n == len(A1_S) - 1:
                            w = tokens(i)
                            pool.wait_ge(s_max1, i + 1)
                            max_row(rmax1[0:w, i:i + 1], qb[0:w, i, C:C + 1], qb[0:w, i, C + 1:C + 2], s_mrow1)

                    def S2(i, h, n):
                        if h == NH - 1 and n == len(a2_s(i)) - 1:
                            w, m = tokens(i), 3 * HD
                            pool.wait_ge(s_max2, PLACE[i] + 1)
                            max_row(rmax[0:w, i, :], fqb[0:w, i, :, m], fqb[0:w, i, :, m + 1], s_mrow2)

                    def ln1b(_):
                        if is_first:
                            pool.wait_ge(s_const, 16)
                        if plan.before("ystart", "ln1b"):
                            pool.wait_ge(s_hl_y, plan.count("ystart", SPLIT_Y))
                        gain("ln1a", G1)
                        pool.wait_ge(s_norm_x, plan.count("ln1b", NORM_X))
                        rstd(stat_x, 3, 1, 6).then_inc(s_rstd_x, 1)

                    def gain(name, off):
                        pool.wait_ge(s_cent, plan.count(name, CENTER))
                        nc.gpsimd.tensor_tensor(hn[:, :, :], xc[:, :, :], par_b(off), ALU.mult)

                    def proj(k):
                        t, w = (slice(0, FULL), P) if k == 0 else (slice(FULL, NT), REST)
                        nc.gpsimd.tensor_tensor(h0[0:w, t, :], h0[0:w, t, :], par_b(B2, C, t.stop - t.start, w), ALU.add).then_inc(s_h0, 1)

                    def ln2b(_):
                        gain("ln2a", G2)
                        pool.wait_ge(s_norm_x, plan.count("ln2b", NORM_X))
                        rstd(stat_x, 3, 1, 6).then_inc(s_rstd_x, 1)

                    def ln3b(_):
                        gain("ln3a", FW1)
                        pool.wait_ge(s_norm_x, plan.count("ln3b", NORM_X))
                        rstd(stat_x, 5, 1, 7).then_inc(s_rstd_x, 1)
                        link(rstd(stat_x, 3, 1, 6))
                        nc.gpsimd.tensor_tensor(xl[:, :, :], xc[:, :, :], per_token(stat_x[:, 6, :], C), ALU.mult).then_inc(s_xl, 1)

                    def rope_(_):
                        for k in range(3):
                            taken(pool, "qkv2", k)
                        nc.gpsimd.memset(fqb[:, :, :, 3 * HD:3 * HD + 2], 0.0)
                        qk = qkv_y[:, :, 0:96].rearrange("p t (h c) -> p t h c", c=HD)
                        rot = rope[:, 1, :, :].rearrange("p t (h c) -> p t h c", c=HD)
                        sin = const[:, K_SIN:K_SIN + NT * HD].rearrange("p (t c) -> p t c", c=HD)
                        for a, z in ((0, HD // 2), (HD // 2, HD)):
                            o = HD // 2 - a
                            last = nc.gpsimd.tensor_tensor(rot[:, :, :, a:z], qk[:, :, :, o:o + HD // 2],
                                                           sin[:, :, a:z].unsqueeze(2).to_broadcast([P, NT, 6, HD // 2]), ALU.mult)
                        last.then_inc(s_rot, 1)

                    def rmsa(_):
                        for k in range(2):
                            taken(pool, "wo", k)
                        nc.gpsimd.tensor_tensor(hn_y[:, :, :], x1[:, :, :], par_b(FW2), ALU.mult)
                        pool.wait_ge(s_norm_y, 1)
                        rstd(stat_y, 3, 1, 6).then_inc(s_rstd_y, 1)
                        pool.wait_ge(s_out, 48)
                        nc.gpsimd.sem_clear(range(s_out.num, s_out.num + 1))
                        nc.gpsimd.tensor_tensor(base[:, :, :], h1[:, :, :], x1[:, :, :], ALU.add).then_inc(s_base, 1)

                    steps = {
                        "ln1b": ln1b, "ln2b": ln2b, "ln3b": ln3b, "rope": rope_, "rmsa": rmsa,
                        "proj": proj, "w2blocks": w2_blocks_, "S1": S1, "S2": S2,
                    }
                    if is_first:
                        set_up()
                        nc.gpsimd.memset(gsum[:, :], 0.0).then_inc(s_out, 48)
                    for s in plan.order:
                        if s[0] in steps:
                            steps[s[0]](*s[1:])

                @block.vector
                def _(dve):
                    count = [0]

                    def link(ins):
                        count[0] += 1
                        ins.then_inc(s_dve, 1)
                        dve.wait_ge(s_dve, count[0])

                    def job(name, k):
                        n = plan.job[name, k]
                        dve.wait_ge(s_job, n + 1)
                        return bank[6 + n % 2], bankb[6 + n % 2], s_taken[n % 2]

                    def center(src):
                        link(nc.vector.tensor_reduce(stat_x[:, 0, :], src[:, :, :], AX.X, ALU.add))
                        link(nc.vector.tensor_scalar(stat_x[:, 1, :], stat_x[:, 0, :], 1.0 / C, None, ALU.mult))
                        nc.vector.tensor_tensor(xc[:, :, :], src[:, :, :], per_token(stat_x[:, 1, :], C), ALU.subtract).then_inc(s_cent, 1)

                    def mean_square(stat, ready, n):
                        dve.wait_ge(ready, n)
                        link(nc.vector.tensor_reduce(stat[:, 0, :], sq[:, :, :], AX.X, ALU.add))
                        link(nc.vector.tensor_scalar(stat[:, 2, :], stat[:, 0, :], 1.0 / C, None, ALU.mult))

                    def lo(src, hl, s_hi, n, s_hl):
                        dve.wait_ge(s_hi, n)
                        nc.vector.tensor_tensor(hl[:, :, C:P], src[:, :, :], hl[:, :, 0:C], ALU.subtract).then_inc(s_hl, 1)

                    def fold(_):
                        dve.wait_ge(s_tokw, 1)
                        src = bank[4][:, :].rearrange("p (o l j q) -> p j q l o", l=2, j=2, q=HALF)
                        for j in range(2):
                            dst = w_tok[64 * j:64 * j + 64, :, :, :].rearrange("p q l (o two) -> p two q l o", two=2)
                            for odd in range(2):
                                for late in range(2):
                                    last = nc.vector.tensor_copy(dst[:, odd, :, late, :], src[64 * odd:64 * odd + 64, j, :, late, :])
                        last.then_inc(s_tokc, 1)
                        dve.wait_ge(s_const, 16)
                        for dst, off in ((identb, K_ID), (flipb, K_FLIP), (mask_s, K_MS), (mask_t, K_MT)):
                            nc.vector.tensor_copy(dst[:, :], const[:, off:off + P])

                    def first_weights(_):
                        dve.wait_ge(s_wa, 64)
                        nc.vector.tensor_copy(wa_hi[:, :], w_a[:, :]).then_inc(s_cast, 1)
                        dve.wait_ge(s_cast, 1)
                        nc.vector.tensor_tensor(wa_lo[:, :], w_a[:, :], wa_hi[:, :], ALU.subtract).then_inc(s_cast, 1)

                    def relative_bias(_):
                        dve.wait_ge(s_rel, 16)
                        nc.vector.tensor_scalar(rel[:, 0:BIAS_W - 1], rel[:, 0:BIAS_W - 1], rel[:, BIAS_W - 1:BIAS_W], None,
                                                ALU.subtract).then_inc(s_cast, 1)
                        dve.wait_ge(s_cast, 3)
                        nc.vector.memset(rel[:, BIAS_W - 1:BIAS_W], 0.0).then_inc(s_cast, 1)
                        dve.wait_ge(s_cast, 4)
                        nc.vector.tensor_copy(rel_hi[:, :], rel[:, :]).then_inc(s_cast, 1)
                        dve.wait_ge(s_cast, 5)
                        nc.vector.tensor_tensor(rel_lo[:, :], rel[:, :], rel_hi[:, :], ALU.subtract)

                    def weights(n):
                        dve.wait_ge(s_hi, n + 1)
                        for k in wt_banks[n]:
                            r = nat_rows(k)
                            last = nc.vector.tensor_tensor(wt_lo[:, k * P:k * P + r], bank[n % 4][:, (k % 4) * P:(k % 4) * P + r],
                                                           wt_hi[:, k * P:k * P + r], ALU.subtract)
                        last.then_inc(s_lo, 1)

                    def w2_weights(n):
                        dve.wait_ge(s_trn, len(wt_banks) + n + 1)
                        ks = w2_banks[n]
                        nc.vector.tensor_copy(w2s[:, ks[0] * C:ks[0] * C + len(ks) * C], bank[3 + n][:, 0:len(ks) * C])

                    def tok(g):
                        n0, n1, u0 = ((0, 7, 1), (7, 15, 0), (15, 16, 0))[g]
                        o, _, s = job("tok", g)
                        dve.wait_ge(s_early, min(g, 1) + 1)
                        late = o[C:P, :].rearrange("p (u v) -> p v u", v=V)[:, :, u0:u0 + n1 - n0]
                        nc.vector.tensor_tensor(h_feat[:, :, n0:n1], late, h_feat[:, :, n0:n1], ALU.add).then_inc(s, 1)

                    def apply_x(name, row):
                        dve.wait_ge(s_rstd_x, plan.count(name, NORM_X))
                        link(nc.vector.tensor_tensor(hn[:, :, :], hn[:, :, :], per_token(stat_x[:, row, :], C), ALU.mult))

                    def ln1a(_):
                        taken(dve, "tokT", 0)
                        dve.wait_ge(s_txt, 16)
                        if is_first:
                            dve.wait_ge(s_zero, 1)
                            dve.wait_ge(s_par, 16 * 9)
                        if has_end:
                            dve.wait_ge(s_xl, 1)
                        center(h0)

                    def ln1b(_):
                        mean_square(stat_x, s_sq_x, plan.count("ln1b", NORM_X))
                        nc.vector.tensor_scalar(stat_x[:, 3, :], stat_x[:, 2, :], 1.0 + LN_EPS, LN_EPS * LN_EPS,
                                                ALU.mult, ALU.add).then_inc(s_norm_x, 1)

                    def ln1c(_):
                        apply_x("ln1b", 6)
                        nc.vector.tensor_tensor(hn[:, :, :], hn[:, :, :], par_b(B1), ALU.add).then_inc(s_gain_x, 1)
                        lo(hn, hl_x, s_hi_x, plan.count("ln1c", SPLIT_X), s_hl_x)

                    def qkv1(k):
                        o, _, s = job("qkv1", k)
                        n, w = (2, P) if k < 4 else (1, REST)
                        nc.vector.tensor_tensor(qkv[0:w, 2 * k:2 * k + n, :], o[0:w, 0:192 * n].rearrange("p (i n) -> p i n", n=192),
                                                par_b(BQKV, 192, n, w), ALU.add).then_inc(s, 1)

                    def split1(_):
                        dve.wait_ge(s_qk_hi, 1)
                        nc.vector.tensor_tensor(ql[:, :, C:P], qkv[:, :, 0:C], ql[:, :, 0:C], ALU.subtract)
                        nc.vector.tensor_tensor(kb[:, :, 0:C], qkv[:, :, C:P], ka[:, :, 0:C], ALU.subtract).then_inc(s_qk_lo, 1)

                    def split2(_):
                        dve.wait_ge(s_fqk_hi, 1)
                        rq = rope[:, 0, :, 0:64].rearrange("p t (h c) -> p t h c", c=HD)
                        rk = rope[:, 0, :, 64:96].rearrange("p t (h c) -> p t h c", c=HD)
                        nc.vector.tensor_tensor(fqb[:, :, :, HD:2 * HD], rq, fqb[:, :, :, 0:HD], ALU.subtract)
                        nc.vector.tensor_tensor(fkb[:, :, :, 2 * HD:3 * HD], rk, fkb[:, :, :, 0:HD], ALU.subtract).then_inc(s_fqk_lo, 1)

                    def stack2(k):
                        if k < 4:
                            return
                        _, o, s = job("stack2", k)
                        c0, n = P * PARTS[k % 2][0], sum(tokens(i) for i in PARTS[k % 2])
                        for g in range(NKV):
                            last = nc.vector.tensor_copy(fk[FS * g:FS * g + FS, g, c0:c0 + n], o[FS * g:FS * g + FS, 0:n])
                        last.then_inc(s, 1)

                    def reduce_group(g, parts, n, cols):
                        dve.wait_ge(s_sc, g + 1)
                        w = parts.shape[0]
                        nc.vector.tensor_reduce(parts[:, n:n + 1], bank[g % 2][0:w, 0:cols[1] - cols[0]],
                                                AX.X, ALU.max).then_inc(s_red, 1)

                    def S1(i, n):
                        w, g = tokens(i), plan.score["S1", i, n]
                        reduce_group(g, pmax1[0:w, i % 2, :], n, A1_S[n])
                        if n == len(A1_S) - 1:
                            dve.wait_ge(s_red, g + 1)
                            nc.vector.tensor_reduce(rmax1[0:w, i:i + 1], pmax1[0:w, i % 2, :], AX.X, ALU.max).then_inc(s_max1, 1)

                    def O1(i):
                        w = tokens(i)
                        dve.wait_ge(s_used, plan.output["V1", i])
                        link(nc.vector.reciprocal(rec1[0:w, 0:1], bank[5][0:w, C:C + 1]))
                        nc.vector.tensor_scalar(ao_x[0:w, i, :], bank[5][0:w, 0:C], rec1[0:w, 0:1], scale[0:w, 0:1],
                                                ALU.mult, ALU.mult).then_inc(s_ao1, 1)

                    def S2(i, h, n):
                        w, g, m = tokens(i), plan.score["S2", i, h, n], len(a2_s(i))
                        reduce_group(g, pmax[0:w, i % 2, h, :], n, a2_s(i)[n])
                        if h == NH - 1 and n == m - 1:
                            dve.wait_ge(s_red, g + 1)
                            nc.vector.tensor_reduce(rmax[0:w, i, :], pmax[0:w, i % 2, :, 0:m], AX.X, ALU.max).then_inc(s_max2, 1)

                    def O2(i):
                        w = tokens(i)
                        dve.wait_ge(s_oT, PLACE[i] + 1)
                        o = bank[4][0:w, P:2 * P].rearrange("p (h c) -> p h c", c=32)
                        link(nc.vector.reciprocal(rec[0:w, :], o[:, :, HD]))
                        nc.vector.tensor_tensor(ao_y[0:w, i, :].rearrange("p (g r c) -> p r g c", g=2, r=2),
                                                o[:, :, 0:HD].rearrange("p (r g) c -> p r g c", r=2),
                                                rec[0:w, :].rearrange("p (r g) -> p r g", r=2).unsqueeze(3).to_broadcast([w, 2, 2, HD]),
                                                ALU.mult).then_inc(s_ao2, 1)

                    def from_project(name, k, dst, add):
                        o, _, s = job(name, k)
                        if k == 0:
                            nc.vector.tensor_tensor(dst[:, 0:FULL, :], o[:, :].rearrange("p (i c) -> p i c", c=C),
                                                    add[:, 0:FULL, :], ALU.add).then_inc(s, 1)
                        else:
                            nc.vector.tensor_tensor(dst[0:REST, FULL, :], o[0:REST, 0:C], add[0:REST, FULL, :], ALU.add).then_inc(s, 1)

                    def ln2a(_):
                        for k in range(2):
                            taken(dve, "proj", k)
                        center(xt)

                    def ln2b(_):
                        mean_square(stat_x, s_sq_x, plan.count("ln2b", NORM_X))
                        nc.vector.tensor_scalar(stat_x[:, 3, :], stat_x[:, 2, :], LN_EPS, None, ALU.add).then_inc(s_norm_x, 1)

                    def ln2c(_):
                        apply_x("ln2b", 6)
                        dve.wait_ge(s_h0, 2)
                        if has_y:
                            dve.wait_ge(s_base, 1)
                        nc.vector.tensor_tensor(h1[:, :, :], hn[:, :, :], h0[:, :, :], ALU.add).then_inc(s_h1, 1)

                    def ln3a(_):
                        dve.wait_ge(s_h1, 1)
                        center(h1)

                    def ln3b(_):
                        mean_square(stat_x, s_sq_x, plan.count("ln3b", NORM_X))
                        link(nc.vector.tensor_scalar(stat_x[:, 3, :], stat_x[:, 2, :], LN_EPS, None, ALU.add))
                        link(nc.vector.reciprocal(stat_x[:, 4, :], stat_x[:, 3, :]))
                        link(nc.vector.tensor_tensor(stat_x[:, 4, :], stat_x[:, 2, :], stat_x[:, 4, :], ALU.mult))
                        link(nc.vector.tensor_scalar(stat_x[:, 4, :], stat_x[:, 4, :], RMS_EPS, None, ALU.add))
                        nc.vector.tensor_tensor(stat_x[:, 5, :], stat_x[:, 3, :], stat_x[:, 4, :], ALU.mult).then_inc(s_norm_x, 1)

                    def ln3c(_):
                        dve.wait_ge(s_rstd_x, plan.count("ln3b", NORM_X))
                        nc.vector.tensor_tensor(hn[:, :, :], hn[:, :, :], per_token(stat_x[:, 7, :], C), ALU.mult).then_inc(s_gain_x, 1)

                    def rope_(_):
                        for k in range(3):
                            taken(dve, "qkv2", k)
                        cos = const[:, K_COS:K_COS + NT * HD].rearrange("p (t c) -> p t c", c=HD)
                        link(nc.vector.tensor_tensor(rope[:, 0, :, :].rearrange("p t (h c) -> p t h c", c=HD),
                                                     qkv_y[:, :, 0:96].rearrange("p t (h c) -> p t h c", c=HD),
                                                     cos.unsqueeze(2).to_broadcast([P, NT, 6, HD]), ALU.mult))
                        dve.wait_ge(s_rot, 1)
                        nc.vector.tensor_tensor(rope[:, 0, :, :], rope[:, 0, :, :], rope[:, 1, :, :], ALU.add).then_inc(s_rope, 1)

                    def rmsa(_):
                        mean_square(stat_y, s_sq_y, 1)
                        nc.vector.tensor_scalar(stat_y[:, 3, :], stat_y[:, 2, :], RMS_EPS, None, ALU.add).then_inc(s_norm_y, 1)

                    def rmsb(_):
                        dve.wait_ge(s_rstd_y, 1)
                        nc.vector.tensor_tensor(hn_y[:, :, :], hn_y[:, :, :], per_token(stat_y[:, 6, :], C), ALU.mult).then_inc(s_gain_y, 1)
                        lo(hn_y, hl_y, s_hi_y, plan.count("rmsb", SPLIT_Y), s_hl_y)

                    def router(_):
                        o, _, s = job("router", 0)
                        nc.vector.tensor_copy(gate_l[:, 0:FULL, :], o[:, 0:FULL * NE].rearrange("p (i e) -> p i e", e=NE)).then_inc(s_logit, 1)
                        nc.vector.tensor_copy(gate_l[0:REST, FULL, :], o[0:REST, FULL * NE:NT * NE]).then_inc(s, 1)
                        dve.wait_ge(s_logit, 1)
                        taken(dve, "router", 0)
                        nc.vector.tensor_reduce(gate_s[:, 0, :], gate_l[:, :, :], AX.X, ALU.max).then_inc(s_logit, 1)
                        dve.wait_ge(s_logit, 2)
                        nc.vector.tensor_tensor(gate_l[:, :, :], gate_l[:, :, :], per_token(gate_s[:, 0, :], NE), ALU.subtract).then_inc(s_logit, 1)

                    def pick(m, probs, sel):
                        desc = const[:, K_DESC:K_DESC + NE].unsqueeze(1).to_broadcast([P, NT, NE])
                        link(nc.vector.tensor_reduce(gate_s[:, m, :], probs[:, :, :], AX.X, ALU.max))
                        link(nc.vector.tensor_tensor(sel[:, :, :], probs[:, :, :], per_token(gate_s[:, m, :], NE), ALU.is_equal))
                        link(nc.vector.tensor_tensor(sel[:, :, :], sel[:, :, :], desc, ALU.mult))
                        link(nc.vector.tensor_reduce(gate_s[:, 3, :], sel[:, :, :], AX.X, ALU.max))
                        link(nc.vector.tensor_tensor(sel[:, :, :], sel[:, :, :], per_token(gate_s[:, 3, :], NE), ALU.is_equal))

                    def gates(part):
                        if part == 0:
                            dve.wait_ge(s_gexp, 1)
                            link(nc.vector.tensor_reduce(gate_s[:, 0, :], gate_e[:, :, :], AX.X, ALU.add))
                            link(nc.vector.reciprocal(gate_s[:, 5, :], gate_s[:, 0, :]))
                            link(nc.vector.tensor_tensor(gate_e[:, :, :], gate_e[:, :, :], per_token(gate_s[:, 5, :], NE), ALU.mult))
                        if part == 1:
                            pick(1, gate_e, gate_m)
                            link(nc.vector.scalar_tensor_tensor(gate_p[:, :, :], gate_m[:, :, :], -2.0, gate_e[:, :, :], ALU.mult, ALU.add))
                        if part == 2:
                            pick(2, gate_p, gate_w)
                            link(nc.vector.tensor_tensor(gate_m[:, :, :], gate_m[:, :, :], gate_w[:, :, :], ALU.add))
                        if part == 3:
                            link(nc.vector.tensor_tensor(gate_m[:, :, :], gate_m[:, :, :], gate_e[:, :, :], ALU.mult))
                            link(nc.vector.tensor_tensor(gate_s[:, 4, :], gate_s[:, 1, :], gate_s[:, 2, :], ALU.add))
                            link(nc.vector.tensor_scalar(gate_s[:, 4, :], gate_s[:, 4, :], 1e-9, None, ALU.add))
                            link(nc.vector.reciprocal(gate_s[:, 5, :], gate_s[:, 4, :]))
                            link(nc.vector.tensor_tensor(gate_w[:, :, :], gate_m[:, :, :], per_token(gate_s[:, 5, :], NE), ALU.mult))

                    def gate_tile(i):
                        w = tokens(i)
                        dve.wait_ge(s_w2, i + 1)
                        link(nc.vector.tensor_tensor(gated[0:w, :].rearrange("p (e c) -> p e c", c=C),
                                                     bank[4 + i % 2][0:w, :].rearrange("p (e c) -> p e c", c=C),
                                                     per_token(gate_w[0:w, i, :], C), ALU.mult))
                        link(nc.vector.tensor_reduce(gsum[0:w, :], gated[0:w, :].rearrange("p (e c) -> p c e", c=C), AX.X, ALU.add))
                        if i == 0:
                            dve.wait_ge(s_base, 1)
                        nc.vector.tensor_tensor(res[0:w, i, :], gsum[0:w, :], base[0:w, i, :], ALU.add).then_inc(s_res, 1)

                    def up(t, c):
                        n, r, (a, z) = t * NC + c, rows_of(c), chunk_cols(t)
                        dve.wait_ge(s_silu, n + 1)
                        if t == 2 and c == 0:
                            dve.wait_ge(s_w2, CHUNK_TILES)
                        nc.vector.tensor_tensor(hid[0:r, t % 2, c, 0:z - a], bank[2 * pair(n) + 1][0:r, 0:z - a],
                                                silu[0:r, n % 3, 0:z - a], ALU.mult).then_inc(s_u, 1)
                        if t == 0 and c in (4, 6, 8, 10):
                            gates(c // 2 - 2)
                        if t >= 1:
                            for m in range(3 * c + 1, 3 * c + 4):
                                if m % NC == 0:
                                    gate_tile(CHUNK_TILES * (t - 1) + m // NC - 1)

                    def down(m):
                        if (m + 1) % NC == 0:
                            gate_tile(CHUNK_TILES * 2 + m // NC)

                    steps = {
                        "aosplit1": lambda _: lo(ao_x, hl_x, s_hi_x, plan.count("aosplit1", SPLIT_X), s_hl_x),
                        "ystart": lambda _: lo(hn, hl_y, s_hi_y, plan.count("ystart", SPLIT_Y), s_hl_y),
                        "aosplit2": lambda _: lo(ao_y, hl_y, s_hi_y, plan.count("aosplit2", SPLIT_Y), s_hl_y),
                        "split1": split1, "split2": split2,
                        "fold": fold, "wa": first_weights, "rel": relative_bias, "wt": weights, "w2": w2_weights,
                        "tok": tok, "ln1a": ln1a, "ln1b": ln1b, "ln1c": ln1c, "qkv1": qkv1,
                        "stack2": stack2, "S1": S1, "O1": O1, "S2": S2, "O2": O2, "ln2a": ln2a, "ln2b": ln2b, "ln2c": ln2c,
                        "ln3a": ln3a, "ln3b": ln3b, "ln3c": ln3c, "rope": rope_, "rmsa": rmsa, "rmsb": rmsb, "router": router,
                        "up": up, "down": down,
                        "proj": lambda k: from_project("proj", k, xt, par_b(BPROJ)),
                        "wo": lambda k: from_project("wo", k, x1, xl),
                    }
                    for s in plan.order:
                        if s[0] in steps:
                            steps[s[0]](*s[1:])

            nums = [s.num for s in sems]
            nc.gpsimd.sem_clear(range(min(nums), max(nums) + 1))
            nc.all_engine_barrier()

        run_pass(Plan(ORDER_FIRST), None, 0)
        run_pass(Plan(ORDER_START), None, 1)
        with nc.Fori(0, B - 2) as b:
            run_pass(Plan(ORDER_FULL), b, b + 2)
        run_pass(Plan(ORDER_LAST1), B - 2, None)
        run_pass(Plan(ORDER_END), B - 1, None)


def constants():
    import numpy as np
    k = np.arange(P)
    c = np.zeros((P, NCONST), np.float32)
    c[:, K_ID:K_ID + P] = np.eye(P)
    c[:, K_FLIP:K_FLIP + P] = np.eye(P)[::-1]
    c[:, K_MS:K_MS + P] = np.where(k[None, :] > k[:, None], -1e30, 0)
    c[:, K_MT:K_MT + P] = np.where(k[:, None] > k[None, :], -1e30, 0)
    inv = 1.0 / 10000.0 ** (np.arange(0, HD, 2, dtype=np.float32) / HD)
    fr = np.outer(np.arange(NT * P, dtype=np.float32), inv)
    emb = np.concatenate([fr, fr], axis=-1)
    sign = np.concatenate([-np.ones(HD // 2), np.ones(HD // 2)])
    for off, t in ((K_COS, np.cos(emb)), (K_SIN, np.sin(emb) * sign)):
        c[:, off:off + NT * HD] = t.reshape(NT, P, HD).transpose(1, 0, 2).reshape(P, NT * HD)
    c[:, K_DESC:K_DESC + NE] = np.arange(NE, 0, -1)
    c[:, K_HALF] = -0.5
    f, p = np.arange(NFREQ)[:, None], np.arange(PATCH)[None, :]
    ang = 2 * np.pi * f * p / PATCH
    dft = np.concatenate([np.cos(ang), -np.sin(ang)]) / np.sqrt(PATCH)
    return c, dft.astype(np.float32)


_INS = {
    'x': ('x', None), 'txt': ('txt', None), 'tok_w': ('L0_tok_W', None),
    'ln1_g': ('L0_attn_ln1_g', (1, -1)), 'ln1_b': ('L0_attn_ln1_b', (1, -1)), 'qkv_w': ('L0_attn_qkv_w', None),
    'qkv_b': ('L0_attn_qkv_b', (1, -1)), 'bias_table': ('L0_attn_bias_table', (1, -1)),
    'attn_scale': ('L0_attn_scale', (1, 1)), 'proj_w': ('L0_attn_proj_w', None), 'proj_b': ('L0_attn_proj_b', (1, -1)),
    'ln2_g': ('L0_attn_ln2_g', (1, -1)), 'ln2_b': ('L0_attn_ln2_b', (1, -1)), 'f_ln1': ('L0_ffn_ln1_w', (1, -1)),
    'f_ln2': ('L0_ffn_ln2_w', (1, -1)), 'wq': ('L0_ffn_wq', None), 'wk': ('L0_ffn_wk', None), 'wv': ('L0_ffn_wv', None),
    'wo': ('L0_ffn_wo', None), 'router_w': ('L0_ffn_router_w', None), 'w1': ('L0_ffn_w1', None),
    'w2': ('L0_ffn_w2', None), 'w3': ('L0_ffn_w3', None),
}


def kernel(**inputs):
    import numpy as np
    import concourse.bacc as bacc
    from concourse.bass_utils import run_bass_kernel_spmd as run

    nc = bacc.Bacc("TRN2", target_bir_lowering=False, num_devices=1)
    arrays, aps = {}, {}

    def give(name, a):
        arrays[f"in_{name}"] = a
        aps[name] = nc.dram_tensor(f"in_{name}", a.shape, mybir.dt.from_np(a.dtype), kind="ExternalInput").ap()

    for name, (key, shape) in _INS.items():
        a = np.ascontiguousarray(inputs[key])
        give(name, a if shape is None else a.reshape(shape))
    const, dft = constants()
    give("const", const)
    give("dft", dft)
    out = nc.dram_tensor("out_dram", (B, TOK, C), F32, kind="ExternalOutput").ap()
    program(nc, aps, out)
    r = run(nc, [arrays], core_ids=[0])
    return r.results[0]["out_dram"]
```
